# Optimizing a Trainium2 kernel written in Bass

```python
import numpy as np
import jax
import jax.numpy as jnp

def _softmax(x, axis=-1):
    return jax.nn.softmax(x, axis=axis)
def _gelu(x):
    return jax.nn.gelu(x, approximate=True)
def _silu(x):
    return jax.nn.silu(x)
def _sigmoid(x):
    return jax.nn.sigmoid(x)
def _layernorm(x, axis=-1, eps=1e-5):
    m = jnp.mean(x, axis=axis, keepdims=True)
    v = jnp.var(x, axis=axis, keepdims=True)
    return (x - m) / jnp.sqrt(v + eps)
def _scatter_add(tgt, idx, src, axis=0):
    return tgt.at[idx].add(src)
def _segment_sum(src, seg, n):
    return jax.ops.segment_sum(src, seg, n)

kernel_name = 'mk_adj_resnorm_d4_adj_128_6c685b'

def setup_inputs(seed: int = 0):
    np.random.seed(seed)
    _w = jnp.asarray
    def _rec_inputs():
        import jax
        import jax.numpy as jnp
        _gk = jax.random.key(seed)
        x = -0.0005207 + 1.001 * jax.random.normal(jax.random.fold_in(_gk, 1), (16, 1024, 128), jnp.float32)
        _a = jax.random.bernoulli(jax.random.fold_in(_gk, 2), 0.015625, (16, 1024, 1024))
        _af = _a.astype(jnp.float32)
        adj = _af
        _nm = jnp.ones((16, 1024), dtype=bool)
        nodemask = jnp.where(_nm, 1.0, 0.0).astype(jnp.int32)
        return x, adj, nodemask
    x, adj, nodemask = _rec_inputs()
    def _L0_gnn_setup():
        import jax, jax.numpy as jnp
        import numpy as np
        B, N, D = (4, 4096, 128)
        key = jax.random.key(seed)
        k1, k2, k3 = jax.random.split(key, 3)
        x = jax.random.normal(k1, (B, N, D), dtype=jnp.float32)
        adj_mat = jax.random.randint(k2, (B, N, N), 0, 2).astype(jnp.float32)
        U = jax.random.normal(k3, (D, D), dtype=jnp.float32) * np.sqrt(2.0 / (D + D))
        return {'x': x, 'adj_mat': adj_mat, 'U': U}
    _L0_gnn_all = _L0_gnn_setup()
    _L0_gnn_in = {k: v for k, v in _L0_gnn_all.items() if k in ('U', )}
    del _L0_gnn_all

    def _L1_gnn_setup():
        import jax, jax.numpy as jnp
        import numpy as np
        B, N, DIN, HID = (8, 2048, 128, 128)
        CLAMP_HI = 90000000000000.0
        NEG_PENALTY = 9000000000000000.0
        key = jax.random.key(seed)
        ks = jax.random.split(key, 8)
        s = 1.0 / np.sqrt(DIN)
        x = jax.random.normal(ks[0], (B, N, DIN), dtype=jnp.float32)
        mask = jax.random.randint(ks[1], (B, N, N), 0, 2).astype(jnp.float32)
        Wv = jax.random.uniform(ks[2], (HID, DIN), jnp.float32, -s, s)
        bv = jax.random.uniform(ks[3], (HID,), jnp.float32, -s, s)
        Wk = jax.random.uniform(ks[4], (HID, DIN), jnp.float32, -s, s)
        bk = jax.random.uniform(ks[5], (HID,), jnp.float32, -s, s)
        Wq = jax.random.uniform(ks[6], (HID, DIN), jnp.float32, -s, s)
        bq = jax.random.uniform(ks[7], (HID,), jnp.float32, -s, s)
        return {'x': x, 'mask': mask, 'Wv': Wv, 'bv': bv, 'Wk': Wk, 'bk': bk, 'Wq': Wq, 'bq': bq}
    _L1_gnn_all = _L1_gnn_setup()
    _L1_gnn_in = {k: v for k, v in _L1_gnn_all.items() if k in ('Wv', 'bv', 'Wk', 'bk', 'Wq', 'bq', )}
    del _L1_gnn_all

    def _L2_gnn_setup():
        import jax, jax.numpy as jnp
        import numpy as np
        NEG_SLOPE = 0.2
        MASK_EPS = 1e-08
        NEG_INF = -1000000000.0
        key = jax.random.key(seed)
        k1, k2, k3, k4 = jax.random.split(key, 4)
        B, N, D_in, D_out, H = (32, 512, 128, 128, 4)
        h = jax.random.normal(k1, (B, N, D_in), dtype=jnp.float32)
        adj = jax.random.uniform(k2, (B, N, N), dtype=jnp.float32)
        W = jax.random.normal(k3, (D_in, D_out), dtype=jnp.float32) * (1.0 / np.sqrt(D_in))
        a = jax.random.normal(k4, (H, 2 * (D_out // H)), dtype=jnp.float32) * 0.1
        return {'h': h, 'adj': adj, 'W': W, 'a': a}
    _L2_gnn_all = _L2_gnn_setup()
    _L2_gnn_in = {k: v for k, v in _L2_gnn_all.items() if k in ('W', 'a', )}
    del _L2_gnn_all

    def _L3_gnn_setup():
        import jax, jax.numpy as jnp
        import numpy as np
        T_DIL = 10
        K_DIL = 2
        BN_EPS = 1e-05
        NORM_EPS = 1e-12

        def _dilate_pattern(adj_bool, mask_b):
            N = adj_bool.shape[0]

            def step(carry, n):
                row = jnp.take(carry, n, axis=0)
                nbi = row.astype(jnp.int32)
                num = jnp.sum(nbi)
                sf = jnp.where(num > T_DIL, (num + K_DIL - 1) // K_DIL, 1)
                rank = jnp.cumsum(nbi)
                rm = row & (rank % sf == 0)
                valid = (mask_b[n] != 0) & (num > 1)
                rm = jnp.where(valid, rm, False)
                keep = ~rm
                carry = carry.at[n].set(row & keep)
                carry = carry.at[:, n].set(carry[:, n] & keep)
                return (carry, None)
            out, _ = jax.lax.scan(step, adj_bool, jnp.arange(N))
            return out

        def _dilate(adj, mask):
            keep = jax.vmap(_dilate_pattern)(adj > 0, mask)
            return adj * keep.astype(adj.dtype)

        def _sage(x, adj, Wr, Wx, b, mf):
            deg = jnp.clip(jnp.sum(adj, axis=-1, keepdims=True), 1.0, None)
            agg = jnp.einsum('bij,bjd->bid', adj, x) / deg
            out = agg @ Wr + x @ Wx + b
            nrm = jnp.maximum(jnp.linalg.norm(out, axis=-1, keepdims=True), NORM_EPS)
            return out / nrm * mf[..., None]

        def _bn(x, g, b):
            m = jnp.mean(x, axis=(0, 1))
            v = jnp.var(x, axis=(0, 1))
            return (x - m) * jax.lax.rsqrt(v + BN_EPS) * g + b

        def _forward(x, adj, mask, Wr1, Wx1, b1, g1, be1, Wr2, Wx2, b2, g2, be2, Wr3, Wx3, b3, g3, be3, Wl, bl):
            mf = mask.astype(x.dtype)
            adj_d = _dilate(adj, mask)
            h1 = _bn(jax.nn.relu(_sage(x, adj_d, Wr1, Wx1, b1, mf)), g1, be1)
            h2 = _bn(jax.nn.relu(_sage(h1, adj_d, Wr2, Wx2, b2, mf)), g2, be2)
            h3 = _bn(jax.nn.relu(_sage(h2, adj_d, Wr3, Wx3, b3, mf)), g3, be3)
            xc = jnp.concatenate([h1, h2, h3], axis=-1) * mf[..., None]
            return (xc @ Wl + bl) * mf[..., None]
        B, N, D, H, E = (8, 2048, 128, 128, 128)
        key = jax.random.key(seed)
        ks = jax.random.split(key, 24)
        x = jax.random.normal(ks[0], (B, N, D), dtype=jnp.float32)
        a = jax.random.bernoulli(ks[1], 0.01, (B, N, N))
        a = a | jnp.swapaxes(a, 1, 2)
        a = a & ~jnp.eye(N, dtype=bool)[None]
        adj = a.astype(jnp.float32)
        mask = jnp.ones((B, N), dtype=jnp.int32)
        s = 0.05
        p = {}
        dims = [(D, H), (H, H), (H, E)]
        for i, (di, do) in enumerate(dims, 1):
            p[f'Wr{i}'] = s * jax.random.normal(ks[2 * i], (di, do), dtype=jnp.float32)
            p[f'Wx{i}'] = s * jax.random.normal(ks[2 * i + 1], (di, do), dtype=jnp.float32)
            p[f'b{i}'] = jnp.zeros((do,), dtype=jnp.float32)
            p[f'g{i}'] = jnp.ones((do,), dtype=jnp.float32)
            p[f'be{i}'] = jnp.zeros((do,), dtype=jnp.float32)
        p['Wl'] = s * jax.random.normal(ks[10], (2 * H + E, E), dtype=jnp.float32)
        p['bl'] = jnp.zeros((E,), dtype=jnp.float32)
        return {'x': x, 'adj': adj, 'mask': mask, **p}
    _L3_gnn_all = _L3_gnn_setup()
    _L3_gnn_in = {k: v for k, v in _L3_gnn_all.items() if k in ('Wr1', 'Wx1', 'b1', 'g1', 'be1', 'Wr2', 'Wx2', 'b2', 'g2', 'be2', 'Wr3', 'Wx3', 'b3', 'g3', 'be3', 'Wl', 'bl', )}
    del _L3_gnn_all

    return {
        "x": x,
        "adj": adj,
        "nodemask": nodemask,
        "L0_gnn_U": _L0_gnn_in["U"],
        "L1_gnn_Wv": _L1_gnn_in["Wv"],
        "L1_gnn_bv": _L1_gnn_in["bv"],
        "L1_gnn_Wk": _L1_gnn_in["Wk"],
        "L1_gnn_bk": _L1_gnn_in["bk"],
        "L1_gnn_Wq": _L1_gnn_in["Wq"],
        "L1_gnn_bq": _L1_gnn_in["bq"],
        "L2_gnn_W": _L2_gnn_in["W"],
        "L2_gnn_a": _L2_gnn_in["a"],
        "L3_gnn_Wr1": _L3_gnn_in["Wr1"],
        "L3_gnn_Wx1": _L3_gnn_in["Wx1"],
        "L3_gnn_b1": _L3_gnn_in["b1"],
        "L3_gnn_g1": _L3_gnn_in["g1"],
        "L3_gnn_be1": _L3_gnn_in["be1"],
        "L3_gnn_Wr2": _L3_gnn_in["Wr2"],
        "L3_gnn_Wx2": _L3_gnn_in["Wx2"],
        "L3_gnn_b2": _L3_gnn_in["b2"],
        "L3_gnn_g2": _L3_gnn_in["g2"],
        "L3_gnn_be2": _L3_gnn_in["be2"],
        "L3_gnn_Wr3": _L3_gnn_in["Wr3"],
        "L3_gnn_Wx3": _L3_gnn_in["Wx3"],
        "L3_gnn_b3": _L3_gnn_in["b3"],
        "L3_gnn_g3": _L3_gnn_in["g3"],
        "L3_gnn_be3": _L3_gnn_in["be3"],
        "L3_gnn_Wl": _L3_gnn_in["Wl"],
        "L3_gnn_bl": _L3_gnn_in["bl"],
    }

def reference(x, adj, nodemask, L0_gnn_U, L1_gnn_Wv, L1_gnn_bv, L1_gnn_Wk, L1_gnn_bk, L1_gnn_Wq, L1_gnn_bq, L2_gnn_W, L2_gnn_a, L3_gnn_Wr1, L3_gnn_Wx1, L3_gnn_b1, L3_gnn_g1, L3_gnn_be1, L3_gnn_Wr2, L3_gnn_Wx2, L3_gnn_b2, L3_gnn_g2, L3_gnn_be2, L3_gnn_Wr3, L3_gnn_Wx3, L3_gnn_b3, L3_gnn_g3, L3_gnn_be3, L3_gnn_Wl, L3_gnn_bl):
    import jax
    import jax.numpy as jnp
    def _L0_gnn_ref(x, adj_mat, U):
        import jax, jax.numpy as jnp
        import numpy as np
        B, N, D = (4, 4096, 128)
        mask = (adj_mat > 0).astype(x.dtype)
        deg = jnp.sum(adj_mat, axis=1)
        agg = jnp.einsum('bji,bjd->bid', mask, x)
        out = jax.nn.relu(jnp.einsum('bid,de->bie', agg, U) / deg[..., None])
        return out

    def _L1_gnn_ref(x, mask, Wv, bv, Wk, bk, Wq, bq):
        import jax, jax.numpy as jnp
        import numpy as np
        B, N, DIN, HID = (8, 2048, 128, 128)
        CLAMP_HI = 90000000000000.0
        NEG_PENALTY = 9000000000000000.0
        v = jax.nn.relu(jnp.einsum('bnd,hd->bnh', x, Wv) + bv)
        q = jax.nn.relu(jnp.einsum('bnd,hd->bnh', x, Wq) + bq)
        k = jax.nn.relu(jnp.einsum('bnd,hd->bnh', x, Wk) + bk)
        scores = jnp.einsum('bih,bjh->bij', q, k)
        h = jnp.clip(scores * mask, 0.0, CLAMP_HI) - NEG_PENALTY * (1.0 - mask)
        att = jax.nn.softmax(h, axis=2)
        out = jnp.einsum('bij,bjh->bih', att, v)
        return out

    def _L2_gnn_ref(h, adj, W, a):
        import jax, jax.numpy as jnp
        import numpy as np
        NEG_SLOPE = 0.2
        MASK_EPS = 1e-08
        NEG_INF = -1000000000.0
        B, N, _ = h.shape
        H, two_dh = a.shape
        Dh = two_dh // 2
        Wh = (h @ W).reshape(B, N, H, Dh)
        a_src, a_dst = (a[:, :Dh], a[:, Dh:])
        s_i = jnp.einsum('bnhd,hd->bnh', Wh, a_src)
        s_j = jnp.einsum('bnhd,hd->bnh', Wh, a_dst)
        e = s_i[:, :, None, :] + s_j[:, None, :, :]
        e = jnp.where(e >= 0, e, NEG_SLOPE * e)
        mask = adj[..., None] > MASK_EPS
        e = jnp.where(mask, e, NEG_INF)
        alpha = jax.nn.softmax(e, axis=-3)
        out = jnp.einsum('bijh,bihd->bjhd', alpha, Wh)
        return out.reshape(B, N, H * Dh)

    def _L3_gnn_ref(x, adj, mask, Wr1, Wx1, b1, g1, be1, Wr2, Wx2, b2, g2, be2, Wr3, Wx3, b3, g3, be3, Wl, bl):
        import jax, jax.numpy as jnp
        import numpy as np
        T_DIL = 10
        K_DIL = 2
        BN_EPS = 1e-05
        NORM_EPS = 1e-12

        def _dilate_pattern(adj_bool, mask_b):
            N = adj_bool.shape[0]

            def step(carry, n):
                row = jnp.take(carry, n, axis=0)
                nbi = row.astype(jnp.int32)
                num = jnp.sum(nbi)
                sf = jnp.where(num > T_DIL, (num + K_DIL - 1) // K_DIL, 1)
                rank = jnp.cumsum(nbi)
                rm = row & (rank % sf == 0)
                valid = (mask_b[n] != 0) & (num > 1)
                rm = jnp.where(valid, rm, False)
                keep = ~rm
                carry = carry.at[n].set(row & keep)
                carry = carry.at[:, n].set(carry[:, n] & keep)
                return (carry, None)
            out, _ = jax.lax.scan(step, adj_bool, jnp.arange(N))
            return out

        def _dilate(adj, mask):
            keep = jax.vmap(_dilate_pattern)(adj > 0, mask)
            return adj * keep.astype(adj.dtype)

        def _sage(x, adj, Wr, Wx, b, mf):
            deg = jnp.clip(jnp.sum(adj, axis=-1, keepdims=True), 1.0, None)
            agg = jnp.einsum('bij,bjd->bid', adj, x) / deg
            out = agg @ Wr + x @ Wx + b
            nrm = jnp.maximum(jnp.linalg.norm(out, axis=-1, keepdims=True), NORM_EPS)
            return out / nrm * mf[..., None]

        def _bn(x, g, b):
            m = jnp.mean(x, axis=(0, 1))
            v = jnp.var(x, axis=(0, 1))
            return (x - m) * jax.lax.rsqrt(v + BN_EPS) * g + b

        def _forward(x, adj, mask, Wr1, Wx1, b1, g1, be1, Wr2, Wx2, b2, g2, be2, Wr3, Wx3, b3, g3, be3, Wl, bl):
            mf = mask.astype(x.dtype)
            adj_d = _dilate(adj, mask)
            h1 = _bn(jax.nn.relu(_sage(x, adj_d, Wr1, Wx1, b1, mf)), g1, be1)
            h2 = _bn(jax.nn.relu(_sage(h1, adj_d, Wr2, Wx2, b2, mf)), g2, be2)
            h3 = _bn(jax.nn.relu(_sage(h2, adj_d, Wr3, Wx3, b3, mf)), g3, be3)
            xc = jnp.concatenate([h1, h2, h3], axis=-1) * mf[..., None]
            return (xc @ Wl + bl) * mf[..., None]
        return _forward(x, adj, mask, Wr1, Wx1, b1, g1, be1, Wr2, Wx2, b2, g2, be2, Wr3, Wx3, b3, g3, be3, Wl, bl)

    x = _layernorm(x + _L0_gnn_ref(x, adj, L0_gnn_U), axis=-1)
    x = _layernorm(x + _L1_gnn_ref(x, adj, L1_gnn_Wv, L1_gnn_bv, L1_gnn_Wk, L1_gnn_bk, L1_gnn_Wq, L1_gnn_bq), axis=-1)
    x = _layernorm(x + _L2_gnn_ref(x, adj, L2_gnn_W, L2_gnn_a), axis=-1)
    x = _layernorm(x + _L3_gnn_ref(x, adj, nodemask, L3_gnn_Wr1, L3_gnn_Wx1, L3_gnn_b1, L3_gnn_g1, L3_gnn_be1, L3_gnn_Wr2, L3_gnn_Wx2, L3_gnn_b2, L3_gnn_g2, L3_gnn_be2, L3_gnn_Wr3, L3_gnn_Wx3, L3_gnn_b3, L3_gnn_g3, L3_gnn_be3, L3_gnn_Wl, L3_gnn_bl), axis=-1)
    return x


_drawn_inputs = setup_inputs


def setup_inputs(seed=0):
    import zlib

    import numpy as np

    out = dict(_drawn_inputs(seed))
    spreads = {'L3_gnn_b1': (0.0, 0.1),
     'L3_gnn_g1': (1.0, 0.2),
     'L3_gnn_be1': (0.0, 0.1),
     'L3_gnn_b2': (0.0, 0.1),
     'L3_gnn_g2': (1.0, 0.2),
     'L3_gnn_be2': (0.0, 0.1),
     'L3_gnn_b3': (0.0, 0.1),
     'L3_gnn_g3': (1.0, 0.2),
     'L3_gnn_be3': (0.0, 0.1),
     'L3_gnn_bl': (0.0, 0.1)}
    factors = {'L1_gnn_bk': 3.107}
    for name, (base, spread) in spreads.items():
        noise = np.random.default_rng([zlib.crc32(name.encode()), seed]).standard_normal(out[name].shape)
        drawn = base * np.exp(spread * noise) if base else spread * noise
        out[name] = jnp.asarray(drawn.astype(out[name].dtype))
    for name, factor in factors.items():
        out[name] = (out[name] * factor).astype(out[name].dtype)
    return out
```

```python
from contextlib import ExitStack

import concourse.bass as bass
from concourse import mybir

G, N, D = 16, 1024, 128
P = 128
T = N // P
HALF = N // 2
HEADS = 4
DH = D // HEADS
EPS = 1e-5
BIG = 9.0e15
CLAMP = 9.0e13
SLOPE = 0.2
W32 = 32
CH = N // W32
QB = 2
GROUP = 4 * QB
MAGIC = 8388608.0

USES = (["xt", "y", "agg", "agg", "x1t", "q", "k", "v"] + ["s"] * T + ["mt"]
        + ["pt"] * 4 + ["o"] + ["pt"] * 2 + ["o"] + ["pt"] * 2 + ["o", "o"]
        + ["x2t", "wh", "wh", "qa", "qa", "sj", "sj", "ph", "sj", "ph", "sj", "ph", "ph", "x3t"])
USES_SAGE = ["adt"] * T + ["yz", "yz", "agg", "agg", "rt"]
USES_SAGE_LATER = ["yz", "yz", "agg", "agg", "rt"]
SLOTS = 4


def counts(uses):
    return {kind: uses.count(kind) for kind in uses}


def earlier_use(uses, n):
    if n >= SLOTS:
        return n - SLOTS, False
    return max(m for m in range(len(uses)) if m % SLOTS == n % SLOTS), True


def number(uses, n):
    return uses[:n].count(uses[n])


def layers_0_to_2(nc, S):
    f32, bf16, f16 = mybir.dt.float32, mybir.dt.bfloat16, mybir.dt.float16
    u8, i32 = mybir.dt.uint8, mybir.dt.int32
    ALU, ACT, AX = mybir.AluOpType, mybir.ActivationFunctionType, mybir.AxisListType
    V, A, PE, GP = nc.vector, nc.scalar, nc.tensor, nc.gpsimd
    x, adj, mask_rows, U0, Wv, bv, Wk, bk, Wq, bq, W2, a2 = S.inputs_0_to_2
    dilated, x3_dram, h_dram = S.dilated, S.x3_dram, S.h_dram
    ident, ident16, row0, eps_t = S.ident, S.ident16, S.row0, S.eps_t

    ctx = ExitStack()
    with ctx:
        def sb(name, shape, dt):
            return ctx.enter_context(nc.sbuf_tensor(name, shape, dt))

        def sem(name):
            return ctx.enter_context(nc.semaphore(name))

        bigI = sb("bigI", [P, P], bf16)
        sel = sb("sel", [96, T, P], bf16)
        wload = sb("wload", [P, 5, D], f32)
        wt = sb("wt", [P, 4, D], f32)
        wext = sb("wext", [P, D + 2 * HEADS], f32)
        ablk = sb("ablk", [P, 2 * HEADS], f32)
        wab = sb("wab", [P, HEADS, P], f32)
        bqk = sb("bqk", [P, 2], f32)
        bvrow = sb("bvrow", [P, D], f32)

        adjb = [sb(f"adj{i}", [P, T, N], bf16) for i in range(2)]
        abar_all = sb("abar", [P, T * N // 2], f32)
        abar = abar_all[:, :].bitcast(bf16).rearrange("p (t n) -> p t n", t=T)
        x_in = sb("x_in", [P, T, D], f32)
        xn = sb("xn", [P, T, D], f32)
        xT = sb("xT", [P, N], f32)
        region = sb("region", [P, 2 * T * N // 2], f32)
        ind = region[:, :].bitcast(bf16).rearrange("p (b t n) -> p b t n", b=2, t=T)
        pT = region[:, 0:2 * T * 256].rearrange("p (b t n) -> p b t n", b=2, t=T)
        o1 = 2 * T * 256
        qT = region[:, o1:o1 + N]
        kT = region[:, o1 + N:o1 + 2 * N]
        vo = region[:, o1 + 2 * N:o1 + 2 * N + T * 129].rearrange("p (t n) -> p t n", t=T)
        parts = sb("parts", [P, T * 3 * HEADS * 66], bf16)
        vs = parts[:, :].rearrange("p (t s h c) -> p t s h c", t=T, s=3, h=HEADS)
        y3 = parts[:, 0:3 * T * 129].rearrange("p (s t c) -> p s t c", s=3, t=T)
        n_va, n_qa = T * HEADS * 66, T * HEADS * 33
        va = abar_all[:, 0:n_va].rearrange("p (t h c) -> p t h c", t=T, h=HEADS)
        qa = abar_all[:, n_va:n_va + n_qa].rearrange("p (t h c) -> p t h c", t=T, h=HEADS)
        rest = sb("rest", [P, T, D], f32)
        wh = sb("wh", [P, T, D + 2 * HEADS], f32)
        rden = sb("rden", [P, T], f32)
        stats = sb("stats", [P, T, 6], f32)
        mv = sb("mv", [P, T, 2], f32)
        std = sb("std", [P, T], f32)
        mx = sb("mx", [P, T], f32)
        mpart = sb("mpart", [P, T], bf16)
        m3 = sb("m3", [P, 96], f32)
        mt3 = sb("mt3", [96, P], bf16)
        smax = sb("smax", [P, HEADS], f32)
        gmax = sb("gmax", [P, HEADS], f32)
        sc = sb("sc", [P, 3, T, HEADS], f32)
        ex = sb("ex", [P, 4, T, HEADS], f32)
        nsrc = sb("nsrc", [P, T, HEADS], f32)
        comb = sb("comb", [P, 2, T, 33], f32)

        M = sb("M", [P, CH, QB, N], u8)
        mrow_i = sb("mrow_i", [P, QB, CH], i32)
        mrow = sb("mrow", [P, QB, CH], f32)
        cnt = sb("cnt", [P, QB, CH], f32)
        side = sb("side", [P, 2, QB, CH], f32)
        around = sb("around", [P, 2, QB], f32)
        idx = sb("idx", [P, QB, CH], f32)
        tcol = sb("tcol", [P, 1], f32)
        upper = sb("upper", [P, QB, W32], f32)
        cw = sb("cw", [P, QB, W32], f32)
        cu = sb("cu", [P, QB, W32], f32)
        dwin = sb("dwin", [P, QB, W32 + 1], f32)
        keepz = sb("keepz", [P, QB, W32 + 1], f32)
        rk = sb("rk", [P, QB, W32 + 1], f32)
        rem = sb("rem", [P, QB, W32], f32)
        rem2 = sb("rem2", [P, QB, W32], f32)
        remT = sb("remT", [P, QB, W32], f32)
        e1 = sb("e1", [P, QB, W32], f32)
        small = sb("small", [P, 5, QB], f32)
        num, half_up, first, last, tiny = (small[:, i, :] for i in range(5))
        fl = sb("fl", [P, W32], f32)
        flT = sb("flT", [P, W32], f32)
        fl0 = sb("fl0", [1, P], f32)
        flag = sb("flag", [1, 1], i32)
        rank = sb("rank", [P, QB, N], f16)
        rm = sb("rm", [P, QB, N], f16)
        rmT = rank

        ps = ctx.enter_context(nc.psum_tensor("ps", [P, SLOTS, N], f32))

        s_const = sem("const_ready")
        s_turn = sem("gpsimd_waited")
        s_w = sem("weights_loaded")
        s_wt = sem("weights_transposed")
        s_wtc = sem("weights_copied")
        s_wa = sem("wa_in_psum")
        s_wac = sem("wa_copied")
        s_dconst = sem("vector_constants")
        full = {k: sem(f"{k}_in_psum") for k in counts(USES)}
        read = {k: sem(f"{k}_read") for k in counts(USES)}
        s_adj = [sem(f"adj{i}_loaded") for i in range(2)]
        s_x = sem("x_loaded")
        s_parts = sem("y_parts_ready")
        s_abar = sem("abar_ready")
        s_var = sem("variance_ready")
        s_std = sem("std_ready")
        s_xn = sem("xn_ready")
        s_xnst = sem("x3_stored")
        s_m3 = sem("row_max_parts_ready")
        s_clamped = sem("p_clamped")
        s_smax = sem("src_max_of_partitions")
        s_gmax = sem("src_max_everywhere")
        s_sc = sem("exponents_ready")
        s_ex = sem("exponentials_ready")
        s_va = sem("values_weighted")
        s_vh = sem("value_part_rounded")
        s_ind = sem("indicator_ready")
        s_hT = sem("x3t_stored")
        s_M = sem("dilation_loaded")
        s_dil = sem("dilation_done")
        s_Mst = sem("dilation_stored")

        cn = counts(USES)

        def nth(b, kind_count, i=0):
            return b * kind_count + (i + 1)

        def graphs():
            return [(h, 0, G // 4) for h in range(2)]

        block = ctx.enter_context(nc.Block())

        @block.sync
        def _(sp):
            for i, w in enumerate((Wv, Wk, Wq, U0, W2)):
                sp.dma_start(wload[:, i, :], w).then_inc(s_w, 16)
            sp.dma_start(bqk[:, 0:1], bq.rearrange("(d o) -> d o", o=1)).then_inc(s_w, 16)
            sp.dma_start(bqk[:, 1:2], bk.rearrange("(d o) -> d o", o=1)).then_inc(s_w, 16)
            sp.wait_ge(s_const, 1)
            sp.dma_start(bvrow[0:1, :], bv.rearrange("(o d) -> o d", o=1)).then_inc(s_w, 16)
            for h in range(HEADS):
                for e in range(2):
                    sp.dma_start(ablk[DH * h:DH * h + DH, HEADS * e + h:HEADS * e + h + 1],
                                 a2[h, DH * e:DH * e + DH].rearrange("(d o) -> d o", o=1)).then_inc(s_w, 16)

            def graph(b, first_one):
                if not first_one:
                    sp.wait_ge(read["agg"], b * cn["agg"])
                sp.dma_start(x_in[:, :, :], x[b].rearrange("(t p) d -> p t d", p=P)).then_inc(s_x, 16)
                if not first_one:
                    store(b - 1)

            def store(b):
                sp.wait_ge(s_xn, nth(b, 3, 2))
                sp.dma_start(x3_dram[b].rearrange("(t p) d -> p t d", p=P), xn[:, :, :]).then_inc(s_xnst, 16)
                sp.wait_ge(read["x3t"], nth(b, 1))
                sp.dma_start(h_dram[0, b], xT[:, :]).then_inc(s_hT, 16)

            graph(0, True)
            graph(1, False)
            with sp.Fori(2, G) as b:
                graph(b, False)
            store(G - 1)
            sp.wait_ge(s_xnst, 16 * G)
            sp.wait_ge(s_hT, 16 * G)

        @block.gpsimd
        def _(gp):
            GP.memset(bvrow[:, :], 0.0)
            GP.memset(ablk[:, :], 0.0)
            GP.memset(ident[:, :], 0.0)
            GP.memset(row0[:, :], 0.0)
            GP.memset(sel[:, :, :], 0.0)
            GP.memset(m3[:, :], 0.0)
            GP.memset(upper[:, :, :], 0.0)
            GP.memset(eps_t[:, :], EPS)
            GP.iota(idx[:, :, :], [[0, QB], [1, CH]], base=0, channel_multiplier=0,
                    allow_small_or_imprecise_dtypes=True)
            gp.drain()
            GP.memset(row0[0:1, :], 1.0)
            GP.affine_select(out=ident[:, :], in_=ident[:, :], compare_op=ALU.not_equal, fill=1.0,
                             base=0, pattern=[[-1, P]], channel_multiplier=1)
            gp.drain()
            for part in range(3):
                GP.affine_select(out=sel[32 * part:32 * part + 32, :, :], in_=sel[32 * part:32 * part + 32, :, :],
                                 compare_op=ALU.not_equal, fill=1.0, base=0,
                                 pattern=[[-1, T], [0, P]], channel_multiplier=1)
                gp.drain()
            for q in range(4):
                u = upper[32 * q:32 * q + 32, :, :]
                GP.affine_select(out=u, in_=u, compare_op=ALU.is_ge, fill=1.0, base=0,
                                 pattern=[[0, QB], [-1, W32]], channel_multiplier=1)
                gp.drain()
            gp.drain()
            GP.tensor_copy(ident16[:, :], ident[:, :])
            GP.tensor_scalar(bigI[:, :], ident[:, :], -BIG, None, ALU.mult)
            gp.drain().then_inc(s_const, 1)

            def load_adj(b, par, first_one=False):
                if not first_one:
                    gp.wait_ge(full["ph"], (b - 1) * cn["ph"])
                    gp.wait_ge(s_ind, (b - 1) * HEADS)
                gp.dma_start(adjb[par][:, :, :], adj[b].rearrange("(t p) c -> p t c", p=P)).then_inc(s_adj[par], 16)

            def load_dilation(half):
                for q in range(4):
                    for g in range(QB):
                        b = GROUP * half + QB * q + g
                        gp.dma_start(M[32 * q:32 * q + 32, :, g, :],
                                     adj[b].rearrange("(s r) c -> r s c", r=W32)).then_inc(s_M, 16)
                        gp.dma_start(mrow_i[32 * q:32 * q + 32, g, :], mask_rows[b]).then_inc(s_M, 16)

            def store_dilation(half):
                gp.wait_ge(s_dil, half + 1)
                for q in range(4):
                    for g in range(QB):
                        b = GROUP * half + QB * q + g
                        gp.dma_start(dilated[b].rearrange("(s r) c -> r s c", r=W32),
                                     M[32 * q:32 * q + 32, :, g, :]).then_inc(s_Mst, 16)
                gp.wait_ge(s_Mst, 16 * GROUP * (half + 1))

            load_adj(0, 0, True)
            load_adj(1, 1, True)
            for half, lo, hi in graphs():
                load_dilation(half)
                def pair_of(pair, more):
                    for par in range(2):
                        b = pair * 2 + (GROUP * half + par)
                        for n in range(cn["pt"]):
                            gp.wait_ge(read["pt"], nth(b, cn["pt"], n))
                            gp.sem_inc(s_turn, 1)
                            piece = pT[:, (n // 2) % 2, 4 * (n % 2):4 * (n % 2) + 4, :]
                            GP.tensor_scalar(piece, piece, 1.0, None, ALU.min)
                            gp.drain().then_inc(s_clamped, 1)
                        gp.wait_ge(s_smax, nth(b, 1))
                        gp.sem_inc(s_turn, 1)
                        GP.partition_all_reduce(gmax[:, :], smax[:, :], P, bass.bass_isa.ReduceOp.max).then_inc(s_gmax, 1)
                        if more:
                            load_adj(b + 2, par)

                with gp.Fori(lo, hi - half) as pair:
                    pair_of(pair, True)
                if half:
                    pair_of(hi - 1, False)
                store_dilation(half)

        @block.tensor
        def _(pe):
            pe.wait_ge(s_const, 1)
            pe.wait_ge(s_w, 16 * 16)
            for i, w in enumerate((0, 1, 2, 4)):
                PE.transpose(ps[:, 0, P * i:P * i + P], wload[:, w, :], ident[:, :])
            pe.drain().then_inc(s_wt, 1)
            pe.wait_ge(s_wtc, 1)
            PE.matmul(ps[:, 1, 0:2 * HEADS], wt[:, 3, :], ablk[:, :], start=True, stop=True).then_inc(s_wa, 1)
            pe.wait_ge(s_wac, 1)

            def graph(b, par, first_one):
                at = [0]

                def slot():
                    n = at[0]
                    at[0] += 1
                    m, before = earlier_use(USES, n)
                    kind = USES[m]
                    if before and not first_one:
                        pe.wait_ge(read[kind], nth(b - 1, cn[kind], number(USES, m)))
                    elif not before:
                        pe.wait_ge(read[kind], nth(b, cn[kind], number(USES, m)))
                    return ps[:, n % SLOTS, :]

                def transposes(kind, src):
                    o = slot()
                    for t in range(T):
                        ins = PE.transpose(o[:, P * t:P * t + P], src[:, t, :], ident[:, :])
                    ins.then_inc(full[kind], 1)

                pe.wait_ge(s_x, 16 * (b + 1))
                transposes("xt", x_in)
                o = slot()
                pe.wait_ge(read["xt"], nth(b, 1))
                for t in range(T):
                    ins = PE.matmul(o[:, P * t:P * t + P], xT[:, P * t:P * t + P], wload[:, 3, :], start=True, stop=True)
                ins.then_inc(full["y"], 1)
                pe.wait_ge(s_adj[par], b * 8 + (16 - 8 * par))
                pe.wait_ge(s_parts, nth(b, 1))
                for i in range(T):
                    if i % 4 == 0:
                        o = slot()
                    r = 256 * (i % 4)
                    for j in range(T):
                        w = adjb[par][:, j, P * i:P * i + P]
                        PE.matmul(o[:, r:r + 129], w, y3[:, 0, j, :], start=(j == 0), stop=False)
                        PE.matmul(o[:, r:r + 128], w, y3[:, 1, j, 0:D], start=False, stop=False)
                        ins = PE.matmul(o[:, r:r + 128], w, y3[:, 2, j, 0:D], start=False, stop=(j == T - 1))
                    if i % 4 == 3:
                        ins.then_inc(full["agg"], 1)

                pe.wait_ge(s_xn, nth(b, 3, 0))
                transposes("x1t", xn)
                for kind, w in (("q", 2), ("k", 1)):
                    o = slot()
                    pe.wait_ge(read["x1t"], nth(b, 1))
                    for c in range(2):
                        ins = PE.matmul(o[:, HALF * c:HALF * c + HALF], wt[:, w, :], xT[:, HALF * c:HALF * c + HALF],
                                        start=True, stop=True)
                    ins.then_inc(full[kind], 1)
                o = slot()
                for t in range(T):
                    PE.matmul(o[:, P * t:P * t + P], xT[:, P * t:P * t + P], wt[:, 0, :], start=True, stop=False)
                    ins = PE.matmul(o[:, P * t:P * t + P], row0[:, :], bvrow[:, :], start=False, stop=True)
                ins.then_inc(full["v"], 1)
                pe.wait_ge(read["q"], nth(b, 1))
                pe.wait_ge(read["k"], nth(b, 1))
                pe.wait_ge(s_abar, nth(b, 1))
                for i in range(T):
                    o = slot()
                    for c in range(2):
                        cols = slice(HALF * c, HALF * c + HALF)
                        PE.matmul(o[:, cols], bigI[:, :], abar[:, i, cols], start=True, stop=False)
                        ins = PE.matmul(o[:, cols], qT[:, P * i:P * i + P], kT[:, cols], start=False, stop=True)
                    ins.then_inc(full["s"], 1)
                o = slot()
                pe.wait_ge(s_m3, nth(b, 1))
                PE.transpose(o[0:96, 0:P], m3[:, :], ident[:, :]).then_inc(full["mt"], 1)

                def scores_t(quarter):
                    for jh in range(2):
                        o = slot()
                        if quarter == 0 and jh == 0:
                            pe.wait_ge(read["mt"], nth(b, 1))
                        for jj in range(4):
                            j, r = 4 * jh + jj, 256 * jj
                            for e in range(2):
                                PE.matmul(o[:, r + P * e:r + P * e + P], abar[:, 2 * quarter + e, P * j:P * j + P],
                                          bigI[:, :], start=(jj % 2 == 0 and e == 0), stop=False)
                            PE.matmul(o[:, r:r + 256], kT[:, P * j:P * j + P], qT[:, 256 * quarter:256 * quarter + 256],
                                      start=False, stop=False)
                            for e in range(2):
                                ins = PE.matmul(o[:, r + P * e:r + P * e + P], sel[:, 2 * quarter + e, :], mt3[:, :],
                                                start=False, stop=(jj % 2 == 1 and e == 1))
                        ins.then_inc(full["pt"], 1)

                def weighted_v(quarter):
                    o = slot()
                    pe.wait_ge(s_clamped, nth(b, cn["pt"], 2 * quarter + 1))
                    if quarter == 0:
                        pe.wait_ge(read["v"], nth(b, 1))
                    for e in range(2):
                        for j in range(T):
                            ins = PE.matmul(o[:, 256 * e:256 * e + 129], pT[:, quarter % 2, j, P * e:P * e + P], vo[:, j, :],
                                            start=(j == 0), stop=(j == T - 1))
                    ins.then_inc(full["o"], 1)

                scores_t(0)
                scores_t(1)
                weighted_v(0)
                scores_t(2)
                weighted_v(1)
                scores_t(3)
                weighted_v(2)
                weighted_v(3)

                pe.wait_ge(s_xn, nth(b, 3, 1))
                transposes("x2t", xn)
                for t in range(T):
                    if t % 4 == 0:
                        o = slot()
                    if t == 0:
                        pe.wait_ge(read["x2t"], nth(b, 1))
                    r = 256 * (t % 4)
                    ins = PE.matmul(o[:, r:r + D + 2 * HEADS], xT[:, P * t:P * t + P], wext[:, :], start=True, stop=True)
                    if t % 4 == 3:
                        ins.then_inc(full["wh"], 1)
                for j in range(T):
                    if j % 4 == 0:
                        o = slot()
                    if j == 0:
                        pe.wait_ge(s_vh, nth(b, 3, 2))
                    r = 256 * (j % 4)
                    for i in range(T):
                        for s in range(3):
                            ins = PE.matmul(o[:, r:r + HEADS * 33].rearrange("p (h c) -> p h c", h=HEADS),
                                            adjb[par][:, i, P * j:P * j + P], vs[:, i, s, :, 33:66],
                                            start=(i == 0 and s == 0), stop=(i == T - 1 and s == 2))
                    if j % 4 == 3:
                        ins.then_inc(full["qa"], 1)

                def dst_scores(h):
                    o = slot()
                    for c in range(2):
                        ins = PE.matmul(o[:, HALF * c:HALF * c + HALF], wab[:, h, :], xT[:, HALF * c:HALF * c + HALF],
                                        start=True, stop=True)
                    ins.then_inc(full["sj"], 1)

                def head(h):
                    o = slot()
                    pe.wait_ge(s_ind, nth(b, HEADS, h))
                    for j in range(T):
                        for i in range(T):
                            for s in range(3):
                                ins = PE.matmul(o[:, P * j:P * j + 66], ind[:, h % 2, i, P * j:P * j + P], vs[:, i, s, h, :],
                                                start=(i == 0 and s == 0), stop=(i == T - 1 and s == 2))
                    ins.then_inc(full["ph"], 1)

                dst_scores(0)
                dst_scores(1)
                head(0)
                dst_scores(2)
                head(1)
                dst_scores(3)
                head(2)
                head(3)
                pe.wait_ge(s_xn, nth(b, 3, 2))
                transposes("x3t", xn)
                assert at[0] == len(USES)

            graph(0, 0, True)
            graph(1, 1, False)
            with pe.Fori(1, G // 2) as pair:
                for par in range(2):
                    graph(pair * 2 + par, par, False)

        @block.scalar
        def _(act):
            act.wait_ge(s_wt, 1)
            A.copy(wt[:, :, :], ps[:, 0, 0:4 * P].rearrange("p (i d) -> p i d", i=4))
            A.copy(wext[:, 0:D], wload[:, 4, :])
            act.drain().then_inc(s_wtc, 1)
            act.wait_ge(s_wa, 1)
            A.copy(wext[:, D:D + 2 * HEADS], ps[:, 1, 0:2 * HEADS])
            act.drain()
            for h in range(HEADS):
                A.copy(wab[:, h, :], wext[:, D + HEADS + h:D + HEADS + h + 1].broadcast_to([P, P]))
            act.drain().then_inc(s_wac, 1)

            def graph(b):
                at = [0]

                def slot(kind):
                    n = USES.index(kind, at[0])
                    at[0] = n + 1
                    act.wait_ge(full[kind], nth(b, cn[kind], number(USES, n)))
                    return ps[:, n % SLOTS, :]

                def std_of(which):
                    act.wait_ge(s_var, nth(b, 3, which))
                    A.activation(std[:, :], mv[:, :, 1], ACT.Sqrt, bias=eps_t[:, 0:1]).then_inc(s_std, 1)

                if not (isinstance(b, int) and b == 0):
                    act.wait_ge(s_hT, b * 16)
                A.copy(xT[:, :], slot("xt")).then_inc(read["xt"], 1)
                std_of(0)
                A.copy(xT[:, :], slot("x1t")).then_inc(read["x1t"], 1)
                A.activation(qT, slot("q"), ACT.Relu, bias=bqk[:, 0:1]).then_inc(read["q"], 1)
                A.activation(kT, slot("k"), ACT.Relu, bias=bqk[:, 1:2]).then_inc(read["k"], 1)
                A.activation(vo[:, :, 0:D], slot("v").rearrange("p (t d) -> p t d", t=T), ACT.Relu).then_inc(read["v"], 1)
                A.copy(mt3[:, :], slot("mt")[0:96, 0:P]).then_inc(read["mt"], 1)
                for n in range(cn["pt"]):
                    if n >= 4:
                        act.wait_ge(full["o"], nth(b, cn["o"], n // 2 - 2))
                    A.activation(pT[:, (n // 2) % 2, 4 * (n % 2):4 * (n % 2) + 4, :],
                                 slot("pt").rearrange("p (j i) -> p j i", j=4), ACT.Exp).then_inc(read["pt"], 1)
                std_of(1)
                A.copy(xT[:, :], slot("x2t")).then_inc(read["x2t"], 1)
                for c in range(2):
                    A.copy(wh[:, 4 * c:4 * c + 4, :],
                           slot("wh").rearrange("p (t d) -> p t d", t=4)[:, :, 0:D + 2 * HEADS]).then_inc(read["wh"], 1)
                act.wait_ge(s_sc, nth(b, 1))
                A.activation(ex[:, 0], sc[:, 0], ACT.Exp)
                A.activation(ex[:, 1], sc[:, 0], ACT.Exp, scale=SLOPE)
                A.activation(ex[:, 2], sc[:, 1], ACT.Exp, scale=1.0 - SLOPE)
                A.activation(ex[:, 3], sc[:, 2], ACT.Exp, scale=SLOPE - 1.0)
                act.drain().then_inc(s_ex, 1)
                for s in range(3):
                    act.wait_ge(s_va, nth(b, 3, s))
                    A.copy(vs[:, :, s, :, :], va[:, :, :, :]).then_inc(s_vh, 1)
                for c in range(2):
                    A.copy(qa[:, 4 * c:4 * c + 4, :, :].rearrange("p t h c -> p t (h c)"),
                           slot("qa").rearrange("p (t d) -> p t d", t=4)[:, :, 0:HEADS * 33]).then_inc(read["qa"], 1)
                std_of(2)
                A.copy(xT[:, :], slot("x3t")).then_inc(read["x3t"], 1)

            graph(0)
            with act.Fori(1, G) as b:
                graph(b)

        @block.vector
        def _(v):
            V.memset(keepz[:, :, :], 1.0)
            V.memset(fl[:, :], 0.0)
            V.memset(tcol[:, :], -1.0)
            v.drain()
            V.memset(keepz[:, :, 0:1], 0.0)
            v.wait_ge(s_const, 1)
            v.drain()

            def flat(t):
                return t[:, :, :].rearrange("p a b -> p (a b)")

            def spread(t):
                return t.unsqueeze(2).broadcast_to([P, QB, W32])

            def removed_in_window(dest):
                V.tensor_tensor_scan(flat(rk), flat(keepz), flat(dwin), 0.0, ALU.mult, ALU.add)
                v.drain()
                V.tensor_tensor(num, rk[:, :, W32], around[:, 1, :], ALU.add)
                v.drain()
                V.tensor_scalar(half_up, num, 0.5, MAGIC, ALU.mult, ALU.add)
                V.tensor_scalar(tiny, num, 2.0, 2.0, ALU.is_lt, ALU.mult)
                v.drain()
                V.tensor_scalar(half_up, half_up, MAGIC, None, ALU.subtract)
                v.drain()
                V.scalar_tensor_tensor(first, num, 11.0, half_up, ALU.is_ge, ALU.mult)
                v.drain()
                V.scalar_tensor_tensor(last, first, 2.0, tiny, ALU.mult, ALU.add)
                V.tensor_tensor(e1[:, :, :], rk[:, :, 1:W32 + 1], spread(first), ALU.is_equal)
                v.drain()
                V.tensor_tensor(dest[:, :, :], rk[:, :, 1:W32 + 1], spread(last), ALU.is_ge)
                v.drain()
                V.tensor_tensor(dest[:, :, :], dest[:, :, :], e1[:, :, :], ALU.max)
                v.drain()
                V.tensor_tensor(dest[:, :, :], dest[:, :, :], cu[:, :, :], ALU.mult)
                v.drain()

            def dilation_step(t):
                V.tensor_scalar(tcol[:, :], tcol[:, :], 1.0, None, ALU.add)
                V.tensor_reduce(cnt[:, :, :], M[:, t, :, :].rearrange("p b (s c) -> p b s c", c=W32), AX.X, ALU.add)
                V.tensor_copy(cw[:, :, :], M[:, t, :, bass.ds(t * W32, W32)])
                v.drain()
                V.scalar_tensor_tensor(side[:, 0], idx[:, :, :], tcol[:, 0:1], cnt[:, :, :], ALU.is_lt, ALU.mult)
                V.scalar_tensor_tensor(side[:, 1], idx[:, :, :], tcol[:, 0:1], cnt[:, :, :], ALU.is_gt, ALU.mult)
                V.tensor_tensor(cu[:, :, :], cw[:, :, :], upper[:, :, :], ALU.mult)
                V.tensor_copy(dwin[:, :, 1:W32 + 1], cw[:, :, :])
                v.drain()
                V.tensor_reduce(around[:, :, :], side[:, :, :, :], AX.X, ALU.add)
                V.tensor_tensor(cu[:, :, :], cu[:, :, :], mrow[:, :, bass.ds(t, 1)].broadcast_to([P, QB, W32]), ALU.mult)
                v.drain()
                V.tensor_copy(dwin[:, :, 0], around[:, 0, :])
                V.tensor_scalar(around[:, 1, :], around[:, 1, :], 0.5, None, ALU.add)
                v.drain()
                removed_in_window(rem)
                V.memset(flag[:, :], 1)
                v.drain()
                with v.While(lambda: v.value_load(flag[0:1, 0:1], min_val=0, max_val=1) != 0):
                    V.transpose(flat(remT), flat(rem))
                    v.drain()
                    V.tensor_tensor(dwin[:, :, 1:W32 + 1], cw[:, :, :], remT[:, :, :], ALU.is_gt)
                    v.drain()
                    removed_in_window(rem2)
                    V.tensor_tensor(e1[:, :, :], rem2[:, :, :], rem[:, :, :], ALU.not_equal)
                    v.drain()
                    V.tensor_copy(rem[:, :, :], rem2[:, :, :])
                    V.tensor_reduce(fl[:, 0:1], e1[:, :, :], AX.XY, ALU.max)
                    v.drain()
                    V.transpose(flT[:, :], fl[:, :])
                    v.drain()
                    for q in range(4):
                        V.tensor_copy(fl0[0:1, 32 * q:32 * q + 32], flT[32 * q:32 * q + 1, :])
                    v.drain()
                    V.tensor_reduce(flag[:, :], fl0[:, :], AX.X, ALU.max)
                    v.drain()
                V.tensor_copy(M[:, t, :, bass.ds(t * W32, W32)], dwin[:, :, 1:W32 + 1])
                v.drain()
                for g in range(QB):
                    V.tensor_tensor_scan(rank[:, g, :], M[:, t, g, :], M[:, t, g, :], 0.0, ALU.add, ALU.max)
                v.drain()
                for g in range(QB):
                    V.tensor_scalar(rm[:, g, :], rank[:, g, :], small[:, 2, g:g + 1], None, ALU.is_equal)
                v.drain()
                for g in range(QB):
                    V.scalar_tensor_tensor(rm[:, g, :], rank[:, g, :], small[:, 3, g:g + 1], rm[:, g, :], ALU.is_ge, ALU.max)
                v.drain()
                for g in range(QB):
                    V.scalar_tensor_tensor(rm[:, g, :], rm[:, g, :], mrow[:, g, bass.ds(t, 1)], M[:, t, g, :], ALU.mult, ALU.mult)
                v.drain()
                V.tensor_tensor(M[:, t, :, :], M[:, t, :, :], rm[:, :, :], ALU.is_gt)
                for g in range(QB):
                    V.transpose(rmT[:, g, :], rm[:, g, :])
                v.drain()
                for g in range(QB):
                    V.tensor_tensor(M[:, :, g, bass.ds(t * W32, W32)], M[:, :, g, bass.ds(t * W32, W32)],
                                    rmT[:, g, :].rearrange("p (s c) -> p s c", c=W32), ALU.is_gt)
                v.drain()

            def graph(b, par, steps):
                at = [0]

                def slot(kind):
                    n = USES.index(kind, at[0])
                    at[0] = n + 1
                    v.wait_ge(full[kind], nth(b, cn[kind], number(USES, n)))
                    return ps[:, n % SLOTS, :]

                def layernorm(which):
                    v.drain()
                    for t in range(T):
                        V.bn_stats(stats[:, t, :], xn[:, t, :])
                    v.drain()
                    for t in range(T):
                        V.bn_aggr(mv[:, t, :], stats[:, t, :])
                    v.drain().then_inc(s_var, 1)
                    v.wait_ge(s_std, nth(b, 3, which))
                    V.reciprocal(rden[:, :], std[:, :])
                    v.drain()
                    for t in range(T):
                        V.tensor_scalar(xn[:, t, :], xn[:, t, :], mv[:, t, 0:1], rden[:, t:t + 1], ALU.subtract, ALU.mult)
                    v.drain().then_inc(s_xn, 1)

                v.wait_ge(s_adj[par], b * 8 + (16 - 8 * par))
                V.memset(y3[:, 0, :, D:D + 1], 1.0)
                V.tensor_scalar(abar[:, :, :], adjb[par][:, :, :], 0.0, None, ALU.is_le)
                v.drain().then_inc(s_abar, 1)
                y = slot("y").rearrange("p (t d) -> p t d", t=T)
                V.tensor_copy(y3[:, 0, :, 0:D], y)
                v.drain()
                V.tensor_tensor(rest[:, :, :], y, y3[:, 0, :, 0:D], ALU.subtract).then_inc(read["y"], 1)
                v.drain()
                V.tensor_copy(y3[:, 1, :, 0:D], rest[:, :, :])
                v.drain()
                V.tensor_tensor(rest[:, :, :], rest[:, :, :], y3[:, 1, :, 0:D], ALU.subtract)
                v.drain()
                V.tensor_copy(y3[:, 2, :, 0:D], rest[:, :, :]).then_inc(s_parts, 1)
                if not (isinstance(b, int) and b == 0):
                    v.wait_ge(s_xnst, b * 16)
                for c in range(2):
                    a = slot("agg").rearrange("p (t d) -> p t d", t=4)
                    V.reciprocal(rden[:, 4 * c:4 * c + 4], a[:, :, D])
                    v.drain()
                    for t in range(4):
                        V.tensor_scalar(xn[:, 4 * c + t, :], a[:, t, 0:D], rden[:, 4 * c + t:4 * c + t + 1], 0.0,
                                        ALU.mult, ALU.max)
                    v.drain()
                    V.tensor_tensor(xn[:, 4 * c:4 * c + 4, :], xn[:, 4 * c:4 * c + 4, :], x_in[:, 4 * c:4 * c + 4, :],
                                    ALU.add).then_inc(read["agg"], 1)
                layernorm(0)

                V.memset(vo[:, :, D:D + 1], 1.0)
                for i in range(T):
                    V.reduce_max(mx[:, i:i + 1], slot("s"), AX.X).then_inc(read["s"], 1)
                v.drain()
                V.tensor_scalar(mx[:, :], mx[:, :], CLAMP, -1.0, ALU.min, ALU.mult)
                v.drain()
                for part in range(3):
                    V.tensor_copy(mpart[:, :], mx[:, :])
                    v.drain()
                    V.tensor_copy(m3[:, 32 * part:32 * part + T], mpart[:, :])
                    if part < 2:
                        V.tensor_tensor(mx[:, :], mx[:, :], mpart[:, :], ALU.subtract)
                    v.drain()
                v.sem_inc(s_m3, 1)
                if steps:
                    steps(0)
                for quarter in range(4):
                    o = slot("o")[:, 0:512].rearrange("p (e d) -> p e d", e=2)
                    V.reciprocal(rden[:, 0:2], o[:, :, D])
                    v.drain()
                    for e in range(2):
                        t = 2 * quarter + e
                        V.scalar_tensor_tensor(xn[:, t, :], o[:, e, 0:D], rden[:, e:e + 1], xn[:, t, :], ALU.mult, ALU.add)
                    v.drain().then_inc(read["o"], 1)
                layernorm(1)

                v.wait_ge(read["wh"], nth(b, cn["wh"], 1))
                V.tensor_reduce(smax[:, :], wh[:, :, D:D + HEADS].rearrange("p t h -> p h t"), AX.X, ALU.max).then_inc(s_smax, 1)
                V.tensor_scalar(nsrc[:, :, :], wh[:, :, D:D + HEADS], -1.0, None, ALU.mult)
                v.wait_ge(s_gmax, nth(b, 1))
                top = gmax[:, :].unsqueeze(1).broadcast_to([P, T, HEADS])
                V.tensor_tensor(sc[:, 0], wh[:, :, D:D + HEADS], top, ALU.subtract)
                V.tensor_tensor(sc[:, 2], wh[:, :, D + HEADS:D + 2 * HEADS], top, ALU.add)
                v.drain()
                V.tensor_scalar(sc[:, 1], sc[:, 2], 0.0, None, ALU.min)
                v.drain()
                V.tensor_scalar(sc[:, 2], sc[:, 2], 0.0, None, ALU.max)
                v.drain().then_inc(s_sc, 1)
                v.wait_ge(s_ex, nth(b, 1))
                whh = wh[:, :, 0:D].rearrange("p t (h c) -> p t h c", h=HEADS)
                for e in range(2):
                    V.tensor_tensor(va[:, :, :, 33 * e:33 * e + DH], whh, ex[:, e].unsqueeze(3).broadcast_to([P, T, HEADS, DH]),
                                    ALU.mult)
                    V.tensor_copy(va[:, :, :, 33 * e + DH], ex[:, e])
                v.drain().then_inc(s_va, 1)
                for s in range(2):
                    v.wait_ge(s_vh, nth(b, 3, s))
                    V.tensor_tensor(va[:, :, :, :], va[:, :, :, :], vs[:, :, s, :, :], ALU.subtract).then_inc(s_va, 1)

                def indicator(h):
                    o = slot("sj")
                    if h >= 2:
                        v.wait_ge(full["ph"], nth(b, HEADS, h - 2))
                    for i in range(T):
                        V.scalar_tensor_tensor(ind[:, h % 2, i, :], o, nsrc[:, i, h:h + 1], adjb[par][:, i, :],
                                               ALU.is_ge, ALU.mult)
                    v.drain().then_inc(read["sj"], 1)
                    v.sem_inc(s_ind, 1)

                def combine(h):
                    o = slot("ph").rearrange("p (t d) -> p t d", t=T)
                    if h == 0:
                        v.wait_ge(read["qa"], nth(b, cn["qa"], 1))
                    V.tensor_tensor(comb[:, 1], qa[:, :, h, :], o[:, :, 33:66], ALU.subtract)
                    V.tensor_tensor(comb[:, 0], o[:, :, 0:33], ex[:, 2, :, h].unsqueeze(2).broadcast_to([P, T, 33]), ALU.mult)
                    v.drain().then_inc(read["ph"], 1)
                    V.tensor_tensor(comb[:, 1], comb[:, 1], ex[:, 3, :, h].unsqueeze(2).broadcast_to([P, T, 33]), ALU.mult)
                    v.drain()
                    V.tensor_tensor(comb[:, 0], comb[:, 0], comb[:, 1], ALU.add)
                    v.drain()
                    V.reciprocal(rden[:, :], comb[:, 0, :, DH])
                    v.drain()
                    V.tensor_tensor(comb[:, 0, :, 0:DH], comb[:, 0, :, 0:DH],
                                    rden[:, :].unsqueeze(2).broadcast_to([P, T, DH]), ALU.mult)
                    v.drain()
                    V.tensor_tensor(xn[:, :, DH * h:DH * h + DH], xn[:, :, DH * h:DH * h + DH], comb[:, 0, :, 0:DH], ALU.add)

                indicator(0)
                indicator(1)
                combine(0)
                indicator(2)
                combine(1)
                indicator(3)
                combine(2)
                if steps:
                    steps(1)
                combine(3)
                layernorm(2)

            def steps_of(t0):
                def steps(part):
                    for s in range(2):
                        dilation_step(t0 + (2 * part + s))
                return steps

            for half, lo, hi in graphs():
                v.wait_ge(s_M, 32 * GROUP * (half + 1))
                V.tensor_scalar(mrow[:, :, :], mrow_i[:, :, :], 0.0, None, ALU.not_equal)
                V.memset(tcol[:, :], -1.0)
                v.drain()
                if half == 0:
                    graph(0, 0, steps_of(0))
                    graph(1, 1, steps_of(4))
                with v.Fori(1 - half, hi) as pair:
                    for par in range(2):
                        graph(pair * 2 + (GROUP * half + par), par, steps_of(pair * 8 + 4 * par))
                v.drain().then_inc(s_dil, 1)


def layer_3(nc, S):
    f32, bf16, u8, i32 = mybir.dt.float32, mybir.dt.bfloat16, mybir.dt.uint8, mybir.dt.int32
    ALU, ACT, AX = mybir.AluOpType, mybir.ActivationFunctionType, mybir.AxisListType
    V, A, PE, GP = nc.vector, nc.scalar, nc.tensor, nc.gpsimd
    mask_tiles, blocks, Wl, bl = S.inputs_3
    ident, ident16, row0, eps_t = S.ident, S.ident16, S.row0, S.eps_t
    L = len(blocks)

    ctx = ExitStack()
    with ctx:
        def sb(name, shape, dt):
            return ctx.enter_context(nc.sbuf_tensor(name, shape, dt))

        def sem(name):
            return ctx.enter_context(nc.semaphore(name))

        wrx = sb("wrx", [P, L, 2 * D], f32)
        wrx_s = sb("wrx_s", [P, 2 * D], f32)
        wl = sb("wl", [P, L, D], f32)
        wl_s = sb("wl_s", [P, L, D], f32)
        brow = sb("brow", [P, L + 1, 2 * D], f32)
        gb = sb("gb", [P, L, 2], f32)
        crow = sb("crow", [P, 2 * D], f32)
        blrow = sb("blrow", [P, D], f32)
        mask_i = sb("mask_i", [P, G, T], i32)
        mf = sb("mf", [P, G, T], f32)
        ad = [sb(f"ad{i}", [P, T, N], bf16) for i in range(2)]
        adt = [sb(f"adt{i}", [P, T, N], bf16) for i in range(2)]
        hin = [sb(f"hin{i}", [P, L, N], f32) for i in range(2)]
        hout = [sb(f"hout{i}", [P, N], f32) for i in range(2)]
        rest = sb("rest3", [P, T, D], f32)
        z = sb("z", [P, T, D], f32)
        sq = sb("sq", [P, T, D], f32)
        junk = sb("junk", [P, N], f32)
        y3 = sb("y33", [P, 3, T, D + 1], bf16)
        rden = sb("rden3", [P, T], f32)
        ss = sb("ss", [P, T], f32)
        nrm = sb("nrm", [P, T], f32)
        sums = sb("sums", [P, 2, G], f32)
        bn = sb("bn", [P, 8], f32)
        betas = sb("betas", [P, L, P], f32)
        x3 = [sb(f"x3{i}", [P, T, D], f32) for i in range(2)]
        xo = [sb(f"xo{i}", [P, T, D], f32) for i in range(2)]
        stats = sb("stats3", [P, T, 6], f32)
        mv = sb("mv3", [P, T, 2], f32)
        std = sb("std3", [P, T], f32)
        ps = ctx.enter_context(nc.psum_tensor("ps3", [P, SLOTS, N], f32))

        cn = counts(USES_SAGE)
        full = {k: sem(f"sage_{k}_in_psum") for k in cn}
        read = {k: sem(f"sage_{k}_read") for k in cn}
        s_w = sem("sage_weights_loaded")
        s_ad = [sem(f"dilated{i}_loaded") for i in range(2)]
        s_adt = [sem(f"adt{i}_loaded") for i in range(2)]
        s_adts = [sem(f"adt{i}_stored") for i in range(2)]
        s_hin = [sem(f"h{i}_loaded") for i in range(2)]
        s_hs = [sem(f"h{i}_stored") for i in range(2)]
        s_parts = sem("sage_y_parts_ready")
        s_ss = sem("squares_summed")
        s_nrm = sem("norms_ready")
        s_r = sem("r_ready")
        s_bnv = sem("bn_variance_ready")
        s_bns = sem("bn_std_ready")
        s_beta = sem("beta_ready")
        s_crow = sem("crow_in_psum")
        s_crowc = sem("crow_copied")
        s_pin = [sem(f"final{i}_loaded") for i in range(2)]
        s_pp = sem("projection_in_psum")
        s_pr = sem("projection_read")
        s_var = sem("final_variance_ready")
        s_std = sem("final_std_ready")
        s_out = sem("out_ready")
        s_st = [sem(f"out{i}_stored") for i in range(2)]

        def nth(g, count, i=0):
            return g * count + (i + 1)

        def even(g, par):
            return g * 8 + (16 - 8 * par)

        def each_graph(eng, body):
            body(0, 0, True)
            body(1, 1, True)
            with eng.Fori(1, G // 2) as pair:
                for par in range(2):
                    body(pair * 2 + par, par, False)

        block = ctx.enter_context(nc.Block())

        @block.sync
        def _(sp):
            sp.dma_start(mask_i[:, :, :], mask_tiles).then_inc(s_w, 16)
            for l, (Wr, Wx, b, g, be) in enumerate(blocks):
                sp.dma_start(wrx[:, l, 0:D], Wr).then_inc(s_w, 16)
                sp.dma_start(wrx[:, l, D:2 * D], Wx).then_inc(s_w, 16)
                sp.dma_start(wl[:, l, :], Wl[D * l:D * l + D, :]).then_inc(s_w, 16)
                sp.dma_start(gb[:, l, 0:1], g.rearrange("(d o) -> d o", o=1)).then_inc(s_w, 16)
                sp.dma_start(gb[:, l, 1:2], be.rearrange("(d o) -> d o", o=1)).then_inc(s_w, 16)
            sp.wait_ge(S.zeroed, 1)
            for l, (Wr, Wx, b, g, be) in enumerate(blocks):
                sp.dma_start(brow[0:1, l, D:2 * D], b.rearrange("(o d) -> o d", o=1)).then_inc(s_w, 16)
            sp.dma_start(brow[0:1, L, 0:D], bl.rearrange("(o d) -> o d", o=1)).then_inc(s_w, 16)

            for l in range(L):
                def graph(b, par, peeled):
                    g = b + l * G
                    if l > 0:
                        sp.wait_ge(full["agg"], (g - 1) * cn["agg"])
                        sp.dma_start(adt[par][:, :, :], S.adt_dram[b]).then_inc(s_adt[par], 16)
                    if l > 0 or not peeled:
                        sp.wait_ge(full["yz"], (g - 1) * cn["yz"])
                    sp.dma_start(hin[par][:, 0, :], S.h_dram[l, b]).then_inc(s_hin[par], 16)
                    if not peeled:
                        store(g - 2, b - 2, par)

                def store(g, b, par):
                    if l == 0:
                        sp.wait_ge(read["adt"], nth(g, cn["adt"], T - 1))
                        sp.dma_start(S.adt_dram[b], adt[par][:, :, :]).then_inc(s_adts[par], 16)
                    sp.wait_ge(read["rt"], nth(g, 1))
                    sp.dma_start(S.h_dram[l + 1, b], hout[par][:, :]).then_inc(s_hs[par], 16)

                each_graph(sp, graph)
                for par in range(2):
                    store(l * G + G - 2 + par, G - 2 + par, par)
                for par in range(2):
                    sp.wait_ge(s_hs[par], 8 * G * (l + 1))
                    sp.wait_ge(s_adts[par], 8 * G)

            def final(b, par, peeled):
                if not peeled:
                    sp.wait_ge(s_pp, b - 1)
                    sp.wait_ge(s_out, b - 1)
                else:
                    sp.wait_ge(full["yz"], L * G * cn["yz"])
                for l in range(L):
                    sp.dma_start(hin[par][:, l, :], S.h_dram[l + 1, b]).then_inc(s_pin[par], 16)
                sp.dma_start(x3[par][:, :, :], S.x3_dram[b].rearrange("(t p) d -> p t d", p=P)).then_inc(s_pin[par], 16)
                if not peeled:
                    final_store(b - 2, par)

            def final_store(b, par):
                sp.wait_ge(s_out, nth(b, 1))
                sp.dma_start(S.out[b].rearrange("(t p) d -> p t d", p=P), xo[par][:, :, :]).then_inc(s_st[par], 16)

            each_graph(sp, final)
            for par in range(2):
                final_store(G - 2 + par, par)
            for par in range(2):
                sp.wait_ge(s_st[par], 8 * G)

        @block.gpsimd
        def _(gp):
            GP.memset(brow[:, :, :], 0.0)
            gp.drain().then_inc(S.zeroed, 1)

            def graph(b, par, peeled):
                if not peeled:
                    gp.wait_ge(full["adt"], (b - 1) * cn["adt"])
                gp.dma_start(ad[par][:, :, :], S.dilated[b].rearrange("(t p) c -> p t c", p=P)).then_inc(s_ad[par], 16)

            each_graph(gp, graph)

        @block.tensor
        def _(pe):
            pe.wait_ge(s_w, 16 * (1 + 5 * L + L + 1))
            PE.matmul(ps[:, 0, 0:2 * D], row0[:, :], brow[:, 0, :], start=True, stop=True).then_inc(s_crow, 1)
            pe.wait_ge(s_crowc, 1)

            for l in range(L):
                uses = USES_SAGE if l == 0 else USES_SAGE_LATER

                def graph(b, par, peeled):
                    g = b + l * G
                    at = [0]

                    def slot():
                        n = at[0]
                        at[0] += 1
                        m, before = earlier_use(uses, n)
                        kind = uses[m]
                        if not before:
                            pe.wait_ge(read[kind], nth(g, cn[kind], number(uses, m)))
                        elif not (isinstance(b, int) and b == 0):
                            pe.wait_ge(read[kind], nth(g - 1, cn[kind], number(uses, m)))
                        return ps[:, slot_of(n), :]

                    def slot_of(n):
                        return n % SLOTS

                    if l == 0:
                        pe.wait_ge(s_ad[par], even(b, par))
                        for j in range(T):
                            o = slot()
                            for i in range(T):
                                ins = PE.matmul(o[:, P * i:P * i + P], ad[par][:, i, P * j:P * j + P], ident16[:, :],
                                                start=True, stop=True)
                            ins.then_inc(full["adt"], 1)
                    pe.wait_ge(s_hin[par], even(g, par))
                    w = wrx[:, 0, :] if l == 0 else wrx_s[:, :]
                    for t in range(T):
                        if t % 4 == 0:
                            o = slot()
                        r = 256 * (t % 4)
                        ins = PE.matmul(o[:, r:r + 256], hin[par][:, 0, P * t:P * t + P], w, start=True, stop=True)
                        if t % 4 == 3:
                            ins.then_inc(full["yz"], 1)
                    if l == 0:
                        pe.wait_ge(read["adt"], nth(b, cn["adt"], T - 1))
                    else:
                        pe.wait_ge(s_adt[par], even(b + (l - 1) * G, par))
                    for i in range(T):
                        if i % 4 == 0:
                            o = slot()
                        if i == 0:
                            pe.wait_ge(s_parts, nth(g, 1))
                        r = 256 * (i % 4)
                        for j in range(T):
                            wj = adt[par][:, j, P * i:P * i + P]
                            PE.matmul(o[:, r:r + 129], wj, y3[:, 0, j, :], start=(j == 0), stop=False)
                            PE.matmul(o[:, r:r + 128], wj, y3[:, 1, j, 0:D], start=False, stop=False)
                            ins = PE.matmul(o[:, r:r + 128], wj, y3[:, 2, j, 0:D], start=False, stop=(j == T - 1))
                        if i % 4 == 3:
                            ins.then_inc(full["agg"], 1)
                    o = slot()
                    pe.wait_ge(s_r, nth(g, 1))
                    for t in range(T):
                        ins = PE.transpose(o[:, P * t:P * t + P], z[:, t, :], ident[:, :])
                    ins.then_inc(full["rt"], 1)

                each_graph(pe, graph)
                pe.wait_ge(s_beta, l + 1)
                if l < L - 1:
                    PE.matmul(ps[:, 0, 0:2 * D], betas[:, l, :], wrx[:, l + 1, :], start=True, stop=False)
                    PE.matmul(ps[:, 0, 0:2 * D], row0[:, :], brow[:, l + 1, :], start=False, stop=True).then_inc(s_crow, 1)
                else:
                    for m in range(L):
                        PE.matmul(ps[:, 0, 0:D], betas[:, m, :], wl[:, m, :], start=(m == 0), stop=(m == L - 1))
                    PE.matmul(ps[:, 1, 0:D], row0[:, :], brow[:, L, 0:D], start=True, stop=True).then_inc(s_crow, 1)
                pe.wait_ge(s_crowc, l + 2)

            def final(b, par, peeled):
                pe.wait_ge(s_pin[par], even(b, par) * (L + 1))
                if not peeled:
                    pe.wait_ge(s_pr, b - 1)
                for t in range(T):
                    for l in range(L):
                        ins = PE.matmul(ps[:, par, P * t:P * t + P], hin[par][:, l, P * t:P * t + P], wl_s[:, l, :],
                                        start=(l == 0), stop=(l == L - 1))
                ins.then_inc(s_pp, 1)

            each_graph(pe, final)

        @block.scalar
        def _(act):
            for l in range(L):
                uses = USES_SAGE if l == 0 else USES_SAGE_LATER

                def graph(b, par, peeled):
                    g = b + l * G
                    if l == 0:
                        if not peeled:
                            act.wait_ge(s_adts[par], even(b - 2, par))
                        for j in range(T):
                            act.wait_ge(full["adt"], nth(b, cn["adt"], j))
                            A.copy(adt[par][:, j, :], ps[:, j % SLOTS, :]).then_inc(read["adt"], 1)
                    act.wait_ge(s_ss, nth(g, 1))
                    A.activation(nrm[:, :], ss[:, :], ACT.Sqrt).then_inc(s_nrm, 1)
                    if l > 0 or not peeled:
                        act.wait_ge(s_hs[par], even(g - 2, par))
                    act.wait_ge(full["rt"], nth(g, 1))
                    o = ps[:, (len(uses) - 1) % SLOTS, :]
                    A.activation(hout[par][:, :], o, ACT.Copy, accum_out=sums[:, 0, bass.ds(b, 1)])
                    A.activation(junk[:, :], o, ACT.Square, accum_out=sums[:, 1, bass.ds(b, 1)])
                    act.drain().then_inc(read["rt"], 1)

                each_graph(act, graph)
                act.wait_ge(s_bnv, l + 1)
                A.activation(bn[:, 3:4], bn[:, 2:3], ACT.Sqrt, bias=eps_t[:, 0:1]).then_inc(s_bns, 1)

            def final(b, par, peeled):
                act.wait_ge(s_var, nth(b, 1))
                A.activation(std[:, :], mv[:, :, 1], ACT.Sqrt, bias=eps_t[:, 0:1]).then_inc(s_std, 1)

            each_graph(act, final)

        @block.vector
        def _(v):
            V.memset(y3[:, 0, :, D:D + 1], 1.0)
            v.wait_ge(s_w, 16 * (1 + 5 * L + L + 1))
            V.tensor_copy(mf[:, :, :], mask_i[:, :, :])
            v.wait_ge(s_crow, 1)
            V.tensor_copy(crow[:, :], ps[:, 0, 0:2 * D])
            v.drain().then_inc(s_crowc, 1)

            for l in range(L):
                uses = USES_SAGE if l == 0 else USES_SAGE_LATER
                yz0, agg0 = uses.index("yz"), uses.index("agg")

                def graph(b, par, peeled):
                    g = b + l * G
                    for c in range(2):
                        v.wait_ge(full["yz"], nth(g, cn["yz"], c))
                        o = ps[:, (yz0 + c) % SLOTS, :].rearrange("p (t d) -> p t d", t=4)
                        rows = slice(4 * c, 4 * c + 4)
                        V.tensor_tensor(rest[:, rows, :], o[:, :, 0:D], crow[:, 0:D].unsqueeze(1).broadcast_to([P, 4, D]), ALU.add)
                        V.tensor_tensor(z[:, rows, :], o[:, :, D:2 * D], crow[:, D:2 * D].unsqueeze(1).broadcast_to([P, 4, D]), ALU.add)
                        v.drain().then_inc(read["yz"], 1)
                    for s in range(3):
                        V.tensor_copy(y3[:, s, :, 0:D], rest[:, :, :])
                        v.drain()
                        if s < 2:
                            V.tensor_tensor(rest[:, :, :], rest[:, :, :], y3[:, s, :, 0:D], ALU.subtract)
                            v.drain()
                    v.sem_inc(s_parts, 1)
                    for c in range(2):
                        v.wait_ge(full["agg"], nth(g, cn["agg"], c))
                        o = ps[:, (agg0 + c) % SLOTS, :].rearrange("p (t d) -> p t d", t=4)
                        V.tensor_scalar(rden[:, 4 * c:4 * c + 4], o[:, :, D], 1.0, None, ALU.max)
                        v.drain()
                        V.reciprocal(rden[:, 4 * c:4 * c + 4], rden[:, 4 * c:4 * c + 4])
                        v.drain()
                        for t in range(4):
                            m = 4 * c + t
                            V.scalar_tensor_tensor(z[:, m, :], o[:, t, 0:D], rden[:, m:m + 1], z[:, m, :], ALU.mult, ALU.add)
                        v.drain().then_inc(read["agg"], 1)
                    V.tensor_tensor(sq[:, :, :], z[:, :, :], z[:, :, :], ALU.mult)
                    v.drain()
                    V.tensor_reduce(ss[:, :], sq[:, :, :], AX.X, ALU.add).then_inc(s_ss, 1)
                    v.wait_ge(s_nrm, nth(g, 1))
                    V.tensor_scalar(nrm[:, :], nrm[:, :], 1e-12, None, ALU.max)
                    v.drain()
                    V.reciprocal(nrm[:, :], nrm[:, :])
                    v.drain()
                    V.tensor_tensor(nrm[:, :], nrm[:, :], mf[:, bass.ds(b, 1), :].rearrange("p o t -> p (o t)"), ALU.mult)
                    v.drain()
                    for t in range(T):
                        V.tensor_scalar(z[:, t, :], z[:, t, :], nrm[:, t:t + 1], 0.0, ALU.mult, ALU.max)
                    v.drain().then_inc(s_r, 1)

                def graph_in_order(b, par, peeled):
                    graph(b, par, peeled)
                    v.wait_ge(full["rt"], nth(b + l * G, 1))

                each_graph(v, graph_in_order)
                v.wait_ge(read["rt"], (l + 1) * G)
                V.tensor_reduce(bn[:, 0:2], sums[:, :, :], AX.X, ALU.add)
                v.drain()
                V.tensor_scalar(bn[:, 0:2], bn[:, 0:2], 1.0 / (G * N), None, ALU.mult)
                v.drain()
                V.tensor_tensor(bn[:, 4:5], bn[:, 0:1], bn[:, 0:1], ALU.mult)
                v.drain()
                V.tensor_tensor(bn[:, 2:3], bn[:, 1:2], bn[:, 4:5], ALU.subtract)
                v.drain().then_inc(s_bnv, 1)
                v.wait_ge(s_bns, l + 1)
                V.reciprocal(bn[:, 5:6], bn[:, 3:4])
                v.drain()
                V.tensor_tensor(bn[:, 5:6], bn[:, 5:6], gb[:, l, 0:1], ALU.mult)
                v.drain()
                V.tensor_tensor(bn[:, 6:7], bn[:, 0:1], bn[:, 5:6], ALU.mult)
                v.drain()
                V.tensor_tensor(bn[:, 6:7], gb[:, l, 1:2], bn[:, 6:7], ALU.subtract)
                v.drain()
                V.tensor_copy(betas[:, l, :], bn[:, 6:7].broadcast_to([P, P]))
                V.tensor_scalar(wl_s[:, l, :], wl[:, l, :], bn[:, 5:6], None, ALU.mult)
                if l < L - 1:
                    V.tensor_scalar(wrx_s[:, :], wrx[:, l + 1, :], bn[:, 5:6], None, ALU.mult)
                v.drain().then_inc(s_beta, 1)
                v.wait_ge(s_crow, l + 2)
                V.tensor_copy(crow[:, 0:2 * D if l < L - 1 else D], ps[:, 0, 0:2 * D if l < L - 1 else D])
                if l == L - 1:
                    V.tensor_copy(blrow[:, :], ps[:, 1, 0:D])
                v.drain().then_inc(s_crowc, 1)

            def final(b, par, peeled):
                xf = xo[par]
                m = mf[:, bass.ds(b, 1), :].rearrange("p o t -> p (o t)").unsqueeze(2).broadcast_to([P, T, D])
                if not peeled:
                    v.wait_ge(s_st[par], even(b - 2, par))
                v.wait_ge(s_pp, nth(b, 1))
                v.wait_ge(s_pin[par], even(b, par) * (L + 1))
                V.tensor_tensor(xf[:, :, :], ps[:, par, :].rearrange("p (t d) -> p t d", t=T),
                                crow[:, 0:D].unsqueeze(1).broadcast_to([P, T, D]), ALU.add)
                v.drain().then_inc(s_pr, 1)
                V.tensor_tensor(xf[:, :, :], xf[:, :, :], m, ALU.mult)
                v.drain()
                V.tensor_tensor(xf[:, :, :], xf[:, :, :], blrow[:, :].unsqueeze(1).broadcast_to([P, T, D]), ALU.add)
                v.drain()
                V.tensor_tensor(xf[:, :, :], xf[:, :, :], m, ALU.mult)
                v.drain()
                V.tensor_tensor(xf[:, :, :], xf[:, :, :], x3[par][:, :, :], ALU.add)
                v.drain()
                for t in range(T):
                    V.bn_stats(stats[:, t, :], xf[:, t, :])
                v.drain()
                for t in range(T):
                    V.bn_aggr(mv[:, t, :], stats[:, t, :])
                v.drain().then_inc(s_var, 1)
                v.wait_ge(s_std, nth(b, 1))
                V.reciprocal(rden[:, :], std[:, :])
                v.drain()
                for t in range(T):
                    V.tensor_scalar(xf[:, t, :], xf[:, t, :], mv[:, t, 0:1], rden[:, t:t + 1], ALU.subtract, ALU.mult)
                v.drain().then_inc(s_out, 1)

            each_graph(v, final)


def build(nc, S):
    f32, bf16, u8 = mybir.dt.float32, mybir.dt.bfloat16, mybir.dt.uint8
    S.dilated = nc.dram_tensor("dilated", [G, N, N], u8, kind="Internal").ap()
    S.adt_dram = nc.dram_tensor("adt_dram", [G, P, T, N], bf16, kind="Internal").ap()
    S.x3_dram = nc.dram_tensor("x3_dram", [G, N, D], f32, kind="Internal").ap()
    S.h_dram = nc.dram_tensor("h_dram", [4, G, D, N], f32, kind="Internal").ap()
    with ExitStack() as ctx:
        S.ident = ctx.enter_context(nc.sbuf_tensor("ident", [P, P], f32))
        S.ident16 = ctx.enter_context(nc.sbuf_tensor("ident16", [P, P], bf16))
        S.row0 = ctx.enter_context(nc.sbuf_tensor("row0", [P, P], f32))
        S.eps_t = ctx.enter_context(nc.sbuf_tensor("eps_t", [P, 1], f32))
        S.zeroed = ctx.enter_context(nc.semaphore("bias_rows_zeroed"))
        layers_0_to_2(nc, S)
        layer_3(nc, S)


_NAMES = ["x", "adj", "nodemask", "L0_gnn_U", "L1_gnn_Wv", "L1_gnn_bv", "L1_gnn_Wk", "L1_gnn_bk",
          "L1_gnn_Wq", "L1_gnn_bq", "L2_gnn_W", "L2_gnn_a"]
_NAMES += [f"L3_gnn_{w}{l}" for l in (1, 2, 3) for w in ("Wr", "Wx", "b", "g", "be")]
_NAMES += ["L3_gnn_Wl", "L3_gnn_bl"]


def kernel(**inputs):
    from types import SimpleNamespace

    import numpy as np
    import concourse.bacc as bacc
    from concourse.bass_utils import run_bass_kernel_spmd

    nc = bacc.Bacc("TRN2", target_bir_lowering=False, num_devices=1)
    arrays, ap = {}, {}

    def give(name, a):
        arrays[name] = a
        ap[name] = nc.dram_tensor(name, a.shape, mybir.dt.from_np(a.dtype), kind="ExternalInput").ap()

    for name in _NAMES:
        a = np.ascontiguousarray(inputs[name])
        if name == "nodemask":
            give("mask_rows", np.ascontiguousarray(a.reshape(G, CH, W32).transpose(0, 2, 1)))
            give("mask_tiles", np.ascontiguousarray(a.reshape(G, T, P).transpose(2, 0, 1)))
        else:
            give(name, a)
    out = nc.dram_tensor("out", (G, N, D), mybir.dt.float32, kind="ExternalOutput").ap()
    S = SimpleNamespace(out=out)
    S.inputs_0_to_2 = [ap[n] for n in ["x", "adj", "mask_rows"] + _NAMES[3:12]]
    S.inputs_3 = (ap["mask_tiles"], [[ap[f"L3_gnn_{w}{l}"] for w in ("Wr", "Wx", "b", "g", "be")] for l in (1, 2, 3)],
                  ap["L3_gnn_Wl"], ap["L3_gnn_bl"])
    build(nc, S)
    r = run_bass_kernel_spmd(nc, [arrays], core_ids=[0])
    return r.results[0]["out"]
```

```python
from contextlib import ExitStack

import concourse.bass as bass
from concourse import mybir

G, N, D = 16, 1024, 128
P = 128
T = N // P
HALF = N // 2
HEADS = 4
DH = D // HEADS
EPS = 1e-5
BIG = 9.0e15
CLAMP = 9.0e13
SLOPE = 0.2
W32 = 32
CH = N // W32
QB = 2
GROUP = 4 * QB
MAGIC = 8388608.0

USES_START = ["xt", "y", "agg", "agg"]


def uses_of(first=False, last=False):
    u = ["x1t", "q", "k", "v", "s", "s"] + ([] if first else ["x3t"])
    for i in range(T):
        u += ["t"] + (["s"] if i + 2 < T else []) + ["o"]
    u += ([] if last else ["xt", "y"]) + ["x2t", "wh", "wh", "sj"] + ([] if last else ["agg", "agg"])
    return u + ["qa", "sj", "qa", "sj", "qa", "sj", "qa"]


USES = uses_of()
RING = 3
HEAD_SLOT = 3
PLAN = (2, 1, 1, 1, 1, 1, 1, 2, 1, 1, 0, 2, 2, 2, 2)
PLAN_LATE = (0, 0, 0, 0, 0, 0, 0, 0, 0, 2, 2, 4, 4, 4, 4)
PLAN_LAST = PLAN[:9] + (3, 2, 2, 2)
TILES2 = HEADS * T
TP = 4
USES_SAGE = ["adt"] * T + ["yz", "yz", "agg", "agg", "rt"]
USES_SAGE_LATER = ["yz", "yz", "agg", "agg", "rt"]
SLOTS = 4


def counts(uses):
    return {kind: uses.count(kind) for kind in uses}


def earlier_use(uses, n, slots=SLOTS):
    if n >= slots:
        return n - slots, False
    return max(m for m in range(len(uses)) if m % slots == n % slots), True


def number(uses, n):
    return uses[:n].count(uses[n])


def layers_0_to_2(nc, S):
    f32, bf16, f16 = mybir.dt.float32, mybir.dt.bfloat16, mybir.dt.float16
    u8, i32 = mybir.dt.uint8, mybir.dt.int32
    ALU, ACT, AX = mybir.AluOpType, mybir.ActivationFunctionType, mybir.AxisListType
    V, A, PE, GP = nc.vector, nc.scalar, nc.tensor, nc.gpsimd
    x, adj, mask_rows, U0, Wv, bv, Wk, bk, Wq, bq, W2, a2 = S.inputs_0_to_2
    dilated, x3_dram, h_dram = S.dilated, S.x3_dram, S.h_dram
    ident, ident16, row0, eps_t = S.ident, S.ident16, S.row0, S.eps_t

    ctx = ExitStack()
    with ctx:
        def sb(name, shape, dt):
            return ctx.enter_context(nc.sbuf_tensor(name, shape, dt))

        def sem(name):
            return ctx.enter_context(nc.semaphore(name))

        bigI = sb("bigI", [P, P], bf16)
        ones0 = sb("ones0", [P, P], bf16)
        negbig = sb("negbig", [P, HALF], bf16)
        u0 = sb("u0", [P, D], f32)
        wt = sb("wt", [P, 4, D], f32)
        wext = sb("wext", [P, D + 2 * HEADS], f32)
        ablk = sb("ablk", [P, 2 * HEADS], f32)
        wab = sb("wab", [P, HEADS, P], f32)
        bqk = sb("bqk", [P, 2], f32)
        bvrow = sb("bvrow", [P, D], f32)

        adjb = [sb(f"adj{i}", [P, T, N], bf16) for i in range(2)]
        xns = [sb(f"xn{i}", [P, T, D], f32) for i in range(2)]
        xTs = [sb(f"xT{i}", [P, N], f32) for i in range(2)]
        pN = sb("pN", [P, 2, N], f32)
        wload = pN[:, 0, 0:4 * D].rearrange("p (i d) -> p i d", i=4)
        pT_qa = sb("pT_qa", [P, HEADS * T * 66], f32)
        pT = pT_qa[:, 0:2 * N].rearrange("p (i j c) -> p i j c", i=2, j=T)
        qa = pT_qa[:, :].rearrange("p (h t c) -> p h t c", h=HEADS, t=T)
        qT = sb("qT", [P, N], f32)
        kT = sb("kT", [P, N], f32)
        y3 = pN[:, :, :].rearrange("p i c -> p (i c)").bitcast(bf16)[:, 0:3 * T * (D + 1)]\
            .rearrange("p (s t c) -> p s t c", s=3, t=T)
        y_rest = kT[:, :].rearrange("p (t c) -> p t c", t=T)
        agg = qT[:, :].rearrange("p (t c) -> p t c", t=T)
        vo = sb("vo", [P, T, D + 1], f32)
        vs = sb("vs", [P, T, 3, HEADS, 66], bf16)
        va = sb("va", [P, T, HEADS, 66], f32)
        wh = sb("wh", [P, T, D + 2 * HEADS], f32)
        sgn = sb("sgn", [P, T, N], bf16)
        rden = sb("rden", [P, T], f32)
        odn = sb("odn", [P, T], f32)
        cden = sb("cden", [P, T], f32)
        stats = sb("stats", [P, T, 6], f32)
        mv = sb("mv", [P, T, 2], f32)
        std = sb("std", [P, T], f32)
        shift = sb("shift", [P, T], f32)
        mx = sb("mx", [P, 2, T], f32)
        smax = sb("smax", [P, HEADS], f32)
        gmax = sb("gmax", [P, HEADS], f32)
        sc = sb("sc", [P, 3, T, HEADS], f32)
        ex = sb("ex", [P, 4, T, HEADS], f32)
        comb = sb("comb", [P, 2, T, 33], f32)

        M32 = sb("M32", [P, CH, QB, N // 4], i32)
        M = M32[:, :, :, :].rearrange("p s g c -> p (s g c)").bitcast(u8).rearrange("p (s g c) -> p s g c", s=CH, g=QB)
        mrow_i = sb("mrow_i", [P, QB, CH], i32)
        bias = sb("bias", [P, QB, CH], f32)
        upper = sb("upper", [P, QB, W32], f32)
        lower = sb("lower", [P, QB, W32], f16)
        cw = sb("cw", [P, QB, W32], f32)
        cu = sb("cu", [P, QB, W32], f32)
        dwin = sb("dwin", [P, QB, W32 + 1], f32)
        dnew = sb("dnew", [P, QB, W32], f32)
        keepz = sb("keepz", [P, QB, W32 + 1], f32)
        rk = sb("rk", [P, QB, W32 + 1], f32)
        rem = sb("rem", [P, QB, W32], f32)
        remT = sb("remT", [P, QB, W32], f32)
        e1 = sb("e1", [P, QB, W32], f32)
        small = sb("small", [P, 6, QB], f32)
        num, even_up, big, first, last, after = (small[:, i, :] for i in range(6))
        tiny = sb("tiny", [P, QB], f32)
        fl = sb("fl", [P, W32], f32)
        flT = sb("flT", [P, W32], f32)
        fl0 = sb("fl0", [1, P], f32)
        flag = sb("flag", [1, 1], i32)
        rank32 = sb("rank32", [P, 2, QB, N // 4], i32)
        rank = rank32[:, :, :, :].rearrange("p i g c -> p (i g c)").bitcast(f16).rearrange("p (g c) -> p g c", g=QB)
        rm = sb("rm", [P, QB, N], f16)
        rm32 = sb("rm32", [P, QB, N // 4], i32)
        rmT32, hit32 = rank32[:, 0], rank32[:, 1]
        rm8, rmT = (w.rearrange("p g c -> p (g c)").bitcast(u8).rearrange("p (g c) -> p g c", g=QB)
                    for w in (rm32[:, :, :], rmT32))

        ps = ctx.enter_context(nc.psum_tensor("ps", [P, SLOTS, N], f32))

        s_const = sem("const_ready")
        s_turn = sem("gpsimd_waited")
        s_w = sem("weights_loaded")
        s_wt = sem("weights_transposed")
        s_wtc = sem("weights_copied")
        s_wa = sem("wa_in_psum")
        s_wac = sem("wa_copied")
        full = {k: sem(f"{k}_in_psum") for k in counts(USES)}
        read = {k: sem(f"{k}_read") for k in counts(USES)}
        s_adj = [sem(f"adj{i}_loaded") for i in range(2)]
        s_x = [sem(f"x{i}_loaded") for i in range(2)]
        s_parts = sem("y_parts_ready")
        s_aggd = sem("degrees_inverted")
        s_var = sem("variance_ready")
        s_std = sem("std_ready")
        s_shift = sem("shift_ready")
        s_xn = sem("xn_ready")
        s_xnst = sem("x3_stored")
        s_nmx = sem("row_max_ready")
        s_clamped = sem("p_clamped")
        s_smax = sem("src_max_of_partitions")
        s_gmax = sem("src_max_everywhere")
        s_sc = sem("exponents_ready")
        s_ex = sem("exponentials_ready")
        s_va = sem("values_weighted")
        s_vb = sem("value_rest_ready")
        s_vh = sem("value_part_rounded")
        s_sgn = sem("sign_ready")
        s_ind = sem("masked_by_gpsimd")
        s_indv = sem("masked_by_vector")
        s_used = sem("sign_used")
        s_phr = sem("head_read")
        s_hT = sem("x3t_stored")
        s_M = sem("dilation_loaded")
        s_dil = sem("dilation_done")
        s_Mst = sem("dilation_stored")

        cn = counts(USES)

        def done(b, kind, i=0):
            return (b + (1 if kind in USES_START else -1 if kind == "x3t" else 0)) * cn[kind] + (i + 1)

        def norm(b, layer, last):
            return 3 * b + {1: 2, 0: 3, 2: 3 if last else 4}[layer]

        def half_of(b, par):
            return b * 8 + (16 - 8 * par)

        def nth(b, kind_count, i=0):
            return b * kind_count + (i + 1)

        block = ctx.enter_context(nc.Block())

        @block.sync
        def _(sp):
            for i, w in enumerate((Wv, Wk, Wq, W2)):
                sp.dma_start(wload[:, i, :], w).then_inc(s_w, 16)
            sp.dma_start(u0[:, :], U0).then_inc(s_w, 16)
            sp.dma_start(bqk[:, 0:1], bq.rearrange("(d o) -> d o", o=1)).then_inc(s_w, 16)
            sp.dma_start(bqk[:, 1:2], bk.rearrange("(d o) -> d o", o=1)).then_inc(s_w, 16)
            sp.wait_ge(s_const, 1)
            sp.dma_start(bvrow[0:1, :], bv.rearrange("(o d) -> o d", o=1)).then_inc(s_w, 16)
            for h in range(HEADS):
                for e in range(2):
                    sp.dma_start(ablk[DH * h:DH * h + DH, HEADS * e + h:HEADS * e + h + 1],
                                 a2[h, DH * e:DH * e + DH].rearrange("(d o) -> d o", o=1)).then_inc(s_w, 16)

            def load(b, par):
                sp.dma_start(xns[par][:, :, :], x[b].rearrange("(t p) d -> p t d", p=P)).then_inc(s_x[par], 16)

            def graph(b, par, last=False, more=True):
                sp.wait_ge(s_xn, norm(b, 2, last))
                sp.dma_start(x3_dram[b].rearrange("(t p) d -> p t d", p=P), xns[par][:, :, :]).then_inc(s_xnst, 16)
                sp.wait_ge(read["x3t"], nth(b, 1))
                sp.dma_start(h_dram[0, b], xTs[par][:, :]).then_inc(s_hT, 16)
                if more:
                    sp.wait_ge(s_xnst, nth(b, 16, 15))
                    load(b + 2, par)

            load(0, 0)
            load(1, 1)
            with sp.Fori(0, G // 2 - 1) as pair:
                for par in range(2):
                    graph(pair * 2 + par, par)
            graph(G - 2, 0, more=False)
            graph(G - 1, 1, last=True, more=False)
            sp.wait_ge(s_xnst, 16 * G)
            sp.wait_ge(s_hT, 16 * G)

        @block.gpsimd
        def _(gp):
            GP.memset(bvrow[:, :], 0.0)
            GP.memset(ablk[:, :], 0.0)
            GP.memset(ident[:, :], 0.0)
            GP.memset(row0[:, :], 0.0)
            GP.memset(ones0[:, :], 0.0)
            GP.memset(negbig[:, :], 0.0)
            GP.memset(upper[:, :, :], 0.0)
            GP.memset(lower[:, :, :], 0.0)
            GP.memset(eps_t[:, :], EPS)
            gp.drain()
            GP.memset(row0[0:1, :], 1.0)
            GP.memset(ones0[0:1, :], 1.0)
            GP.memset(negbig[0:1, :], -BIG)
            GP.affine_select(out=ident[:, :], in_=ident[:, :], compare_op=ALU.not_equal, fill=1.0,
                             base=0, pattern=[[-1, P]], channel_multiplier=1)
            gp.drain()
            for q in range(4):
                u = upper[32 * q:32 * q + 32, :, :]
                GP.affine_select(out=u, in_=u, compare_op=ALU.is_ge, fill=1.0, base=0,
                                 pattern=[[0, QB], [-1, W32]], channel_multiplier=1)
                gp.drain()
                u = lower[32 * q:32 * q + 32, :, :]
                GP.affine_select(out=u, in_=u, compare_op=ALU.is_ge, fill=1.0, base=0,
                                 pattern=[[0, QB], [1, W32]], channel_multiplier=-1)
                gp.drain()
            GP.tensor_copy(ident16[:, :], ident[:, :])
            GP.tensor_scalar(bigI[:, :], ident[:, :], BIG, None, ALU.mult)
            gp.drain().then_inc(s_const, 1)

            def wait(semaphore, value):
                gp.wait_ge(semaphore, value)
                gp.sem_inc(s_turn, 1)

            def load_adj(b, par, first_one=False):
                if not first_one:
                    gp.wait_ge(s_used, (b - 1) * TILES2)
                gp.dma_start(adjb[par][:, :, :], adj[b].rearrange("(t p) c -> p t c", p=P)).then_inc(s_adj[par], 16)

            def load_dilation(half):
                for q in range(4):
                    for g in range(QB):
                        b = GROUP * half + QB * q + g
                        gp.dma_start(M[32 * q:32 * q + 32, :, g, :],
                                     adj[b].rearrange("(s r) c -> r s c", r=W32)).then_inc(s_M, 16)
                        gp.dma_start(mrow_i[32 * q:32 * q + 32, g, :], mask_rows[b]).then_inc(s_M, 16)

            def store_dilation(half):
                gp.wait_ge(s_dil, half + 1)
                for q in range(4):
                    for g in range(QB):
                        b = GROUP * half + QB * q + g
                        gp.dma_start(dilated[b].rearrange("(s r) c -> r s c", r=W32),
                                     M[32 * q:32 * q + 32, :, g, :]).then_inc(s_Mst, 16)
                gp.wait_ge(s_Mst, 16 * GROUP * (half + 1))

            def graph(b, par, more):
                for i in range(T):
                    wait(read["s"], done(b, "s", i))
                    GP.tensor_scalar(pN[:, i % 2, :], pN[:, i % 2, :], 1.0, None, ALU.min)
                    gp.drain().then_inc(s_clamped, 1)
                wait(s_smax, nth(b, 1))
                GP.partition_all_reduce(gmax[:, :], smax[:, :], P, bass.bass_isa.ReduceOp.max).then_inc(s_gmax, 1)
                for h in range(HEADS):
                    for i in range(TP):
                        wait(s_sgn, nth(b, TILES2, T * h + i))
                        GP.tensor_tensor(sgn[:, i, :], sgn[:, i, :], adjb[par][:, i, :], ALU.mult)
                        gp.drain().then_inc(s_ind, 1)
                if more:
                    load_adj(b + 2, par)

            load_adj(0, 0, True)
            load_adj(1, 1, True)
            for half in range(2):
                load_dilation(half)
                with gp.Fori(0, G // 4 - half) as pair:
                    for par in range(2):
                        graph(pair * 2 + (GROUP * half + par), par, True)
                if half:
                    for par in range(2):
                        graph(G - 2 + par, par, False)
                store_dilation(half)

        @block.tensor
        def _(pe):
            pe.wait_ge(s_const, 1)
            pe.wait_ge(s_w, 16 * 16)
            for i in range(4):
                PE.transpose(ps[:, 0, P * i:P * i + P], wload[:, i, :], ident[:, :])
            pe.drain().then_inc(s_wt, 1)
            pe.wait_ge(s_wtc, 1)
            PE.matmul(ps[:, 1, 0:2 * HEADS], wt[:, 3, :], ablk[:, :], start=True, stop=True).then_inc(s_wa, 1)
            pe.wait_ge(s_wac, 1)

            def ring(b, uses, before):
                at = [0]

                def slot():
                    n = at[0]
                    at[0] += 1
                    if n >= RING:
                        pe.wait_ge(read[uses[n - RING]], done(b, uses[n - RING], number(uses, n - RING)))
                    elif before == USES_START:
                        pe.wait_ge(read["agg"], 2)
                    elif before:
                        m = max(m for m in range(len(before)) if m % RING == n)
                        pe.wait_ge(read[before[m]], done(b - 1, before[m], number(before, m)))
                    return ps[:, n % RING, :]

                return slot

            def transposes(slot, kind, src):
                o = slot()
                for t in range(T):
                    ins = PE.transpose(o[:, P * t:P * t + P], src[:, t, :], ident[:, :])
                ins.then_inc(full[kind], 1)

            def x_times_u(b, par, slot):
                pe.wait_ge(s_x[par], half_of(b, par))
                transposes(slot, "xt", xns[par])
                o = slot()
                pe.wait_ge(read["xt"], nth(b, 1))
                for t in range(T):
                    ins = PE.matmul(o[:, P * t:P * t + P], xTs[par][:, P * t:P * t + P], u0[:, :], start=True, stop=True)
                ins.then_inc(full["y"], 1)

            def aggregate(b, par, slot):
                pe.wait_ge(s_adj[par], half_of(b, par))
                pe.wait_ge(s_parts, nth(b, 1))
                for i in range(T):
                    if i % 4 == 0:
                        o = slot()
                    r = 256 * (i % 4)
                    for j in range(T):
                        w = adjb[par][:, j, P * i:P * i + P]
                        PE.matmul(o[:, r:r + 129], w, y3[:, 0, j, :], start=(j == 0), stop=False)
                        PE.matmul(o[:, r:r + 128], w, y3[:, 1, j, 0:D], start=False, stop=False)
                        ins = PE.matmul(o[:, r:r + 128], w, y3[:, 2, j, 0:D], start=False, stop=(j == T - 1))
                    if i % 4 == 3:
                        ins.then_inc(full["agg"], 1)

            def graph(b, par, before=USES, last=False):
                first = before == USES_START
                uses = uses_of(first, last)
                slot = ring(b, uses, before)
                xn, xT = xns[par], xTs[par]

                pe.wait_ge(s_xn, 1 if first else b * 3)
                transposes(slot, "x1t", xn)
                for kind, w in (("q", 2), ("k", 1)):
                    o = slot()
                    pe.wait_ge(read["x1t"], nth(b, 1))
                    for c in range(2):
                        ins = PE.matmul(o[:, HALF * c:HALF * c + HALF], wt[:, w, :], xT[:, HALF * c:HALF * c + HALF],
                                        start=True, stop=True)
                    ins.then_inc(full[kind], 1)
                o = slot()
                for t in range(T):
                    PE.matmul(o[:, P * t:P * t + P], xT[:, P * t:P * t + P], wt[:, 0, :], start=True, stop=False)
                    ins = PE.matmul(o[:, P * t:P * t + P], row0[:, :], bvrow[:, :], start=False, stop=True)
                ins.then_inc(full["v"], 1)
                pe.wait_ge(read["q"], nth(b, 1))
                pe.wait_ge(read["k"], nth(b, 1))

                def scores(i):
                    o = slot()
                    for c in range(2):
                        cols = slice(HALF * c, HALF * c + HALF)
                        PE.matmul(o[:, cols], ones0[:, :], negbig[:, :], start=True, stop=False)
                        PE.matmul(o[:, cols], bigI[:, :], adjb[par][:, i, cols], start=False, stop=False)
                        ins = PE.matmul(o[:, cols], qT[:, P * i:P * i + P], kT[:, cols], start=False, stop=True)
                    ins.then_inc(full["s"], 1)

                scores(0)
                scores(1)
                if not first:
                    pe.wait_ge(s_xn, norm(b - 1, 2, False))
                    transposes(slot, "x3t", xns[1 - par])
                for i in range(T):
                    o = slot()
                    pe.wait_ge(s_clamped, nth(b, T, i))
                    for j in range(T):
                        ins = PE.transpose(o[:, P * j:P * j + P], pN[:, i % 2, P * j:P * j + P], ident[:, :])
                    ins.then_inc(full["t"], 1)
                    if i + 2 < T:
                        scores(i + 2)
                    o = slot()
                    pe.wait_ge(read["t"], nth(b, T, i))
                    if i == 0:
                        pe.wait_ge(read["v"], nth(b, 1))
                    for j in range(T):
                        ins = PE.matmul(o[:, 0:D + 1], pT[:, i % 2, j, :], vo[:, j, :], start=(j == 0), stop=(j == T - 1))
                    ins.then_inc(full["o"], 1)

                if not last:
                    x_times_u(b + 1, 1 - par, slot)
                pe.wait_ge(s_xn, norm(b, 1, last))
                transposes(slot, "x2t", xn)
                for t in range(T):
                    if t % 4 == 0:
                        o = slot()
                    if t == 0:
                        pe.wait_ge(read["x2t"], nth(b, 1))
                    r = 256 * (t % 4)
                    ins = PE.matmul(o[:, r:r + D + 2 * HEADS], xT[:, P * t:P * t + P], wext[:, :], start=True, stop=True)
                    if t % 4 == 3:
                        ins.then_inc(full["wh"], 1)

                def dst_scores(h):
                    o = slot()
                    for c in range(2):
                        ins = PE.matmul(o[:, HALF * c:HALF * c + HALF], wab[:, h, :], xT[:, HALF * c:HALF * c + HALF],
                                        start=True, stop=True)
                    ins.then_inc(full["sj"], 1)

                def head(h):
                    o = ps[:, HEAD_SLOT, :]
                    if h > 0:
                        pe.wait_ge(s_phr, nth(b, HEADS, h - 1))
                    elif not first:
                        pe.wait_ge(s_phr, b * HEADS)
                    for i in range(T):
                        if i < TP:
                            pe.wait_ge(s_ind, nth(b, HEADS * TP, TP * h + i))
                        else:
                            pe.wait_ge(s_indv, nth(b, HEADS * (T - TP), (T - TP) * h + i - TP))
                        for j in range(T):
                            for s in range(3):
                                ins = PE.matmul(o[:, P * j:P * j + 66], sgn[:, i, P * j:P * j + P], vs[:, i, s, h, :],
                                                start=(i == 0 and s == 0 and j % 4 == 0),
                                                stop=(i == T - 1 and s == 2 and j % 4 == 3))
                        ins.then_inc(s_used, 1)

                def neighbours(h):
                    o = slot()
                    if h == 0:
                        pe.wait_ge(s_vh, nth(b, 3, 2))
                    for j in range(T):
                        for i in range(T):
                            for s in range(3):
                                ins = PE.matmul(o[:, P * j:P * j + 66], adjb[par][:, i, P * j:P * j + P], vs[:, i, s, h, :],
                                                start=(i == 0 and s == 0), stop=(i == T - 1 and s == 2))
                    ins.then_inc(full["qa"], 1)

                dst_scores(0)
                if not last:
                    aggregate(b + 1, 1 - par, slot)
                for h in range(HEADS):
                    neighbours(h)
                    if h + 1 < HEADS:
                        dst_scores(h + 1)
                    head(h)

            start = ring(-1, USES_START, None)
            x_times_u(0, 0, start)
            aggregate(0, 0, start)
            graph(0, 0, before=USES_START)
            graph(1, 1, before=uses_of(first=True))
            with pe.Fori(1, G // 2 - 1) as pair:
                for par in range(2):
                    graph(pair * 2 + par, par)
            graph(G - 2, 0)
            graph(G - 1, 1, last=True)
            pe.wait_ge(s_xn, norm(G - 1, 2, True))
            transposes(lambda: ps[:, HEAD_SLOT, :], "x3t", xns[1])

        @block.scalar
        def _(act):
            act.wait_ge(s_wt, 1)
            A.copy(wt[:, :, :], ps[:, 0, 0:4 * P].rearrange("p (i d) -> p i d", i=4))
            A.copy(wext[:, 0:D], wload[:, 3, :])
            act.drain().then_inc(s_wtc, 1)
            act.wait_ge(s_wa, 1)
            A.copy(wext[:, D:D + 2 * HEADS], ps[:, 1, 0:2 * HEADS])
            act.drain()
            for h in range(HEADS):
                A.copy(wab[:, h, :], wext[:, D + HEADS + h:D + HEADS + h + 1].broadcast_to([P, P]))
            act.drain().then_inc(s_wac, 1)

            def ring(b, uses):
                at = [0]

                def slot(kind):
                    n = uses.index(kind, at[0])
                    at[0] = n + 1
                    act.wait_ge(full[kind], done(b, kind, number(uses, n)))
                    return ps[:, n % RING, :]

                return slot

            def deviation(count):
                act.wait_ge(s_var, count)
                A.activation(std[:, :], mv[:, :, 1], ACT.Sqrt, bias=eps_t[:, 0:1]).then_inc(s_std, 1)

            def normalise(count, xn):
                act.wait_ge(s_shift, count)
                for t in range(T):
                    A.activation(xn[:, t, :], xn[:, t, :], ACT.Identity, bias=shift[:, t:t + 1], scale=rden[:, t:t + 1])
                act.drain().then_inc(s_xn, 1)

            def copy_xt(b, par, slot):
                if not isinstance(b, int) or b > 1:
                    act.wait_ge(s_hT, (b - 1) * 16)
                A.copy(xTs[par][:, :], slot("xt")).then_inc(read["xt"], 1)

            def relu_agg(b, slot):
                for c in range(2):
                    a = slot("agg").rearrange("p (t d) -> p t d", t=4)
                    act.wait_ge(s_aggd, nth(b, 2, c))
                    for t in range(4):
                        A.activation(agg[:, 4 * c + t, :], a[:, t, 0:D], ACT.Relu, scale=odn[:, 4 * c + t:4 * c + t + 1])
                    act.drain().then_inc(read["agg"], 1)

            def graph(b, par, first_one=False, last=False):
                uses = uses_of(first_one, last)
                slot = ring(b, uses)
                xn, xT = xns[par], xTs[par]
                A.copy(xT[:, :], slot("x1t")).then_inc(read["x1t"], 1)
                if not first_one:
                    deviation(norm(b - 1, 2, False))
                A.activation(qT[:, :], slot("q"), ACT.Relu, bias=bqk[:, 0:1]).then_inc(read["q"], 1)
                A.activation(kT[:, :], slot("k"), ACT.Relu, bias=bqk[:, 1:2]).then_inc(read["k"], 1)
                A.activation(vo[:, :, 0:D], slot("v").rearrange("p (t d) -> p t d", t=T), ACT.Relu).then_inc(read["v"], 1)

                uses_of_s = [n for n, kind in enumerate(uses) if kind == "s"]

                def exponentials(i):
                    if i >= 2:
                        act.wait_ge(full["t"], nth(b, T, i - 2))
                    act.wait_ge(s_nmx, nth(b, T, i))
                    A.activation(pN[:, i % 2, :], ps[:, uses_of_s[i] % RING, :], ACT.Exp, bias=mx[:, 1, i:i + 1])\
                        .then_inc(read["s"], 1)

                if not first_one:
                    normalise(norm(b - 1, 2, False), xns[1 - par])
                exponentials(0)
                for i in range(T):
                    if i == 0 and not first_one:
                        act.wait_ge(full["x3t"], done(b, "x3t"))
                        A.copy(xTs[1 - par][:, :], ps[:, uses.index("x3t") % RING, :]).then_inc(read["x3t"], 1)
                    if i + 1 < T:
                        exponentials(i + 1)
                    if i >= 2:
                        act.wait_ge(full["o"], nth(b, T, i - 2))
                    A.copy(pT[:, i % 2, :, :], slot("t").rearrange("p (j i) -> p j i", j=T)).then_inc(read["t"], 1)
                if not last:
                    copy_xt(b + 1, 1 - par, slot)
                deviation(norm(b, 1, last))
                normalise(norm(b, 1, last), xn)
                A.copy(xT[:, :], slot("x2t")).then_inc(read["x2t"], 1)
                for c in range(2):
                    A.copy(wh[:, 4 * c:4 * c + 4, :],
                           slot("wh").rearrange("p (t d) -> p t d", t=4)[:, :, 0:D + 2 * HEADS]).then_inc(read["wh"], 1)
                act.drain()

                def signs(h, o, tiles):
                    for i in tiles:
                        if h > 0:
                            act.wait_ge(s_used, nth(b, TILES2, T * (h - 1) + i))
                        elif not first_one:
                            act.wait_ge(s_used, b * TILES2)
                        A.activation(sgn[:, i, :], o, ACT.Sign, bias=wh[:, i, D + h:D + h + 1]).then_inc(s_sgn, 1)
                    if T - 1 in tiles:
                        act.drain().then_inc(read["sj"], 1)

                o = slot("sj")
                signs(0, o, range(T // 2))
                act.wait_ge(s_sc, nth(b, 1))
                A.activation(ex[:, 0], sc[:, 0], ACT.Exp)
                A.activation(ex[:, 1], sc[:, 0], ACT.Exp, scale=SLOPE)
                A.activation(ex[:, 2], sc[:, 1], ACT.Exp, scale=1.0 - SLOPE)
                A.activation(ex[:, 3], sc[:, 2], ACT.Exp, scale=SLOPE - 1.0)
                act.drain().then_inc(s_ex, 1)
                signs(0, o, range(T // 2, T))
                for s in range(3):
                    if s == 0:
                        act.wait_ge(s_va, nth(b, 1))
                    else:
                        act.wait_ge(s_vb, nth(b, 2, s - 1))
                    A.copy(vs[:, :, s, :, :], va[:, :, :, :]).then_inc(s_vh, 1)
                if not last:
                    relu_agg(b + 1, slot)
                for h in range(HEADS):
                    A.copy(qa[:, h, :, :], slot("qa").rearrange("p (t d) -> p t d", t=T)[:, :, 0:66]).then_inc(read["qa"], 1)
                    if h + 1 < HEADS:
                        signs(h + 1, slot("sj"), range(T))
                    if h == 1 and not last:
                        deviation(norm(b, 0, last))
                    if h == 2 and not last:
                        normalise(norm(b, 0, last), xns[1 - par])

            start = ring(-1, USES_START)
            copy_xt(0, 0, start)
            relu_agg(0, start)
            deviation(1)
            normalise(1, xns[0])
            graph(0, 0, first_one=True)
            graph(1, 1)
            with act.Fori(1, G // 2 - 1) as pair:
                for par in range(2):
                    graph(pair * 2 + par, par)
            graph(G - 2, 0)
            graph(G - 1, 1, last=True)
            deviation(norm(G - 1, 2, True))
            normalise(norm(G - 1, 2, True), xns[1])
            act.wait_ge(full["x3t"], G)
            A.copy(xTs[1][:, :], ps[:, HEAD_SLOT, :]).then_inc(read["x3t"], 1)

        @block.vector
        def _(v):
            V.memset(keepz[:, :, :], 1.0)
            V.memset(fl[:, :], 0.0)
            v.drain()
            V.memset(keepz[:, :, 0:1], 0.0)
            v.wait_ge(s_const, 1)
            v.drain()

            def flat(t):
                return t[:, :, :].rearrange("p a b -> p (a b)")

            def spread(t):
                return t.unsqueeze(2).broadcast_to([P, QB, W32])

            def thresholds():
                V.tensor_scalar(even_up, num, 2 * MAGIC, 2 * MAGIC, ALU.add, ALU.subtract)
                V.tensor_scalar(big, num, 11.0, None, ALU.is_ge)
                V.tensor_scalar(tiny[:, :], num, 2.0, 3.0 * N, ALU.is_lt, ALU.mult)
                v.drain()
                V.scalar_tensor_tensor(first, even_up, 0.5, big, ALU.mult, ALU.mult)
                V.tensor_tensor(last, even_up, big, ALU.mult)
                v.drain()
                V.tensor_tensor(last, last, tiny[:, :], ALU.max)
                v.drain()

            def to_flag(changed):
                V.tensor_reduce(fl[:, 0:1], changed, AX.XY, ALU.max)
                v.drain()
                V.transpose(flT[:, :], fl[:, :])
                v.drain()
                for q in range(4):
                    V.tensor_copy(fl0[0:1, 32 * q:32 * q + 32], flT[32 * q:32 * q + 1, :])
                v.drain()
                V.tensor_reduce(flag[:, :], fl0[:, :], AX.X, ALU.max)
                v.drain()

            def flagged():
                return v.value_load(flag[0:1, 0:1], min_val=0, max_val=1) != 0

            def ranks(t):
                for g in range(QB):
                    V.tensor_tensor_scan(rank[:, g, :], M[:, t, g, :], M[:, t, g, :], 0.0, ALU.add, ALU.max)
                v.drain()
                V.tensor_tensor(num, rank[:, :, N - 1], bias[:, :, bass.ds(t, 1)].rearrange("p g o -> p (g o)"), ALU.add)
                v.drain()
                thresholds()

            def rank_flags():
                for g in range(QB):
                    V.tensor_scalar(rm[:, g, :], rank[:, g, :], small[:, 3, g:g + 1], None, ALU.is_equal)
                v.drain()
                for g in range(QB):
                    V.scalar_tensor_tensor(rm[:, g, :], rank[:, g, :], small[:, 4, g:g + 1], rm[:, g, :], ALU.is_ge, ALU.max)
                v.drain()

            def removed(t):
                V.tensor_tensor(rm8, rm[:, :, :], M[:, t, :, :], ALU.mult)
                v.drain()
                V.transpose(rmT.rearrange("p g c -> p (g c)"), rm8.rearrange("p g c -> p (g c)"))
                v.drain()

            def within_window(t):
                win = bass.ds(t * W32, W32)
                ranks(t)
                V.tensor_tensor(dwin[:, :, 0], rank[:, :, bass.ds(t * W32, 1)].rearrange("p g o -> p (g o)"),
                                M[:, t, :, bass.ds(t * W32, 1)].rearrange("p g o -> p (g o)"), ALU.subtract)
                V.tensor_tensor(after, num, rank[:, :, bass.ds(t * W32 + (W32 - 1), 1)].rearrange("p g o -> p (g o)"),
                                ALU.subtract)
                V.tensor_copy(cw[:, :, :], M[:, t, :, win])
                v.drain()
                V.tensor_tensor(cu[:, :, :], cw[:, :, :], upper[:, :, :], ALU.mult)
                V.tensor_copy(dwin[:, :, 1:W32 + 1], cw[:, :, :])
                v.drain()
                V.memset(flag[:, :], 1)
                v.drain()
                with v.While(flagged):
                    V.tensor_tensor_scan(flat(rk), flat(keepz), flat(dwin), 0.0, ALU.mult, ALU.add)
                    v.drain()
                    V.tensor_tensor(num, rk[:, :, W32], after, ALU.add)
                    v.drain()
                    thresholds()
                    V.tensor_tensor(e1[:, :, :], rk[:, :, 1:W32 + 1], spread(first), ALU.is_equal)
                    V.tensor_tensor(rem[:, :, :], rk[:, :, 1:W32 + 1], spread(last), ALU.is_ge)
                    v.drain()
                    V.tensor_tensor(rem[:, :, :], rem[:, :, :], e1[:, :, :], ALU.max)
                    v.drain()
                    V.tensor_tensor(rem[:, :, :], rem[:, :, :], cu[:, :, :], ALU.mult)
                    v.drain()
                    V.transpose(flat(remT), flat(rem))
                    v.drain()
                    V.tensor_tensor(dnew[:, :, :], cw[:, :, :], remT[:, :, :], ALU.is_gt)
                    v.drain()
                    V.tensor_tensor(e1[:, :, :], dnew[:, :, :], dwin[:, :, 1:W32 + 1], ALU.not_equal)
                    v.drain()
                    V.tensor_copy(dwin[:, :, 1:W32 + 1], dnew[:, :, :])
                    to_flag(e1[:, :, :])
                V.tensor_copy(M[:, t, :, win], dwin[:, :, 1:W32 + 1])
                v.drain()
                ranks(t)
                rank_flags()
                removed(t)

            def dilation_pieces(t):
                win = bass.ds(t * W32, W32)

                def scan():
                    ranks(t)

                def remove():
                    removed(t)

                def check():
                    V.tensor_tensor(e1[:, :, :], rmT[:, :, win], lower[:, :, :], ALU.mult)
                    v.drain()
                    V.tensor_tensor(e1[:, :, :], e1[:, :, :], M[:, t, :, win], ALU.mult)
                    v.drain()
                    to_flag(e1[:, :, :])
                    with v.If(flagged()):
                        within_window(t)
                    v.drain()

                def update():
                    V.tensor_tensor(M32[:, t, :, :], M32[:, t, :, :], rm32[:, :, :], ALU.bitwise_xor)
                    v.drain()
                    for op in (0, 1):
                        for g in range(QB):
                            cols = M32[:, :, g, bass.ds(t * (W32 // 4), W32 // 4)]
                            hit = hit32[:, g, :].rearrange("p (s c) -> p s c", s=CH)
                            lost = rmT32[:, g, :].rearrange("p (s c) -> p s c", s=CH)
                            if op == 0:
                                V.tensor_tensor(hit, cols, lost, ALU.bitwise_and)
                            else:
                                V.tensor_tensor(cols, cols, hit, ALU.bitwise_xor)
                        v.drain()

                return [scan, rank_flags, remove, check, update]

            def ring(b, uses):
                at = [0]

                def slot(kind):
                    n = uses.index(kind, at[0])
                    at[0] = n + 1
                    v.wait_ge(full[kind], done(b, kind, number(uses, n)))
                    return ps[:, n % RING, :]

                return slot

            def moments(xn):
                v.drain()
                for t in range(T):
                    V.bn_stats(stats[:, t, :], xn[:, t, :])
                v.drain()
                for t in range(T):
                    V.bn_aggr(mv[:, t, :], stats[:, t, :])
                v.drain().then_inc(s_var, 1)

            def scale_and_shift(count):
                v.wait_ge(s_std, count)
                V.reciprocal(rden[:, :], std[:, :])
                v.drain()
                V.scalar_tensor_tensor(shift[:, :], mv[:, :, 0], -1.0, rden[:, :], ALU.mult, ALU.mult)
                v.drain().then_inc(s_shift, 1)

            def y_parts(slot):
                y = slot("y").rearrange("p (t d) -> p t d", t=T)
                V.memset(y3[:, 0, :, D:D + 1], 1.0)
                V.tensor_copy(y3[:, 0, :, 0:D], y)
                v.drain()
                V.tensor_tensor(y_rest, y, y3[:, 0, :, 0:D], ALU.subtract).then_inc(read["y"], 1)
                v.drain()
                V.tensor_copy(y3[:, 1, :, 0:D], y_rest)
                v.drain()
                V.tensor_tensor(y_rest, y_rest, y3[:, 1, :, 0:D], ALU.subtract)
                v.drain()
                V.tensor_copy(y3[:, 2, :, 0:D], y_rest).then_inc(s_parts, 1)

            def degrees(slot, c):
                a = slot("agg").rearrange("p (t d) -> p t d", t=4)
                V.reciprocal(odn[:, 4 * c:4 * c + 4], a[:, :, D]).then_inc(s_aggd, 1)

            def add_aggregate(b, xn):
                v.wait_ge(read["agg"], nth(b, 2, 1))
                V.tensor_tensor(xn[:, :, :], xn[:, :, :], agg, ALU.add)

            def graph(b, par, t0, plan=PLAN, first=False, last=False):
                pieces = [p for s in range(4) for p in dilation_pieces(t0 + s)]
                uses = uses_of(first, last)
                slot = ring(b, uses)
                xn = xns[par]
                points = list(plan)

                def fill():
                    n = points.pop(0)
                    if n and plan == PLAN_LATE and len(pieces) == 20:
                        start_half(1)
                    for _ in range(n):
                        pieces.pop(0)()

                fill()
                if not first:
                    scale_and_shift(norm(b - 1, 2, False))
                fill()

                def row_max(i):
                    V.reduce_max(mx[:, 0, i:i + 1], slot("s"), AX.X)
                    v.drain()
                    V.tensor_scalar(mx[:, 1, i:i + 1], mx[:, 0, i:i + 1], CLAMP, -1.0, ALU.min, ALU.mult).then_inc(s_nmx, 1)

                uses_of_o = [n for n, kind in enumerate(uses) if kind == "o"]

                def add_attended(i):
                    v.wait_ge(full["o"], done(b, "o", i))
                    o = ps[:, uses_of_o[i] % RING, :]
                    V.reciprocal(cden[:, i:i + 1], o[:, D:D + 1])
                    v.drain()
                    V.scalar_tensor_tensor(xn[:, i, :], o[:, 0:D], cden[:, i:i + 1], xn[:, i, :], ALU.mult, ALU.add)\
                        .then_inc(read["o"], 1)

                row_max(0)
                fill()
                row_max(1)
                for i in range(T):
                    if i + 2 < T:
                        row_max(i + 2)
                    if i % 2:
                        fill()
                    add_attended(i)
                moments(xn)
                scale_and_shift(norm(b, 1, last))
                if not last:
                    y_parts(slot)
                fill()

                v.wait_ge(read["wh"], nth(b, cn["wh"], 1))
                V.tensor_reduce(smax[:, :], wh[:, :, D:D + HEADS].rearrange("p t h -> p h t"), AX.X, ALU.max)
                v.drain().then_inc(s_smax, 1)
                fill()
                v.wait_ge(s_gmax, nth(b, 1))
                top = gmax[:, :].unsqueeze(1).broadcast_to([P, T, HEADS])
                V.tensor_tensor(sc[:, 0], wh[:, :, D:D + HEADS], top, ALU.subtract)
                V.tensor_tensor(sc[:, 2], wh[:, :, D + HEADS:D + 2 * HEADS], top, ALU.add)
                v.drain()
                V.tensor_scalar(sc[:, 1], sc[:, 2], 0.0, None, ALU.min)
                v.drain()
                V.tensor_scalar(sc[:, 2], sc[:, 2], 0.0, None, ALU.max)
                v.drain().then_inc(s_sc, 1)
                v.wait_ge(s_ex, nth(b, 1))
                whh = wh[:, :, 0:D].rearrange("p t (h c) -> p t h c", h=HEADS)
                for e in range(2):
                    V.tensor_tensor(va[:, :, :, 33 * e:33 * e + DH], whh, ex[:, e].unsqueeze(3).broadcast_to([P, T, HEADS, DH]),
                                    ALU.mult)
                    V.tensor_copy(va[:, :, :, 33 * e + DH], ex[:, e])
                v.drain().then_inc(s_va, 1)
                for s in range(2):
                    v.wait_ge(s_vh, nth(b, 3, s))
                    V.tensor_tensor(va[:, :, :, :], va[:, :, :, :], vs[:, :, s, :, :], ALU.subtract)
                    v.drain().then_inc(s_vb, 1)

                def mask(h):
                    for i in range(TP, T):
                        v.wait_ge(s_sgn, nth(b, TILES2, T * h + i))
                        V.tensor_tensor(sgn[:, i, :], sgn[:, i, :], adjb[par][:, i, :], ALU.mult).then_inc(s_indv, 1)

                def combine(h):
                    v.wait_ge(s_used, nth(b, TILES2, T * h + T - 1))
                    o = ps[:, HEAD_SLOT, :].rearrange("p (t d) -> p t d", t=T)
                    v.wait_ge(read["qa"], done(b, "qa", h))
                    V.tensor_tensor(comb[:, 1], qa[:, h, :, 33:66], o[:, :, 33:66], ALU.subtract)
                    V.tensor_tensor(comb[:, 0], qa[:, h, :, 0:33], o[:, :, 0:33], ALU.add)
                    v.drain().then_inc(s_phr, 1)
                    V.tensor_tensor(comb[:, 0], comb[:, 0], ex[:, 2, :, h].unsqueeze(2).broadcast_to([P, T, 33]), ALU.mult)
                    V.tensor_tensor(comb[:, 1], comb[:, 1], ex[:, 3, :, h].unsqueeze(2).broadcast_to([P, T, 33]), ALU.mult)
                    v.drain()
                    V.tensor_tensor(comb[:, 0], comb[:, 0], comb[:, 1], ALU.add)
                    v.drain()
                    V.reciprocal(cden[:, :], comb[:, 0, :, DH])
                    v.drain()
                    V.tensor_tensor(comb[:, 0, :, 0:DH], comb[:, 0, :, 0:DH],
                                    cden[:, :].unsqueeze(2).broadcast_to([P, T, DH]), ALU.mult)
                    v.drain()
                    V.tensor_tensor(xn[:, :, DH * h:DH * h + DH], xn[:, :, DH * h:DH * h + DH], comb[:, 0, :, 0:DH], ALU.add)

                if not last:
                    for c in range(2):
                        degrees(slot, c)
                        fill()
                for h in range(HEADS):
                    mask(h)
                    if h == 1 and not last:
                        add_aggregate(b + 1, xns[1 - par])
                        moments(xns[1 - par])
                    fill()
                    combine(h)
                    if h == 1 and not last:
                        scale_and_shift(norm(b, 0, last))
                v.drain()
                moments(xn)
                assert not pieces and not points

            def start_half(half):
                v.wait_ge(s_M, 32 * GROUP * (half + 1))
                V.tensor_scalar(bias[:, :, :], mrow_i[:, :, :], 0.0, -1.0e5, ALU.is_equal, ALU.mult)
                v.drain()
                V.tensor_scalar(bias[:, :, :], bias[:, :, :], 0.5, None, ALU.add)
                v.drain()

            V.memset(vo[:, :, D:D + 1], 1.0)
            start = ring(-1, USES_START)
            y_parts(start)
            for c in range(2):
                degrees(start, c)
            add_aggregate(0, xns[0])
            moments(xns[0])
            scale_and_shift(1)
            start_half(0)
            graph(0, 0, 0, first=True)
            graph(1, 1, 4)
            with v.Fori(1, G // 4) as pair:
                for par in range(2):
                    graph(pair * 2 + par, par, pair * 8 + 4 * par)
            v.drain().then_inc(s_dil, 1)
            graph(GROUP, 0, 0, plan=PLAN_LATE)
            graph(GROUP + 1, 1, 4)
            with v.Fori(1, G // 4 - 1) as pair:
                for par in range(2):
                    graph(pair * 2 + (GROUP + par), par, pair * 8 + 4 * par)
            graph(G - 2, 0, CH - 8)
            graph(G - 1, 1, CH - 4, plan=PLAN_LAST, last=True)
            scale_and_shift(norm(G - 1, 2, True))
            v.drain().then_inc(s_dil, 1)


def layer_3(nc, S):
    f32, bf16, u8, i32 = mybir.dt.float32, mybir.dt.bfloat16, mybir.dt.uint8, mybir.dt.int32
    ALU, ACT, AX = mybir.AluOpType, mybir.ActivationFunctionType, mybir.AxisListType
    V, A, PE, GP = nc.vector, nc.scalar, nc.tensor, nc.gpsimd
    mask_tiles, blocks, Wl, bl = S.inputs_3
    ident, ident16, row0, eps_t = S.ident, S.ident16, S.row0, S.eps_t
    L = len(blocks)

    ctx = ExitStack()
    with ctx:
        def sb(name, shape, dt):
            return ctx.enter_context(nc.sbuf_tensor(name, shape, dt))

        def sem(name):
            return ctx.enter_context(nc.semaphore(name))

        wrx = sb("wrx", [P, L, 2 * D], f32)
        wrx_s = sb("wrx_s", [P, 2 * D], f32)
        wl = sb("wl", [P, L, D], f32)
        wl_s = sb("wl_s", [P, L, D], f32)
        brow = sb("brow", [P, L + 1, 2 * D], f32)
        gb = sb("gb", [P, L, 2], f32)
        crow = sb("crow", [P, 2 * D], f32)
        blrow = sb("blrow", [P, D], f32)
        mask_i = sb("mask_i", [P, G, T], i32)
        mf = sb("mf", [P, G, T], f32)
        ad = [sb(f"ad{i}", [P, T, N], bf16) for i in range(2)]
        adt = [sb(f"adt{i}", [P, T, N], bf16) for i in range(2)]
        hin = [sb(f"hin{i}", [P, L, N], f32) for i in range(2)]
        hout = [sb(f"hout{i}", [P, N], f32) for i in range(2)]
        rest = sb("rest3", [P, T, D], f32)
        z = sb("z", [P, T, D], f32)
        sq = sb("sq", [P, T, D], f32)
        junk = sb("junk", [P, N], f32)
        y3 = sb("y33", [P, 3, T, D + 1], bf16)
        rden = sb("rden3", [P, T], f32)
        ss = sb("ss", [P, T], f32)
        nrm = sb("nrm", [P, T], f32)
        sums = sb("sums", [P, 2, G], f32)
        bn = sb("bn", [P, 8], f32)
        betas = sb("betas", [P, L, P], f32)
        x3 = [sb(f"x3{i}", [P, T, D], f32) for i in range(2)]
        xo = [sb(f"xo{i}", [P, T, D], f32) for i in range(2)]
        stats = sb("stats3", [P, T, 6], f32)
        mv = sb("mv3", [P, T, 2], f32)
        std = sb("std3", [P, T], f32)
        ps = ctx.enter_context(nc.psum_tensor("ps3", [P, SLOTS, N], f32))

        cn = counts(USES_SAGE)
        full = {k: sem(f"sage_{k}_in_psum") for k in cn}
        read = {k: sem(f"sage_{k}_read") for k in cn}
        s_w = sem("sage_weights_loaded")
        s_ad = [sem(f"dilated{i}_loaded") for i in range(2)]
        s_adt = [sem(f"adt{i}_loaded") for i in range(2)]
        s_adts = [sem(f"adt{i}_stored") for i in range(2)]
        s_hin = [sem(f"h{i}_loaded") for i in range(2)]
        s_hs = [sem(f"h{i}_stored") for i in range(2)]
        s_parts = sem("sage_y_parts_ready")
        s_ss = sem("squares_summed")
        s_nrm = sem("norms_ready")
        s_r = sem("r_ready")
        s_bnv = sem("bn_variance_ready")
        s_bns = sem("bn_std_ready")
        s_beta = sem("beta_ready")
        s_crow = sem("crow_in_psum")
        s_crowc = sem("crow_copied")
        s_pin = [sem(f"final{i}_loaded") for i in range(2)]
        s_pp = sem("projection_in_psum")
        s_pr = sem("projection_read")
        s_var = sem("final_variance_ready")
        s_std = sem("final_std_ready")
        s_out = sem("out_ready")
        s_st = [sem(f"out{i}_stored") for i in range(2)]

        def nth(g, count, i=0):
            return g * count + (i + 1)

        def even(g, par):
            return g * 8 + (16 - 8 * par)

        def each_graph(eng, body):
            body(0, 0, True)
            body(1, 1, True)
            with eng.Fori(1, G // 2) as pair:
                for par in range(2):
                    body(pair * 2 + par, par, False)

        block = ctx.enter_context(nc.Block())

        @block.sync
        def _(sp):
            sp.dma_start(mask_i[:, :, :], mask_tiles).then_inc(s_w, 16)
            for l, (Wr, Wx, b, g, be) in enumerate(blocks):
                sp.dma_start(wrx[:, l, 0:D], Wr).then_inc(s_w, 16)
                sp.dma_start(wrx[:, l, D:2 * D], Wx).then_inc(s_w, 16)
                sp.dma_start(wl[:, l, :], Wl[D * l:D * l + D, :]).then_inc(s_w, 16)
                sp.dma_start(gb[:, l, 0:1], g.rearrange("(d o) -> d o", o=1)).then_inc(s_w, 16)
                sp.dma_start(gb[:, l, 1:2], be.rearrange("(d o) -> d o", o=1)).then_inc(s_w, 16)
            sp.wait_ge(S.zeroed, 1)
            for l, (Wr, Wx, b, g, be) in enumerate(blocks):
                sp.dma_start(brow[0:1, l, D:2 * D], b.rearrange("(o d) -> o d", o=1)).then_inc(s_w, 16)
            sp.dma_start(brow[0:1, L, 0:D], bl.rearrange("(o d) -> o d", o=1)).then_inc(s_w, 16)

            for l in range(L):
                def graph(b, par, peeled):
                    g = b + l * G
                    if l > 0:
                        sp.wait_ge(full["agg"], (g - 1) * cn["agg"])
                        sp.dma_start(adt[par][:, :, :], S.adt_dram[b]).then_inc(s_adt[par], 16)
                    if l > 0 or not peeled:
                        sp.wait_ge(full["yz"], (g - 1) * cn["yz"])
                    sp.dma_start(hin[par][:, 0, :], S.h_dram[l, b]).then_inc(s_hin[par], 16)
                    if not peeled:
                        store(g - 2, b - 2, par)

                def store(g, b, par):
                    if l == 0:
                        sp.wait_ge(read["adt"], nth(g, cn["adt"], T - 1))
                        sp.dma_start(S.adt_dram[b], adt[par][:, :, :]).then_inc(s_adts[par], 16)
                    sp.wait_ge(read["rt"], nth(g, 1))
                    sp.dma_start(S.h_dram[l + 1, b], hout[par][:, :]).then_inc(s_hs[par], 16)

                each_graph(sp, graph)
                for par in range(2):
                    store(l * G + G - 2 + par, G - 2 + par, par)
                for par in range(2):
                    sp.wait_ge(s_hs[par], 8 * G * (l + 1))
                    sp.wait_ge(s_adts[par], 8 * G)

            def final(b, par, peeled):
                if not peeled:
                    sp.wait_ge(s_pp, b - 1)
                    sp.wait_ge(s_out, b - 1)
                else:
                    sp.wait_ge(full["yz"], L * G * cn["yz"])
                for l in range(L):
                    sp.dma_start(hin[par][:, l, :], S.h_dram[l + 1, b]).then_inc(s_pin[par], 16)
                sp.dma_start(x3[par][:, :, :], S.x3_dram[b].rearrange("(t p) d -> p t d", p=P)).then_inc(s_pin[par], 16)
                if not peeled:
                    final_store(b - 2, par)

            def final_store(b, par):
                sp.wait_ge(s_out, nth(b, 1))
                sp.dma_start(S.out[b].rearrange("(t p) d -> p t d", p=P), xo[par][:, :, :]).then_inc(s_st[par], 16)

            each_graph(sp, final)
            for par in range(2):
                final_store(G - 2 + par, par)
            for par in range(2):
                sp.wait_ge(s_st[par], 8 * G)

        @block.gpsimd
        def _(gp):
            GP.memset(brow[:, :, :], 0.0)
            gp.drain().then_inc(S.zeroed, 1)

            def graph(b, par, peeled):
                if not peeled:
                    gp.wait_ge(full["adt"], (b - 1) * cn["adt"])
                gp.dma_start(ad[par][:, :, :], S.dilated[b].rearrange("(t p) c -> p t c", p=P)).then_inc(s_ad[par], 16)

            each_graph(gp, graph)

        @block.tensor
        def _(pe):
            pe.wait_ge(s_w, 16 * (1 + 5 * L + L + 1))
            PE.matmul(ps[:, 0, 0:2 * D], row0[:, :], brow[:, 0, :], start=True, stop=True).then_inc(s_crow, 1)
            pe.wait_ge(s_crowc, 1)

            for l in range(L):
                uses = USES_SAGE if l == 0 else USES_SAGE_LATER

                def graph(b, par, peeled):
                    g = b + l * G
                    at = [0]

                    def slot():
                        n = at[0]
                        at[0] += 1
                        m, before = earlier_use(uses, n)
                        kind = uses[m]
                        if not before:
                            pe.wait_ge(read[kind], nth(g, cn[kind], number(uses, m)))
                        elif not (isinstance(b, int) and b == 0):
                            pe.wait_ge(read[kind], nth(g - 1, cn[kind], number(uses, m)))
                        return ps[:, slot_of(n), :]

                    def slot_of(n):
                        return n % SLOTS

                    if l == 0:
                        pe.wait_ge(s_ad[par], even(b, par))
                        for j in range(T):
                            o = slot()
                            for i in range(T):
                                ins = PE.matmul(o[:, P * i:P * i + P], ad[par][:, i, P * j:P * j + P], ident16[:, :],
                                                start=True, stop=True)
                            ins.then_inc(full["adt"], 1)
                    pe.wait_ge(s_hin[par], even(g, par))
                    w = wrx[:, 0, :] if l == 0 else wrx_s[:, :]
                    for t in range(T):
                        if t % 4 == 0:
                            o = slot()
                        r = 256 * (t % 4)
                        ins = PE.matmul(o[:, r:r + 256], hin[par][:, 0, P * t:P * t + P], w, start=True, stop=True)
                        if t % 4 == 3:
                            ins.then_inc(full["yz"], 1)
                    if l == 0:
                        pe.wait_ge(read["adt"], nth(b, cn["adt"], T - 1))
                    else:
                        pe.wait_ge(s_adt[par], even(b + (l - 1) * G, par))
                    for i in range(T):
                        if i % 4 == 0:
                            o = slot()
                        if i == 0:
                            pe.wait_ge(s_parts, nth(g, 1))
                        r = 256 * (i % 4)
                        for j in range(T):
                            wj = adt[par][:, j, P * i:P * i + P]
                            PE.matmul(o[:, r:r + 129], wj, y3[:, 0, j, :], start=(j == 0), stop=False)
                            PE.matmul(o[:, r:r + 128], wj, y3[:, 1, j, 0:D], start=False, stop=False)
                            ins = PE.matmul(o[:, r:r + 128], wj, y3[:, 2, j, 0:D], start=False, stop=(j == T - 1))
                        if i % 4 == 3:
                            ins.then_inc(full["agg"], 1)
                    o = slot()
                    pe.wait_ge(s_r, nth(g, 1))
                    for t in range(T):
                        ins = PE.transpose(o[:, P * t:P * t + P], z[:, t, :], ident[:, :])
                    ins.then_inc(full["rt"], 1)

                each_graph(pe, graph)
                pe.wait_ge(s_beta, l + 1)
                if l < L - 1:
                    PE.matmul(ps[:, 0, 0:2 * D], betas[:, l, :], wrx[:, l + 1, :], start=True, stop=False)
                    PE.matmul(ps[:, 0, 0:2 * D], row0[:, :], brow[:, l + 1, :], start=False, stop=True).then_inc(s_crow, 1)
                else:
                    for m in range(L):
                        PE.matmul(ps[:, 0, 0:D], betas[:, m, :], wl[:, m, :], start=(m == 0), stop=(m == L - 1))
                    PE.matmul(ps[:, 1, 0:D], row0[:, :], brow[:, L, 0:D], start=True, stop=True).then_inc(s_crow, 1)
                pe.wait_ge(s_crowc, l + 2)

            def final(b, par, peeled):
                pe.wait_ge(s_pin[par], even(b, par) * (L + 1))
                if not peeled:
                    pe.wait_ge(s_pr, b - 1)
                for t in range(T):
                    for l in range(L):
                        ins = PE.matmul(ps[:, par, P * t:P * t + P], hin[par][:, l, P * t:P * t + P], wl_s[:, l, :],
                                        start=(l == 0), stop=(l == L - 1))
                ins.then_inc(s_pp, 1)

            each_graph(pe, final)

        @block.scalar
        def _(act):
            for l in range(L):
                uses = USES_SAGE if l == 0 else USES_SAGE_LATER

                def graph(b, par, peeled):
                    g = b + l * G
                    if l == 0:
                        if not peeled:
                            act.wait_ge(s_adts[par], even(b - 2, par))
                        for j in range(T):
                            act.wait_ge(full["adt"], nth(b, cn["adt"], j))
                            A.copy(adt[par][:, j, :], ps[:, j % SLOTS, :]).then_inc(read["adt"], 1)
                    act.wait_ge(s_ss, nth(g, 1))
                    A.activation(nrm[:, :], ss[:, :], ACT.Sqrt).then_inc(s_nrm, 1)
                    if l > 0 or not peeled:
                        act.wait_ge(s_hs[par], even(g - 2, par))
                    act.wait_ge(full["rt"], nth(g, 1))
                    o = ps[:, (len(uses) - 1) % SLOTS, :]
                    A.activation(hout[par][:, :], o, ACT.Copy, accum_out=sums[:, 0, bass.ds(b, 1)])
                    A.activation(junk[:, :], o, ACT.Square, accum_out=sums[:, 1, bass.ds(b, 1)])
                    act.drain().then_inc(read["rt"], 1)

                each_graph(act, graph)
                act.wait_ge(s_bnv, l + 1)
                A.activation(bn[:, 3:4], bn[:, 2:3], ACT.Sqrt, bias=eps_t[:, 0:1]).then_inc(s_bns, 1)

            def final(b, par, peeled):
                act.wait_ge(s_var, nth(b, 1))
                A.activation(std[:, :], mv[:, :, 1], ACT.Sqrt, bias=eps_t[:, 0:1]).then_inc(s_std, 1)

            each_graph(act, final)

        @block.vector
        def _(v):
            V.memset(y3[:, 0, :, D:D + 1], 1.0)
            v.wait_ge(s_w, 16 * (1 + 5 * L + L + 1))
            V.tensor_copy(mf[:, :, :], mask_i[:, :, :])
            v.wait_ge(s_crow, 1)
            V.tensor_copy(crow[:, :], ps[:, 0, 0:2 * D])
            v.drain().then_inc(s_crowc, 1)

            for l in range(L):
                uses = USES_SAGE if l == 0 else USES_SAGE_LATER
                yz0, agg0 = uses.index("yz"), uses.index("agg")

                def graph(b, par, peeled):
                    g = b + l * G
                    for c in range(2):
                        v.wait_ge(full["yz"], nth(g, cn["yz"], c))
                        o = ps[:, (yz0 + c) % SLOTS, :].rearrange("p (t d) -> p t d", t=4)
                        rows = slice(4 * c, 4 * c + 4)
                        V.tensor_tensor(rest[:, rows, :], o[:, :, 0:D], crow[:, 0:D].unsqueeze(1).broadcast_to([P, 4, D]), ALU.add)
                        V.tensor_tensor(z[:, rows, :], o[:, :, D:2 * D], crow[:, D:2 * D].unsqueeze(1).broadcast_to([P, 4, D]), ALU.add)
                        v.drain().then_inc(read["yz"], 1)
                    for s in range(3):
                        V.tensor_copy(y3[:, s, :, 0:D], rest[:, :, :])
                        v.drain()
                        if s < 2:
                            V.tensor_tensor(rest[:, :, :], rest[:, :, :], y3[:, s, :, 0:D], ALU.subtract)
                            v.drain()
                    v.sem_inc(s_parts, 1)
                    for c in range(2):
                        v.wait_ge(full["agg"], nth(g, cn["agg"], c))
                        o = ps[:, (agg0 + c) % SLOTS, :].rearrange("p (t d) -> p t d", t=4)
                        V.tensor_scalar(rden[:, 4 * c:4 * c + 4], o[:, :, D], 1.0, None, ALU.max)
                        v.drain()
                        V.reciprocal(rden[:, 4 * c:4 * c + 4], rden[:, 4 * c:4 * c + 4])
                        v.drain()
                        for t in range(4):
                            m = 4 * c + t
                            V.scalar_tensor_tensor(z[:, m, :], o[:, t, 0:D], rden[:, m:m + 1], z[:, m, :], ALU.mult, ALU.add)
                        v.drain().then_inc(read["agg"], 1)
                    V.tensor_tensor(sq[:, :, :], z[:, :, :], z[:, :, :], ALU.mult)
                    v.drain()
                    V.tensor_reduce(ss[:, :], sq[:, :, :], AX.X, ALU.add).then_inc(s_ss, 1)
                    v.wait_ge(s_nrm, nth(g, 1))
                    V.tensor_scalar(nrm[:, :], nrm[:, :], 1e-12, None, ALU.max)
                    v.drain()
                    V.reciprocal(nrm[:, :], nrm[:, :])
                    v.drain()
                    V.tensor_tensor(nrm[:, :], nrm[:, :], mf[:, bass.ds(b, 1), :].rearrange("p o t -> p (o t)"), ALU.mult)
                    v.drain()
                    for t in range(T):
                        V.tensor_scalar(z[:, t, :], z[:, t, :], nrm[:, t:t + 1], 0.0, ALU.mult, ALU.max)
                    v.drain().then_inc(s_r, 1)

                def graph_in_order(b, par, peeled):
                    graph(b, par, peeled)
                    v.wait_ge(full["rt"], nth(b + l * G, 1))

                each_graph(v, graph_in_order)
                v.wait_ge(read["rt"], (l + 1) * G)
                V.tensor_reduce(bn[:, 0:2], sums[:, :, :], AX.X, ALU.add)
                v.drain()
                V.tensor_scalar(bn[:, 0:2], bn[:, 0:2], 1.0 / (G * N), None, ALU.mult)
                v.drain()
                V.tensor_tensor(bn[:, 4:5], bn[:, 0:1], bn[:, 0:1], ALU.mult)
                v.drain()
                V.tensor_tensor(bn[:, 2:3], bn[:, 1:2], bn[:, 4:5], ALU.subtract)
                v.drain().then_inc(s_bnv, 1)
                v.wait_ge(s_bns, l + 1)
                V.reciprocal(bn[:, 5:6], bn[:, 3:4])
                v.drain()
                V.tensor_tensor(bn[:, 5:6], bn[:, 5:6], gb[:, l, 0:1], ALU.mult)
                v.drain()
                V.tensor_tensor(bn[:, 6:7], bn[:, 0:1], bn[:, 5:6], ALU.mult)
                v.drain()
                V.tensor_tensor(bn[:, 6:7], gb[:, l, 1:2], bn[:, 6:7], ALU.subtract)
                v.drain()
                V.tensor_copy(betas[:, l, :], bn[:, 6:7].broadcast_to([P, P]))
                V.tensor_scalar(wl_s[:, l, :], wl[:, l, :], bn[:, 5:6], None, ALU.mult)
                if l < L - 1:
                    V.tensor_scalar(wrx_s[:, :], wrx[:, l + 1, :], bn[:, 5:6], None, ALU.mult)
                v.drain().then_inc(s_beta, 1)
                v.wait_ge(s_crow, l + 2)
                V.tensor_copy(crow[:, 0:2 * D if l < L - 1 else D], ps[:, 0, 0:2 * D if l < L - 1 else D])
                if l == L - 1:
                    V.tensor_copy(blrow[:, :], ps[:, 1, 0:D])
                v.drain().then_inc(s_crowc, 1)

            def final(b, par, peeled):
                xf = xo[par]
                m = mf[:, bass.ds(b, 1), :].rearrange("p o t -> p (o t)").unsqueeze(2).broadcast_to([P, T, D])
                if not peeled:
                    v.wait_ge(s_st[par], even(b - 2, par))
                v.wait_ge(s_pp, nth(b, 1))
                v.wait_ge(s_pin[par], even(b, par) * (L + 1))
                V.tensor_tensor(xf[:, :, :], ps[:, par, :].rearrange("p (t d) -> p t d", t=T),
                                crow[:, 0:D].unsqueeze(1).broadcast_to([P, T, D]), ALU.add)
                v.drain().then_inc(s_pr, 1)
                V.tensor_tensor(xf[:, :, :], xf[:, :, :], m, ALU.mult)
                v.drain()
                V.tensor_tensor(xf[:, :, :], xf[:, :, :], blrow[:, :].unsqueeze(1).broadcast_to([P, T, D]), ALU.add)
                v.drain()
                V.tensor_tensor(xf[:, :, :], xf[:, :, :], m, ALU.mult)
                v.drain()
                V.tensor_tensor(xf[:, :, :], xf[:, :, :], x3[par][:, :, :], ALU.add)
                v.drain()
                for t in range(T):
                    V.bn_stats(stats[:, t, :], xf[:, t, :])
                v.drain()
                for t in range(T):
                    V.bn_aggr(mv[:, t, :], stats[:, t, :])
                v.drain().then_inc(s_var, 1)
                v.wait_ge(s_std, nth(b, 1))
                V.reciprocal(rden[:, :], std[:, :])
                v.drain()
                for t in range(T):
                    V.tensor_scalar(xf[:, t, :], xf[:, t, :], mv[:, t, 0:1], rden[:, t:t + 1], ALU.subtract, ALU.mult)
                v.drain().then_inc(s_out, 1)

            each_graph(v, final)


def build(nc, S):
    f32, bf16, u8 = mybir.dt.float32, mybir.dt.bfloat16, mybir.dt.uint8
    S.dilated = nc.dram_tensor("dilated", [G, N, N], u8, kind="Internal").ap()
    S.adt_dram = nc.dram_tensor("adt_dram", [G, P, T, N], bf16, kind="Internal").ap()
    S.x3_dram = nc.dram_tensor("x3_dram", [G, N, D], f32, kind="Internal").ap()
    S.h_dram = nc.dram_tensor("h_dram", [4, G, D, N], f32, kind="Internal").ap()
    with ExitStack() as ctx:
        S.ident = ctx.enter_context(nc.sbuf_tensor("ident", [P, P], f32))
        S.ident16 = ctx.enter_context(nc.sbuf_tensor("ident16", [P, P], bf16))
        S.row0 = ctx.enter_context(nc.sbuf_tensor("row0", [P, P], f32))
        S.eps_t = ctx.enter_context(nc.sbuf_tensor("eps_t", [P, 1], f32))
        S.zeroed = ctx.enter_context(nc.semaphore("bias_rows_zeroed"))
        layers_0_to_2(nc, S)
        layer_3(nc, S)


_NAMES = ["x", "adj", "nodemask", "L0_gnn_U", "L1_gnn_Wv", "L1_gnn_bv", "L1_gnn_Wk", "L1_gnn_bk",
          "L1_gnn_Wq", "L1_gnn_bq", "L2_gnn_W", "L2_gnn_a"]
_NAMES += [f"L3_gnn_{w}{l}" for l in (1, 2, 3) for w in ("Wr", "Wx", "b", "g", "be")]
_NAMES += ["L3_gnn_Wl", "L3_gnn_bl"]


def kernel(**inputs):
    from types import SimpleNamespace

    import numpy as np
    import concourse.bacc as bacc
    from concourse.bass_utils import run_bass_kernel_spmd

    nc = bacc.Bacc("TRN2", target_bir_lowering=False, num_devices=1)
    arrays, ap = {}, {}

    def give(name, a):
        arrays[name] = a
        ap[name] = nc.dram_tensor(name, a.shape, mybir.dt.from_np(a.dtype), kind="ExternalInput").ap()

    for name in _NAMES:
        a = np.ascontiguousarray(inputs[name])
        if name == "nodemask":
            give("mask_rows", np.ascontiguousarray(a.reshape(G, CH, W32).transpose(0, 2, 1)))
            give("mask_tiles", np.ascontiguousarray(a.reshape(G, T, P).transpose(2, 0, 1)))
        else:
            give(name, a)
    out = nc.dram_tensor("out", (G, N, D), mybir.dt.float32, kind="ExternalOutput").ap()
    S = SimpleNamespace(out=out)
    S.inputs_0_to_2 = [ap[n] for n in ["x", "adj", "mask_rows"] + _NAMES[3:12]]
    S.inputs_3 = (ap["mask_tiles"], [[ap[f"L3_gnn_{w}{l}"] for w in ("Wr", "Wx", "b", "g", "be")] for l in (1, 2, 3)],
                  ap["L3_gnn_Wl"], ap["L3_gnn_bl"])
    build(nc, S)
    r = run_bass_kernel_spmd(nc, [arrays], core_ids=[0])
    return r.results[0]["out"]
```

```python
from contextlib import ExitStack

import concourse.bass as bass
from concourse import mybir

G, N, D = 16, 1024, 128
P = 128
T = N // P
HALF = N // 2
HEADS = 4
DH = D // HEADS
HALVES = (slice(0, HEADS // 2), slice(HEADS // 2, HEADS))
EPS = 1e-5
STEEP = 1e20
BIG = 9.0e15
CLAMP = 9.0e13
SLOPE = 0.2
W32 = 32
CH = N // W32
QB = 2
GROUP = 4 * QB
MAGIC = 8388608.0

USES_START = ["xt", "y", "agg", "agg"]


def uses_of(first=False, last=False):
    u = ["x1t", "q", "k", "v", "s", "s"]
    for i in range(T):
        u += ["t"] + (["s"] if i + 2 < T else []) + ["o"]
        if i == 0 and not first:
            u += ["x3t"]
    u += ([] if last else ["xt", "y"]) + ["x2t", "wh", "wh", "sj"] + ([] if last else ["agg", "agg"])
    return u + ["qa", "sj", "sj", "qa", "sj"]


USES = uses_of()
RING = 3
HEAD_SLOT = 3
PLAN = (1, 0, 2, 1, 1, 1, 1, 2, 1, 1, 1, 2, 2, 2, 2)
PLAN_LATE = (0, 0, 0, 0, 0, 0, 0, 0, 0, 2, 2, 4, 4, 4, 4)
PLAN_LAST = PLAN[:9] + (3, 3, 2, 2)
TILES2 = HEADS * T
TP = 5
SLOTS = 4


def counts(uses):
    return {kind: uses.count(kind) for kind in uses}


def number(uses, n):
    return uses[:n].count(uses[n])


def layers_0_to_2(nc, S):
    f32, bf16, f16 = mybir.dt.float32, mybir.dt.bfloat16, mybir.dt.float16
    u8, i32 = mybir.dt.uint8, mybir.dt.int32
    ALU, ACT, AX = mybir.AluOpType, mybir.ActivationFunctionType, mybir.AxisListType
    V, A, PE, GP = nc.vector, nc.scalar, nc.tensor, nc.gpsimd
    x, adj, mask_rows, U0, Wv, bv, Wk, bk, Wq, bq, W2, a2 = S.inputs_0_to_2
    dilated, x3_dram, h_dram = S.dilated, S.x3_dram, S.h_dram
    ident, ident16, row0, ones3, eps_t = S.ident, S.ident16, S.row0, S.ones3, S.eps_t

    ctx = ExitStack()
    with ctx:
        def sb(name, shape, dt):
            return ctx.enter_context(nc.sbuf_tensor(name, shape, dt))

        def sem(name):
            return ctx.enter_context(nc.semaphore(name))

        bigI = sb("bigI", [P, P], bf16)
        ones0 = sb("ones0", [P, P], bf16)
        negbig = sb("negbig", [P, HALF], bf16)
        u0 = sb("u0", [P, D], f32)
        wt = sb("wt", [P, 4, D], f32)
        wext = sb("wext", [P, D + 2 * HEADS], f32)
        ablk = sb("ablk", [P, 2 * HEADS], f32)
        wab = sb("wab", [P, HEADS, P], f32)
        bqk = sb("bqk", [P, 2], f32)
        bv3 = sb("bv3", [P, D], bf16)

        adjb = [sb(f"adj{i}", [P, T, N], bf16) for i in range(2)]
        xns = [sb(f"xn{i}", [P, T, D], f32) for i in range(2)]
        xTs = [sb(f"xT{i}", [P, N], f32) for i in range(2)]
        pN = sb("pN", [P, 2, N], f32)
        wload = pN[:, 0, 0:4 * D].rearrange("p (i d) -> p i d", i=4)
        pT_qa = sb("pT_qa", [P, 2 * T * P], f32)
        pT = pT_qa[:, 0:2 * N].rearrange("p (i j c) -> p i j c", i=2, j=T)
        qa = pT_qa[:, 0:T * HEADS * 33].rearrange("p (two t h c) -> p two t h c", two=2, t=T, h=HEADS // 2)
        qT = sb("qT", [P, N], f32)
        kT = sb("kT", [P, N], f32)
        bvrow = kT[:, 0:D]
        bv16 = qT[:, :].bitcast(bf16)[:, 0:3 * D].rearrange("p (s d) -> p s d", s=3)
        y3 = pN[:, :, :].rearrange("p i c -> p (i c)").bitcast(bf16)[:, 0:3 * T * (D + 1)]\
            .rearrange("p (s t c) -> p s t c", s=3, t=T)
        y_rest = kT[:, :].rearrange("p (t c) -> p t c", t=T)
        agg = qT[:, :].rearrange("p (t c) -> p t c", t=T)
        vo = sb("vo", [P, T, D + 1], f32)
        vs = sb("vs", [P, T, 3, HEADS, 66], bf16)
        va = sb("va", [P, T, HEADS, 66], f32)
        wh = sb("wh", [P, T, D + 2 * HEADS], f32)
        step = sb("step", [P, T, N], bf16)
        steep = sb("steep", [P, T, HEADS], f32)
        rden = sb("rden", [P, T], f32)
        odn = sb("odn", [P, T], f32)
        cden = sb("cden", [P, T], f32)
        stats = sb("stats", [P, T, 6], f32)
        mv = sb("mv", [P, T, 2], f32)
        std = sb("std", [P, T], f32)
        shift = sb("shift", [P, T], f32)
        mx = sb("mx", [P, 2, T], f32)
        smax = sb("smax", [P, HEADS], f32)
        gmax = sb("gmax", [P, HEADS], f32)
        sc = sb("sc", [P, 3, T, HEADS], f32)
        ex = sb("ex", [P, 4, T, HEADS], f32)
        comb = sb("comb", [P, 2, T, 33], f32)

        M32 = sb("M32", [P, CH, QB, N // 4], i32)
        M = M32[:, :, :, :].rearrange("p s g c -> p (s g c)").bitcast(u8).rearrange("p (s g c) -> p s g c", s=CH, g=QB)
        mrow_i = sb("mrow_i", [P, QB, CH], i32)
        bias = sb("bias", [P, QB, CH], f32)
        upper = sb("upper", [P, QB, W32], f32)
        lower = sb("lower", [P, QB, W32], f16)
        cw = sb("cw", [P, QB, W32], f32)
        cu = sb("cu", [P, QB, W32], f32)
        dwin = sb("dwin", [P, QB, W32 + 1], f32)
        dnew = sb("dnew", [P, QB, W32], f32)
        keepz = sb("keepz", [P, QB, W32 + 1], f32)
        rk = sb("rk", [P, QB, W32 + 1], f32)
        rem = sb("rem", [P, QB, W32], f32)
        remT = sb("remT", [P, QB, W32], f32)
        e1 = sb("e1", [P, QB, W32], f32)
        small = sb("small", [P, 6, QB], f32)
        num, even_up, big, first, last, after = (small[:, i, :] for i in range(6))
        tiny = sb("tiny", [P, QB], f32)
        fl = sb("fl", [P, W32], f32)
        flT = sb("flT", [P, W32], f32)
        fl0 = sb("fl0", [1, P], f32)
        flag = sb("flag", [1, 1], i32)
        rank32 = sb("rank32", [P, 2, QB, N // 4], i32)
        rank = rank32[:, :, :, :].rearrange("p i g c -> p (i g c)").bitcast(f16).rearrange("p (g c) -> p g c", g=QB)
        rm = sb("rm", [P, QB, N], f16)
        rm32 = sb("rm32", [P, QB, N // 4], i32)
        rmT32, hit32 = rank32[:, 0], rank32[:, 1]
        rm8, rmT = (w.rearrange("p g c -> p (g c)").bitcast(u8).rearrange("p (g c) -> p g c", g=QB)
                    for w in (rm32[:, :, :], rmT32))

        ps = ctx.enter_context(nc.psum_tensor("ps", [P, SLOTS, N], f32))

        s_const = sem("const_ready")
        s_turn = sem("gpsimd_waited")
        s_w = sem("weights_loaded")
        s_wt = sem("weights_transposed")
        s_wtc = sem("weights_copied")
        s_wa = sem("wa_in_psum")
        s_wac = sem("wa_copied")
        full = {k: sem(f"{k}_in_psum") for k in counts(USES)}
        read = {k: sem(f"{k}_read") for k in counts(USES)}
        s_adj = [sem(f"adj{i}_loaded") for i in range(2)]
        s_x = [sem(f"x{i}_loaded") for i in range(2)]
        s_parts = sem("y_part_ready")
        s_yrest = sem("y_rest_ready")
        s_aggd = sem("degrees_inverted")
        s_var = sem("variance_ready")
        s_std = sem("std_ready")
        s_shift = sem("shift_ready")
        s_xn = sem("xn_ready")
        s_xnst = sem("x3_stored")
        s_nmx = sem("row_max_ready")
        s_clamped = sem("p_clamped")
        s_smax = sem("src_max_of_partitions")
        s_gmax = sem("src_max_everywhere")
        s_sc = sem("exponents_ready")
        s_ex = sem("exponentials_ready")
        s_va = sem("values_weighted")
        s_vb = sem("value_rest_ready")
        s_vh = sem("value_part_rounded")
        s_step = sem("step_ready")
        s_ind = sem("masked_by_gpsimd")
        s_indv = sem("masked_by_vector")
        s_used = sem("step_used")
        s_phr = sem("head_read")
        s_hT = sem("x3t_stored")
        s_M = sem("dilation_loaded")
        s_mrow = sem("node_masks_loaded")
        s_dil = sem("dilation_done")
        s_Mst = sem("dilation_stored")

        cn = counts(USES)

        def done(b, kind, i=0):
            return (b + (1 if kind in USES_START else -1 if kind == "x3t" else 0)) * cn[kind] + (i + 1)

        def norm(b, layer, last):
            return 3 * b + {1: 2, 0: 3, 2: 3 if last else 4}[layer]

        def half_of(b, par):
            return b * 8 + (16 - 8 * par)

        def nth(b, kind_count, i=0):
            return b * kind_count + (i + 1)

        block = ctx.enter_context(nc.Block())

        @block.sync
        def _(sp):
            for i, w in enumerate((Wv, Wk, Wq, W2)):
                sp.dma_start(wload[:, i, :], w).then_inc(s_w, 16)
            sp.dma_start(u0[:, :], U0).then_inc(s_w, 16)
            sp.dma_start(bqk[:, 0:1], bq.rearrange("(d o) -> d o", o=1)).then_inc(s_w, 16)
            sp.dma_start(bqk[:, 1:2], bk.rearrange("(d o) -> d o", o=1)).then_inc(s_w, 16)
            sp.wait_ge(s_const, 1)
            for s in range(3):
                sp.dma_start(bvrow[32 * s:32 * s + 1, :], bv.rearrange("(o d) -> o d", o=1)).then_inc(s_w, 16)
            for h in range(HEADS):
                for e in range(2):
                    sp.dma_start(ablk[DH * h:DH * h + DH, HEADS * e + h:HEADS * e + h + 1],
                                 a2[h, DH * e:DH * e + DH].rearrange("(d o) -> d o", o=1)).then_inc(s_w, 16)

            def load(b, par):
                sp.dma_start(xns[par][:, :, :], x[b].rearrange("(t p) d -> p t d", p=P)).then_inc(s_x[par], 16)

            def graph(b, par, last=False, more=True):
                sp.wait_ge(s_xn, norm(b, 2, last))
                sp.dma_start(x3_dram[b].rearrange("(t p) d -> p t d", p=P), xns[par][:, :, :]).then_inc(s_xnst, 16)
                sp.wait_ge(read["x3t"], nth(b, 1))
                sp.dma_start(h_dram[0, b], xTs[par][:, :]).then_inc(s_hT, 16)
                if more:
                    sp.wait_ge(s_xnst, nth(b, 16, 15))
                    load(b + 2, par)

            def store_dilation(half):
                sp.wait_ge(s_dil, half + 1)
                for q in range(4):
                    for g in range(QB):
                        b = GROUP * half + QB * q + g
                        sp.dma_start(dilated[b].rearrange("(s r) c -> r s c", r=W32),
                                     M[32 * q:32 * q + 32, :, g, :]).then_inc(s_Mst, 16)

            def load_masks(half):
                for q in range(4):
                    for g in range(QB):
                        sp.dma_start(mrow_i[32 * q:32 * q + 32, g, :], mask_rows[GROUP * half + QB * q + g]).then_inc(s_mrow, 16)

            load(0, 0)
            load(1, 1)
            load_masks(0)
            with sp.Fori(0, G // 4 - 1) as pair:
                for par in range(2):
                    graph(pair * 2 + par, par)
            graph(GROUP - 2, 0)
            store_dilation(0)
            load_masks(1)
            graph(GROUP - 1, 1)
            with sp.Fori(G // 4, G // 2 - 1) as pair:
                for par in range(2):
                    graph(pair * 2 + par, par)
            graph(G - 2, 0, more=False)
            graph(G - 1, 1, last=True, more=False)
            store_dilation(1)
            sp.wait_ge(s_Mst, 16 * G)
            sp.wait_ge(s_xnst, 16 * G)
            sp.wait_ge(s_hT, 16 * G)

        @block.gpsimd
        def _(gp):
            GP.memset(bvrow, 0.0)
            GP.memset(ablk[:, :], 0.0)
            GP.memset(ident[:, :], 0.0)
            GP.memset(row0[:, :], 0.0)
            GP.memset(ones0[:, :], 0.0)
            GP.memset(ones3[:, :], 0.0)
            GP.memset(bv3[:, :], 0.0)
            GP.memset(negbig[:, :], 0.0)
            GP.memset(upper[:, :, :], 0.0)
            GP.memset(lower[:, :, :], 0.0)
            GP.memset(eps_t[:, :], EPS)
            gp.drain()
            GP.memset(row0[0:1, :], 1.0)
            GP.memset(ones0[0:1, :], 1.0)
            for s in range(3):
                GP.memset(ones3[32 * s:32 * s + 1, :], 1.0)
            GP.memset(negbig[0:1, :], -BIG)
            gp.drain()
            GP.affine_select(out=ident[:, :], in_=ident[:, :], compare_op=ALU.not_equal, fill=1.0,
                             base=0, pattern=[[-1, P]], channel_multiplier=1)
            gp.drain()
            for q in range(4):
                u = upper[32 * q:32 * q + 32, :, :]
                GP.affine_select(out=u, in_=u, compare_op=ALU.is_ge, fill=1.0, base=0,
                                 pattern=[[0, QB], [-1, W32]], channel_multiplier=1)
                gp.drain()
                u = lower[32 * q:32 * q + 32, :, :]
                GP.affine_select(out=u, in_=u, compare_op=ALU.is_ge, fill=1.0, base=0,
                                 pattern=[[0, QB], [1, W32]], channel_multiplier=-1)
                gp.drain()
            GP.tensor_copy(ident16[:, :], ident[:, :])
            GP.tensor_scalar(bigI[:, :], ident[:, :], BIG, None, ALU.mult)
            gp.drain().then_inc(s_const, 1)

            def wait(semaphore, value):
                gp.wait_ge(semaphore, value)
                gp.sem_inc(s_turn, 1)

            def load_adj(b, par, first_one=False):
                if not first_one:
                    gp.wait_ge(s_used, (b - 1) * TILES2)
                gp.dma_start(adjb[par][:, :, :], adj[b].rearrange("(t p) c -> p t c", p=P)).then_inc(s_adj[par], 16)

            def load_dilation(half):
                for q in range(4):
                    for g in range(QB):
                        b = GROUP * half + QB * q + g
                        gp.dma_start(M[32 * q:32 * q + 32, :, g, :],
                                     adj[b].rearrange("(s r) c -> r s c", r=W32)).then_inc(s_M, 16)

            def graph(b, par, more=True, second_half=False):
                for i in range(T):
                    wait(read["s"], done(b, "s", i))
                    GP.tensor_scalar(pN[:, i % 2, :], pN[:, i % 2, :], 1.0, None, ALU.min)
                    gp.drain().then_inc(s_clamped, 1)
                wait(s_smax, nth(b, 1))
                GP.partition_all_reduce(gmax[:, :], smax[:, :], P, bass.bass_isa.ReduceOp.max).then_inc(s_gmax, 1)
                if second_half:
                    wait(s_Mst, 16 * GROUP)
                    load_dilation(1)
                for h in range(HEADS):
                    for i in range(TP):
                        wait(s_step, nth(b, TILES2, T * h + i))
                        GP.tensor_tensor(step[:, i, :], step[:, i, :], adjb[par][:, i, :], ALU.mult)
                        gp.drain().then_inc(s_ind, 1)
                if more:
                    load_adj(b + 2, par)

            load_adj(0, 0, True)
            load_adj(1, 1, True)
            load_dilation(0)
            with gp.Fori(0, G // 4) as pair:
                for par in range(2):
                    graph(pair * 2 + par, par)
            graph(GROUP, 0, second_half=True)
            graph(GROUP + 1, 1)
            with gp.Fori(1, G // 4 - 1) as pair:
                for par in range(2):
                    graph(pair * 2 + (GROUP + par), par)
            for par in range(2):
                graph(G - 2 + par, par, more=False)

        @block.tensor
        def _(pe):
            pe.wait_ge(s_const, 1)
            pe.wait_ge(s_w, 16 * 18)
            for i in range(4):
                PE.transpose(ps[:, 0, P * i:P * i + P], wload[:, i, :], ident[:, :])
            pe.drain().then_inc(s_wt, 1)
            pe.wait_ge(s_wtc, 1)
            PE.matmul(ps[:, 1, 0:2 * HEADS], wt[:, 3, :], ablk[:, :], start=True, stop=True).then_inc(s_wa, 1)
            pe.wait_ge(s_wac, 1)

            def ring(b, uses, before):
                at = [0]

                def slot():
                    n = at[0]
                    at[0] += 1
                    if n >= RING:
                        pe.wait_ge(read[uses[n - RING]], done(b, uses[n - RING], number(uses, n - RING)))
                    elif before == USES_START:
                        pe.wait_ge(read["agg"], 2)
                    elif before:
                        m = max(m for m in range(len(before)) if m % RING == n)
                        pe.wait_ge(read[before[m]], done(b - 1, before[m], number(before, m)))
                    return ps[:, n % RING, :]

                return slot

            def transposes(slot, kind, src):
                o = slot()
                for t in range(T):
                    ins = PE.transpose(o[:, P * t:P * t + P], src[:, t, :], ident[:, :])
                ins.then_inc(full[kind], 1)

            def x_times_u(b, par, slot):
                pe.wait_ge(s_x[par], half_of(b, par))
                transposes(slot, "xt", xns[par])
                o = slot()
                pe.wait_ge(read["xt"], nth(b, 1))
                for t in range(T):
                    ins = PE.matmul(o[:, P * t:P * t + P], xTs[par][:, P * t:P * t + P], u0[:, :], start=True, stop=True)
                ins.then_inc(full["y"], 1)

            def aggregate(b, par, slot):
                pe.wait_ge(s_adj[par], half_of(b, par))
                pe.wait_ge(s_parts, nth(b, 3, 2))
                for i in range(T):
                    if i % 4 == 0:
                        o = slot()
                    r = 256 * (i % 4)
                    for j in range(T):
                        w = adjb[par][:, j, P * i:P * i + P]
                        PE.matmul(o[:, r:r + 129], w, y3[:, 0, j, :], start=(j == 0), stop=False)
                        PE.matmul(o[:, r:r + 128], w, y3[:, 1, j, 0:D], start=False, stop=False)
                        ins = PE.matmul(o[:, r:r + 128], w, y3[:, 2, j, 0:D], start=False, stop=(j == T - 1))
                    if i % 4 == 3:
                        ins.then_inc(full["agg"], 1)

            def graph(b, par, before=USES, last=False):
                first = before == USES_START
                uses = uses_of(first, last)
                slot = ring(b, uses, before)
                xn, xT = xns[par], xTs[par]

                pe.wait_ge(s_xn, 1 if first else b * 3)
                transposes(slot, "x1t", xn)
                for kind, w in (("q", 2), ("k", 1)):
                    o = slot()
                    pe.wait_ge(read["x1t"], nth(b, 1))
                    for c in range(2):
                        ins = PE.matmul(o[:, HALF * c:HALF * c + HALF], wt[:, w, :], xT[:, HALF * c:HALF * c + HALF],
                                        start=True, stop=True)
                    ins.then_inc(full[kind], 1)
                o = slot()
                for t in range(T):
                    PE.matmul(o[:, P * t:P * t + P], xT[:, P * t:P * t + P], wt[:, 0, :], start=True, stop=False)
                    ins = PE.matmul(o[:, P * t:P * t + P], ones3[:, :], bv3[:, :], start=False, stop=True)
                ins.then_inc(full["v"], 1)
                pe.wait_ge(read["q"], nth(b, 1))
                pe.wait_ge(read["k"], nth(b, 1))

                def scores(i):
                    o = slot()
                    for c in range(2):
                        cols = slice(HALF * c, HALF * c + HALF)
                        PE.matmul(o[:, cols], ones0[:, :], negbig[:, :], start=True, stop=False)
                        PE.matmul(o[:, cols], bigI[:, :], adjb[par][:, i, cols], start=False, stop=False)
                        ins = PE.matmul(o[:, cols], qT[:, P * i:P * i + P], kT[:, cols], start=False, stop=True)
                    ins.then_inc(full["s"], 1)

                scores(0)
                scores(1)
                for i in range(T):
                    o = slot()
                    pe.wait_ge(s_clamped, nth(b, T, i))
                    for j in range(T):
                        ins = PE.transpose(o[:, P * j:P * j + P], pN[:, i % 2, P * j:P * j + P], ident[:, :])
                    ins.then_inc(full["t"], 1)
                    if i + 2 < T:
                        scores(i + 2)
                    o = slot()
                    pe.wait_ge(read["t"], nth(b, T, i))
                    if i == 0:
                        pe.wait_ge(read["v"], nth(b, 1))
                    for j in range(T):
                        ins = PE.matmul(o[:, 0:D + 1], pT[:, i % 2, j, :], vo[:, j, :], start=(j == 0), stop=(j == T - 1))
                    ins.then_inc(full["o"], 1)
                    if i == 0 and not first:
                        pe.wait_ge(s_xn, norm(b - 1, 2, False))
                        transposes(slot, "x3t", xns[1 - par])

                if not last:
                    x_times_u(b + 1, 1 - par, slot)
                pe.wait_ge(s_xn, norm(b, 1, last))
                transposes(slot, "x2t", xn)
                for t in range(T):
                    if t % 4 == 0:
                        o = slot()
                    if t == 0:
                        pe.wait_ge(read["x2t"], nth(b, 1))
                    r = 256 * (t % 4)
                    ins = PE.matmul(o[:, r:r + D + 2 * HEADS], xT[:, P * t:P * t + P], wext[:, :], start=True, stop=True)
                    if t % 4 == 3:
                        ins.then_inc(full["wh"], 1)

                def dst_scores(h):
                    o = slot()
                    for c in range(2):
                        ins = PE.matmul(o[:, HALF * c:HALF * c + HALF], wab[:, h, :], xT[:, HALF * c:HALF * c + HALF],
                                        start=True, stop=True)
                    ins.then_inc(full["sj"], 1)

                def head(h):
                    o = ps[:, HEAD_SLOT, :]
                    if h > 0:
                        pe.wait_ge(s_phr, nth(b, HEADS, h - 1))
                    elif not first:
                        pe.wait_ge(s_phr, b * HEADS)
                    for i in range(T):
                        if i < TP:
                            pe.wait_ge(s_ind, nth(b, HEADS * TP, TP * h + i))
                        else:
                            pe.wait_ge(s_indv, nth(b, HEADS * (T - TP), (T - TP) * h + i - TP))
                        for j in range(T):
                            for s in range(3):
                                ins = PE.matmul(o[:, P * j:P * j + 66], step[:, i, P * j:P * j + P], vs[:, i, s, h, :],
                                                start=(i == 0 and s == 0 and j % 4 == 0),
                                                stop=(i == T - 1 and s == 2 and j % 4 == 3))
                        ins.then_inc(s_used, 1)

                def neighbours(k):
                    o = slot()
                    pe.wait_ge(s_vh, nth(b, 6, 4 + k))
                    for j in range(T):
                        for i in range(T):
                            for s in range(3):
                                ins = PE.matmul(o[:, P * j:P * j + 66].rearrange("p (h c) -> p h c", h=2),
                                                adjb[par][:, i, P * j:P * j + P], vs[:, i, s, HALVES[k], 33:66],
                                                start=(i == 0 and s == 0), stop=(i == T - 1 and s == 2))
                    ins.then_inc(full["qa"], 1)

                dst_scores(0)
                if not last:
                    aggregate(b + 1, 1 - par, slot)
                for h in range(HEADS):
                    if h % 2 == 0:
                        neighbours(h // 2)
                    if h + 1 < HEADS:
                        dst_scores(h + 1)
                    head(h)

            start = ring(-1, USES_START, None)
            x_times_u(0, 0, start)
            aggregate(0, 0, start)
            graph(0, 0, before=USES_START)
            graph(1, 1, before=uses_of(first=True))
            with pe.Fori(1, G // 2 - 1) as pair:
                for par in range(2):
                    graph(pair * 2 + par, par)
            graph(G - 2, 0)
            graph(G - 1, 1, last=True)
            pe.wait_ge(s_xn, norm(G - 1, 2, True))
            transposes(lambda: ps[:, HEAD_SLOT, :], "x3t", xns[1])

        @block.scalar
        def _(act):
            act.wait_ge(s_wt, 1)
            A.copy(wt[:, :, :], ps[:, 0, 0:4 * P].rearrange("p (i d) -> p i d", i=4))
            A.copy(wext[:, 0:D], wload[:, 3, :])
            act.drain().then_inc(s_wtc, 1)
            act.wait_ge(s_wa, 1)
            A.copy(wext[:, D:D + 2 * HEADS], ps[:, 1, 0:2 * HEADS])
            act.drain()
            for h in range(HEADS):
                A.copy(wab[:, h, :], wext[:, D + HEADS + h:D + HEADS + h + 1].broadcast_to([P, P]))
            act.drain().then_inc(s_wac, 1)

            def ring(b, uses):
                at = [0]

                def slot(kind):
                    n = uses.index(kind, at[0])
                    at[0] = n + 1
                    act.wait_ge(full[kind], done(b, kind, number(uses, n)))
                    return ps[:, n % RING, :]

                return slot

            def deviation(count):
                act.wait_ge(s_var, count)
                A.activation(std[:, :], mv[:, :, 1], ACT.Sqrt, bias=eps_t[:, 0:1]).then_inc(s_std, 1)

            def normalise(count, xn):
                act.wait_ge(s_shift, count)
                for t in range(T):
                    A.activation(xn[:, t, :], xn[:, t, :], ACT.Identity, bias=shift[:, t:t + 1], scale=rden[:, t:t + 1])
                act.drain().then_inc(s_xn, 1)

            def copy_xt(b, par, slot):
                if not isinstance(b, int) or b > 1:
                    act.wait_ge(s_hT, (b - 1) * 16)
                A.copy(xTs[par][:, :], slot("xt")).then_inc(read["xt"], 1)

            def y_first(slot):
                A.copy(y3[:, 0, :, 0:D], slot("y").rearrange("p (t d) -> p t d", t=T)).then_inc(s_parts, 1)

            def y_next(b, s):
                act.wait_ge(s_yrest, nth(b, 2, s - 1))
                A.copy(y3[:, s, :, 0:D], y_rest).then_inc(s_parts, 1)

            def relu_agg(b, slot):
                for c in range(2):
                    a = slot("agg").rearrange("p (t d) -> p t d", t=4)
                    act.wait_ge(s_aggd, nth(b, 2, c))
                    for t in range(4):
                        A.activation(agg[:, 4 * c + t, :], a[:, t, 0:D], ACT.Relu, scale=odn[:, 4 * c + t:4 * c + t + 1])
                    act.drain().then_inc(read["agg"], 1)

            def graph(b, par, first_one=False, last=False):
                uses = uses_of(first_one, last)
                slot = ring(b, uses)
                xn, xT = xns[par], xTs[par]
                A.copy(xT[:, :], slot("x1t")).then_inc(read["x1t"], 1)
                A.activation(qT[:, :], slot("q"), ACT.Relu, bias=bqk[:, 0:1]).then_inc(read["q"], 1)
                A.activation(kT[:, :], slot("k"), ACT.Relu, bias=bqk[:, 1:2]).then_inc(read["k"], 1)
                A.activation(vo[:, :, 0:D], slot("v").rearrange("p (t d) -> p t d", t=T), ACT.Relu).then_inc(read["v"], 1)

                uses_of_s = [n for n, kind in enumerate(uses) if kind == "s"]

                def exponentials(i):
                    if i >= 2:
                        act.wait_ge(full["t"], nth(b, T, i - 2))
                    act.wait_ge(s_nmx, nth(b, T, i))
                    A.activation(pN[:, i % 2, :], ps[:, uses_of_s[i] % RING, :], ACT.Exp, bias=mx[:, 1, i:i + 1])\
                        .then_inc(read["s"], 1)

                if not first_one:
                    deviation(norm(b - 1, 2, False))
                exponentials(0)
                if not first_one:
                    normalise(norm(b - 1, 2, False), xns[1 - par])
                for i in range(T):
                    if i + 1 < T:
                        exponentials(i + 1)
                    if i == 1 and not first_one:
                        act.wait_ge(full["x3t"], done(b, "x3t"))
                        A.copy(xTs[1 - par][:, :], ps[:, uses.index("x3t") % RING, :]).then_inc(read["x3t"], 1)
                    if i >= 2:
                        act.wait_ge(full["o"], nth(b, T, i - 2))
                    A.copy(pT[:, i % 2, :, :], slot("t").rearrange("p (j i) -> p j i", j=T)).then_inc(read["t"], 1)
                if not last:
                    copy_xt(b + 1, 1 - par, slot)
                deviation(norm(b, 1, last))
                if not last:
                    y_first(slot)
                normalise(norm(b, 1, last), xn)
                if not last:
                    y_next(b + 1, 1)
                A.copy(xT[:, :], slot("x2t")).then_inc(read["x2t"], 1)
                if not last:
                    y_next(b + 1, 2)
                for c in range(2):
                    A.copy(wh[:, 4 * c:4 * c + 4, :],
                           slot("wh").rearrange("p (t d) -> p t d", t=4)[:, :, 0:D + 2 * HEADS]).then_inc(read["wh"], 1)
                act.drain()
                A.activation(steep[:, :, :], wh[:, :, D:D + HEADS], ACT.Copy, scale=STEEP)
                act.drain()

                def steps(h, o, tiles):
                    for i in tiles:
                        if h > 0:
                            act.wait_ge(s_used, nth(b, TILES2, T * (h - 1) + i))
                        elif not first_one:
                            act.wait_ge(s_used, b * TILES2)
                        A.activation(step[:, i, :], o, ACT.Sigmoid, bias=steep[:, i, h:h + 1], scale=STEEP).then_inc(s_step, 1)
                    if T - 1 in tiles:
                        act.drain().then_inc(read["sj"], 1)

                o = slot("sj")
                steps(0, o, range(4))
                act.wait_ge(s_sc, nth(b, 1))
                A.activation(ex[:, 0], sc[:, 0], ACT.Exp)
                A.activation(ex[:, 1], sc[:, 0], ACT.Exp, scale=SLOPE)
                A.activation(ex[:, 2], sc[:, 1], ACT.Exp, scale=1.0 - SLOPE)
                A.activation(ex[:, 3], sc[:, 2], ACT.Exp, scale=SLOPE - 1.0)
                act.drain().then_inc(s_ex, 1)
                for s in range(3):
                    steps(0, o, ((4, 5), (6,), (7,))[s])
                    for k, two in enumerate(HALVES):
                        if s == 0:
                            act.wait_ge(s_va, nth(b, 2, k))
                        else:
                            act.wait_ge(s_vb, nth(b, 4, 2 * (s - 1) + k))
                        A.copy(vs[:, :, s, two, :], va[:, :, two, :]).then_inc(s_vh, 1)
                if not last:
                    relu_agg(b + 1, slot)
                for h in range(HEADS):
                    if h % 2 == 0:
                        A.copy(qa[:, h // 2].rearrange("p t h c -> p t (h c)"),
                               slot("qa").rearrange("p (t d) -> p t d", t=T)[:, :, 0:66]).then_inc(read["qa"], 1)
                    if h + 1 < HEADS:
                        steps(h + 1, slot("sj"), range(T))
                    if h == 1 and not last:
                        deviation(norm(b, 0, last))
                    if h == 2 and not last:
                        normalise(norm(b, 0, last), xns[1 - par])

            start = ring(-1, USES_START)
            copy_xt(0, 0, start)
            y_first(start)
            y_next(0, 1)
            y_next(0, 2)
            relu_agg(0, start)
            deviation(1)
            normalise(1, xns[0])
            graph(0, 0, first_one=True)
            graph(1, 1)
            with act.Fori(1, G // 2 - 1) as pair:
                for par in range(2):
                    graph(pair * 2 + par, par)
            graph(G - 2, 0)
            graph(G - 1, 1, last=True)
            deviation(norm(G - 1, 2, True))
            normalise(norm(G - 1, 2, True), xns[1])
            act.wait_ge(full["x3t"], G)
            A.copy(xTs[1][:, :], ps[:, HEAD_SLOT, :]).then_inc(read["x3t"], 1)

        @block.vector
        def _(v):
            V.memset(keepz[:, :, :], 1.0)
            V.memset(fl[:, :], 0.0)
            v.drain()
            V.memset(keepz[:, :, 0:1], 0.0)
            v.wait_ge(s_const, 1)
            v.drain()

            def flat(t):
                return t[:, :, :].rearrange("p a b -> p (a b)")

            def spread(t):
                return t.unsqueeze(2).broadcast_to([P, QB, W32])

            def thresholds():
                V.tensor_scalar(even_up, num, 2 * MAGIC, 2 * MAGIC, ALU.add, ALU.subtract)
                V.tensor_scalar(big, num, 11.0, None, ALU.is_ge)
                V.tensor_scalar(tiny[:, :], num, 2.0, 3.0 * N, ALU.is_lt, ALU.mult)
                v.drain()
                V.scalar_tensor_tensor(first, even_up, 0.5, big, ALU.mult, ALU.mult)
                V.tensor_tensor(last, even_up, big, ALU.mult)
                v.drain()
                V.tensor_tensor(last, last, tiny[:, :], ALU.max)
                v.drain()

            def to_flag(changed):
                V.tensor_reduce(fl[:, 0:1], changed, AX.XY, ALU.max)
                v.drain()
                V.transpose(flT[:, :], fl[:, :])
                v.drain()
                for q in range(4):
                    V.tensor_copy(fl0[0:1, 32 * q:32 * q + 32], flT[32 * q:32 * q + 1, :])
                v.drain()
                V.tensor_reduce(flag[:, :], fl0[:, :], AX.X, ALU.max)
                v.drain()

            def flagged():
                return v.value_load(flag[0:1, 0:1], min_val=0, max_val=1) != 0

            def ranks(t):
                for g in range(QB):
                    V.tensor_tensor_scan(rank[:, g, :], M[:, t, g, :], M[:, t, g, :], 0.0, ALU.add, ALU.max)
                v.drain()
                V.tensor_tensor(num, rank[:, :, N - 1], bias[:, :, bass.ds(t, 1)].rearrange("p g o -> p (g o)"), ALU.add)
                v.drain()
                thresholds()

            def rank_flags():
                for g in range(QB):
                    V.tensor_scalar(rm[:, g, :], rank[:, g, :], small[:, 3, g:g + 1], None, ALU.is_equal)
                v.drain()
                for g in range(QB):
                    V.scalar_tensor_tensor(rm8[:, g, :], rank[:, g, :], small[:, 4, g:g + 1], rm[:, g, :], ALU.is_ge, ALU.max)
                v.drain()

            def removed(t):
                V.tensor_tensor(rm32[:, :, :], rm32[:, :, :], M32[:, t, :, :], ALU.bitwise_and)
                v.drain()
                V.transpose(rmT.rearrange("p g c -> p (g c)"), rm8.rearrange("p g c -> p (g c)"))
                v.drain()

            def within_window(t):
                win = bass.ds(t * W32, W32)
                ranks(t)
                V.tensor_tensor(dwin[:, :, 0], rank[:, :, bass.ds(t * W32, 1)].rearrange("p g o -> p (g o)"),
                                M[:, t, :, bass.ds(t * W32, 1)].rearrange("p g o -> p (g o)"), ALU.subtract)
                V.tensor_tensor(after, num, rank[:, :, bass.ds(t * W32 + (W32 - 1), 1)].rearrange("p g o -> p (g o)"),
                                ALU.subtract)
                V.tensor_copy(cw[:, :, :], M[:, t, :, win])
                v.drain()
                V.tensor_tensor(cu[:, :, :], cw[:, :, :], upper[:, :, :], ALU.mult)
                V.tensor_copy(dwin[:, :, 1:W32 + 1], cw[:, :, :])
                v.drain()
                V.memset(flag[:, :], 1)
                v.drain()
                with v.While(flagged):
                    V.tensor_tensor_scan(flat(rk), flat(keepz), flat(dwin), 0.0, ALU.mult, ALU.add)
                    v.drain()
                    V.tensor_tensor(num, rk[:, :, W32], after, ALU.add)
                    v.drain()
                    thresholds()
                    V.tensor_tensor(e1[:, :, :], rk[:, :, 1:W32 + 1], spread(first), ALU.is_equal)
                    V.tensor_tensor(rem[:, :, :], rk[:, :, 1:W32 + 1], spread(last), ALU.is_ge)
                    v.drain()
                    V.tensor_tensor(rem[:, :, :], rem[:, :, :], e1[:, :, :], ALU.max)
                    v.drain()
                    V.tensor_tensor(rem[:, :, :], rem[:, :, :], cu[:, :, :], ALU.mult)
                    v.drain()
                    V.transpose(flat(remT), flat(rem))
                    v.drain()
                    V.tensor_tensor(dnew[:, :, :], cw[:, :, :], remT[:, :, :], ALU.is_gt)
                    v.drain()
                    V.tensor_tensor(e1[:, :, :], dnew[:, :, :], dwin[:, :, 1:W32 + 1], ALU.not_equal)
                    v.drain()
                    V.tensor_copy(dwin[:, :, 1:W32 + 1], dnew[:, :, :])
                    to_flag(e1[:, :, :])
                V.tensor_copy(M[:, t, :, win], dwin[:, :, 1:W32 + 1])
                v.drain()
                ranks(t)
                rank_flags()
                removed(t)

            def dilation_pieces(t):
                win = bass.ds(t * W32, W32)

                def scan():
                    ranks(t)

                def remove():
                    removed(t)

                def check():
                    V.tensor_tensor(e1[:, :, :], rmT[:, :, win], lower[:, :, :], ALU.mult)
                    v.drain()
                    V.tensor_tensor(e1[:, :, :], e1[:, :, :], M[:, t, :, win], ALU.mult)
                    v.drain()
                    to_flag(e1[:, :, :])
                    with v.If(flagged()):
                        within_window(t)
                    v.drain()

                def update():
                    V.tensor_tensor(M32[:, t, :, :], M32[:, t, :, :], rm32[:, :, :], ALU.bitwise_xor)
                    v.drain()
                    for op in (0, 1):
                        for g in range(QB):
                            cols = M32[:, :, g, bass.ds(t * (W32 // 4), W32 // 4)]
                            hit = hit32[:, g, :].rearrange("p (s c) -> p s c", s=CH)
                            lost = rmT32[:, g, :].rearrange("p (s c) -> p s c", s=CH)
                            if op == 0:
                                V.tensor_tensor(hit, cols, lost, ALU.bitwise_and)
                            else:
                                V.tensor_tensor(cols, cols, hit, ALU.bitwise_xor)
                        v.drain()

                return [scan, rank_flags, remove, check, update]

            def ring(b, uses):
                at = [0]

                def slot(kind):
                    n = uses.index(kind, at[0])
                    at[0] = n + 1
                    v.wait_ge(full[kind], done(b, kind, number(uses, n)))
                    return ps[:, n % RING, :]

                return slot

            def moments(xn):
                v.drain()
                for t in range(T):
                    V.bn_stats(stats[:, t, :], xn[:, t, :])
                v.drain()
                for t in range(T):
                    V.bn_aggr(mv[:, t, :], stats[:, t, :])
                v.drain().then_inc(s_var, 1)

            def scale_and_shift(count):
                v.wait_ge(s_std, count)
                V.reciprocal(rden[:, :], std[:, :])
                v.drain()
                V.scalar_tensor_tensor(shift[:, :], mv[:, :, 0], -1.0, rden[:, :], ALU.mult, ALU.mult)
                v.drain().then_inc(s_shift, 1)

            def y_parts(b, slot):
                y = slot("y").rearrange("p (t d) -> p t d", t=T)
                V.memset(y3[:, 0, :, D:D + 1], 1.0)
                v.wait_ge(s_parts, nth(b, 3, 0))
                V.tensor_tensor(y_rest, y, y3[:, 0, :, 0:D], ALU.subtract).then_inc(read["y"], 1)
                v.drain().then_inc(s_yrest, 1)
                v.wait_ge(s_parts, nth(b, 3, 1))
                V.tensor_tensor(y_rest, y_rest, y3[:, 1, :, 0:D], ALU.subtract)
                v.drain().then_inc(s_yrest, 1)

            def degrees(slot, c):
                a = slot("agg").rearrange("p (t d) -> p t d", t=4)
                V.reciprocal(odn[:, 4 * c:4 * c + 4], a[:, :, D]).then_inc(s_aggd, 1)

            def add_aggregate(b, xn):
                v.wait_ge(read["agg"], nth(b, 2, 1))
                V.tensor_tensor(xn[:, :, :], xn[:, :, :], agg, ALU.add)

            def graph(b, par, t0, plan=PLAN, first=False, last=False):
                pieces = [p for s in range(4) for p in dilation_pieces(t0 + s)]
                uses = uses_of(first, last)
                slot = ring(b, uses)
                xn = xns[par]
                points = list(plan)

                def fill():
                    n = points.pop(0)
                    if n and plan == PLAN_LATE and len(pieces) == 20:
                        start_half(1)
                    for _ in range(n):
                        pieces.pop(0)()

                fill()
                if not first:
                    scale_and_shift(norm(b - 1, 2, False))
                fill()

                def row_max(i):
                    V.reduce_max(mx[:, 0, i:i + 1], slot("s"), AX.X)
                    v.drain()
                    V.tensor_scalar(mx[:, 1, i:i + 1], mx[:, 0, i:i + 1], CLAMP, -1.0, ALU.min, ALU.mult).then_inc(s_nmx, 1)

                uses_of_o = [n for n, kind in enumerate(uses) if kind == "o"]

                def add_attended(i):
                    v.wait_ge(full["o"], done(b, "o", i))
                    o = ps[:, uses_of_o[i] % RING, :]
                    V.reciprocal(cden[:, i:i + 1], o[:, D:D + 1])
                    v.drain()
                    V.scalar_tensor_tensor(xn[:, i, :], o[:, 0:D], cden[:, i:i + 1], xn[:, i, :], ALU.mult, ALU.add)\
                        .then_inc(read["o"], 1)

                row_max(0)
                row_max(1)
                fill()
                for i in range(T):
                    if i + 2 < T:
                        row_max(i + 2)
                    if i % 2:
                        fill()
                    add_attended(i)
                moments(xn)
                scale_and_shift(norm(b, 1, last))
                if not last:
                    y_parts(b + 1, slot)
                fill()

                v.wait_ge(read["wh"], nth(b, cn["wh"], 1))
                V.tensor_reduce(smax[:, :], wh[:, :, D:D + HEADS].rearrange("p t h -> p h t"), AX.X, ALU.max)
                v.drain().then_inc(s_smax, 1)
                fill()
                v.wait_ge(s_gmax, nth(b, 1))
                top = gmax[:, :].unsqueeze(1).broadcast_to([P, T, HEADS])
                V.tensor_tensor(sc[:, 0], wh[:, :, D:D + HEADS], top, ALU.subtract)
                V.tensor_tensor(sc[:, 2], wh[:, :, D + HEADS:D + 2 * HEADS], top, ALU.add)
                v.drain()
                V.tensor_scalar(sc[:, 1], sc[:, 2], 0.0, None, ALU.min)
                v.drain()
                V.tensor_scalar(sc[:, 2], sc[:, 2], 0.0, None, ALU.max)
                v.drain().then_inc(s_sc, 1)
                v.wait_ge(s_ex, nth(b, 1))
                whh = wh[:, :, 0:D].rearrange("p t (h c) -> p t h c", h=HEADS)
                for two in HALVES:
                    for e in range(2):
                        V.tensor_tensor(va[:, :, two, 33 * e:33 * e + DH], whh[:, :, two, :],
                                        ex[:, e, :, two].unsqueeze(3).broadcast_to([P, T, HEADS // 2, DH]), ALU.mult)
                        V.tensor_copy(va[:, :, two, 33 * e + DH], ex[:, e, :, two])
                    v.drain().then_inc(s_va, 1)
                for s in range(2):
                    for k, two in enumerate(HALVES):
                        v.wait_ge(s_vh, nth(b, 6, 2 * s + k))
                        V.tensor_tensor(va[:, :, two, :], va[:, :, two, :], vs[:, :, s, two, :], ALU.subtract)
                        v.drain().then_inc(s_vb, 1)

                def mask(h):
                    for i in range(TP, T):
                        v.wait_ge(s_step, nth(b, TILES2, T * h + i))
                        V.tensor_tensor(step[:, i, :], step[:, i, :], adjb[par][:, i, :], ALU.mult).then_inc(s_indv, 1)

                def combine(h):
                    v.wait_ge(s_used, nth(b, TILES2, T * h + T - 1))
                    o = ps[:, HEAD_SLOT, :].rearrange("p (t d) -> p t d", t=T)
                    v.wait_ge(read["qa"], done(b, "qa", h // 2))
                    V.tensor_tensor(comb[:, 1], qa[:, h // 2, :, h % 2, :], o[:, :, 33:66], ALU.subtract)
                    V.tensor_tensor(comb[:, 0], o[:, :, 0:33], ex[:, 2, :, h].unsqueeze(2).broadcast_to([P, T, 33]), ALU.mult)
                    v.drain().then_inc(s_phr, 1)
                    V.tensor_tensor(comb[:, 1], comb[:, 1], ex[:, 3, :, h].unsqueeze(2).broadcast_to([P, T, 33]), ALU.mult)
                    v.drain()
                    V.tensor_tensor(comb[:, 0], comb[:, 0], comb[:, 1], ALU.add)
                    v.drain()
                    V.reciprocal(cden[:, :], comb[:, 0, :, DH])
                    v.drain()
                    V.tensor_tensor(comb[:, 0, :, 0:DH], comb[:, 0, :, 0:DH],
                                    cden[:, :].unsqueeze(2).broadcast_to([P, T, DH]), ALU.mult)
                    v.drain()
                    V.tensor_tensor(xn[:, :, DH * h:DH * h + DH], xn[:, :, DH * h:DH * h + DH], comb[:, 0, :, 0:DH], ALU.add)

                if not last:
                    for c in range(2):
                        degrees(slot, c)
                        fill()
                for h in range(HEADS):
                    mask(h)
                    if h == 1 and not last:
                        add_aggregate(b + 1, xns[1 - par])
                        moments(xns[1 - par])
                    fill()
                    combine(h)
                    if h == 1 and not last:
                        scale_and_shift(norm(b, 0, last))
                v.drain()
                moments(xn)
                assert not pieces and not points

            def start_half(half):
                v.wait_ge(s_M, 16 * GROUP * (half + 1))
                v.wait_ge(s_mrow, 16 * GROUP * (half + 1))
                V.tensor_scalar(bias[:, :, :], mrow_i[:, :, :], 0.0, -1.0e5, ALU.is_equal, ALU.mult)
                v.drain()
                V.tensor_scalar(bias[:, :, :], bias[:, :, :], 0.5, None, ALU.add)
                v.drain()

            V.memset(vo[:, :, D:D + 1], 1.0)
            v.wait_ge(s_w, 16 * 18)
            for s in range(3):
                V.tensor_copy(bv16[:, s, :], bvrow)
                v.drain()
                V.tensor_copy(bv3[32 * s:32 * s + 1, :], bv16[32 * s:32 * s + 1, s, :])
                V.tensor_tensor(bvrow, bvrow, bv16[:, s, :], ALU.subtract)
                v.drain()
            start = ring(-1, USES_START)
            y_parts(0, start)
            for c in range(2):
                degrees(start, c)
            add_aggregate(0, xns[0])
            moments(xns[0])
            scale_and_shift(1)
            start_half(0)
            graph(0, 0, 0, first=True)
            graph(1, 1, 4)
            with v.Fori(1, G // 4) as pair:
                for par in range(2):
                    graph(pair * 2 + par, par, pair * 8 + 4 * par)
            v.drain().then_inc(s_dil, 1)
            graph(GROUP, 0, 0, plan=PLAN_LATE)
            graph(GROUP + 1, 1, 4)
            with v.Fori(1, G // 4 - 1) as pair:
                for par in range(2):
                    graph(pair * 2 + (GROUP + par), par, pair * 8 + 4 * par)
            graph(G - 2, 0, CH - 8)
            graph(G - 1, 1, CH - 4, plan=PLAN_LAST, last=True)
            scale_and_shift(norm(G - 1, 2, True))
            v.drain().then_inc(s_dil, 1)


def layer_3(nc, S):
    f32, bf16, u8, i32 = mybir.dt.float32, mybir.dt.bfloat16, mybir.dt.uint8, mybir.dt.int32
    ALU, ACT, AX = mybir.AluOpType, mybir.ActivationFunctionType, mybir.AxisListType
    V, A, PE, GP = nc.vector, nc.scalar, nc.tensor, nc.gpsimd
    mask_tiles, blocks, Wl, bl = S.inputs_3
    ident, ident16, row0, ones3, eps_t = S.ident, S.ident16, S.row0, S.ones3, S.eps_t
    L = len(blocks)

    ctx = ExitStack()
    with ctx:
        def sb(name, shape, dt):
            return ctx.enter_context(nc.sbuf_tensor(name, shape, dt))

        def sem(name):
            return ctx.enter_context(nc.semaphore(name))

        wrx = sb("wrx", [P, L, 2 * D], f32)
        wrx_s = sb("wrx_s", [P, 2 * D], f32)
        wl = sb("wl", [P, L, D], f32)
        wl_s = sb("wl_s", [P, L, D], f32)
        brow = sb("brow", [P, L + 1, 2 * D], f32)
        gb = sb("gb", [P, L, 2], f32)
        crow = sb("crow", [P, 2 * D], f32)
        blrow = sb("blrow", [P, D], f32)
        mask_i = sb("mask_i", [P, G, T], i32)
        mf = sb("mf", [P, G, T], f32)
        ad = [sb(f"ad{i}", [P, T, N], bf16) for i in range(2)]
        adt = [sb(f"adt{i}", [P, T, N], bf16) for i in range(2)]
        hin = [sb(f"hin{i}", [P, L, N], f32) for i in range(2)]
        hout = [sb(f"hout{i}", [P, N], f32) for i in range(2)]
        rest = sb("rest3", [P, T, D], f32)
        z = [sb(f"z{i}", [P, T, D], f32) for i in range(2)]
        junk = sb("junk", [P, N], f32)
        y3 = [sb(f"y3{i}", [P, 3, T, D + 1], bf16) for i in range(2)]
        crow3 = sb("crow3", [P, 2 * D], bf16)
        crow16 = sb("crow16", [P, 3, 2 * D], bf16)
        mcol = sb("mcol", [P, T], f32)
        shift = sb("shift3", [P, T], f32)
        rden = sb("rden3", [P, T], f32)
        ss = sb("ss", [P, T], f32)
        nrm = sb("nrm", [P, T], f32)
        sums = sb("sums", [P, 2, 2 * G], f32)
        bn = sb("bn", [P, 8], f32)
        betas = sb("betas", [P, L, P], f32)
        x3 = [sb(f"x3{i}", [P, T, D], f32) for i in range(2)]
        xo = [sb(f"xo{i}", [P, T, D], f32) for i in range(2)]
        stats = sb("stats3", [P, T, 6], f32)
        mv = sb("mv3", [P, T, 2], f32)
        std = sb("std3", [P, T], f32)
        ps = ctx.enter_context(nc.psum_tensor("ps3", [P, 4 * N], f32))
        GROUPS = 3
        RT_AT = 7 * HALF

        def agg_at(i):
            return HALF * (4 + i // 3) + (D + 1) * (i % 3)

        def yz(c):
            return ps[:, N * c:N * c + N].rearrange("p (t d) -> p t d", t=4)

        full = {k: sem(f"sage_{k}_in_psum") for k in ("adt", "yz", "agg", "rt")}
        s_adt_a = sem("adt_copied_by_scalar")
        s_adt_v = sem("adt_copied_by_vector")
        read_yz_a = sem("z_read")
        read_yz_v = sem("y_read")
        read_agg = sem("aggregate_read")
        read_rt = sem("r_read")
        s_w = sem("first_block_weights_loaded")
        s_w_later = sem("later_weights_loaded")
        s_ad = [sem(f"dilated{i}_loaded") for i in range(2)]
        s_adt = [sem(f"adt{i}_loaded") for i in range(2)]
        s_adts = [sem(f"adt{i}_stored") for i in range(2)]
        s_hin = [sem(f"h{i}_loaded") for i in range(2)]
        s_hs = [sem(f"h{i}_stored") for i in range(2)]
        s_y0 = sem("y_part_0_ready")
        s_y1 = sem("y_part_1_ready")
        s_y2 = sem("y_part_2_ready")
        s_rest = sem("y_rest_ready")
        s_z = sem("z_ready")
        s_nrm = sem("norms_ready")
        s_r = sem("r_ready")
        s_bnv = sem("bn_variance_ready")
        s_bns = sem("bn_std_ready")
        s_beta = sem("beta_ready")
        s_crow = sem("crow_in_psum")
        s_crowc = sem("crow_copied")
        s_pin = [sem(f"final{i}_loaded") for i in range(2)]
        s_pp = sem("projection_in_psum")
        s_pr = sem("projection_read")
        s_var = sem("final_variance_ready")
        s_std = sem("final_std_ready")
        s_read = sem("x3_read")
        s_shift = sem("final_shift_ready")
        s_out = sem("out_ready")
        s_st = [sem(f"out{i}_stored") for i in range(2)]

        def nth(g, count, i=0):
            return g * count + (i + 1)

        def even(g, par):
            return g * 8 + (16 - 8 * par)

        def each_graph(eng, body):
            body(0, 0, True)
            body(1, 1, True)
            with eng.Fori(1, G // 2) as pair:
                for par in range(2):
                    body(pair * 2 + par, par, False)

        def pipelined(eng, body):
            body(0, 0, start=True)
            body(1, 1)
            with eng.Fori(1, G // 2 - 1) as pair:
                for par in range(2):
                    body(pair * 2 + par, par)
            body(G - 2, 0)
            body(G - 1, 1, last=True)

        def adt_tiles(eng, copy, b, par, which, done):
            if not (isinstance(b, int) and b < 2):
                eng.wait_ge(s_adts[par], even(b - 2, par))
                eng.wait_ge(full["agg"], (b - 1) * GROUPS)
            for j in range(which, T, 2):
                eng.wait_ge(full["adt"], nth(b, T, j))
                copy(adt[par][:, j, :], ps[:, N * which:N * which + N]).then_inc(done, 1)

        block = ctx.enter_context(nc.Block())

        @block.sync
        def _(sp):
            def load_block(l, done):
                Wr, Wx, b, g, be = blocks[l]
                sp.dma_start(wrx[:, l, 0:D], Wr).then_inc(done, 16)
                sp.dma_start(wrx[:, l, D:2 * D], Wx).then_inc(done, 16)
                sp.dma_start(brow[0:1, l, D:2 * D], b.rearrange("(o d) -> o d", o=1)).then_inc(done, 16)

            sp.wait_ge(S.zeroed, 1)
            load_block(0, s_w)
            sp.dma_start(mask_i[:, :, :], mask_tiles).then_inc(s_w, 16)
            for l in range(1, L):
                load_block(l, s_w_later)
            for l, (Wr, Wx, b, g, be) in enumerate(blocks):
                sp.dma_start(wl[:, l, :], Wl[D * l:D * l + D, :]).then_inc(s_w_later, 16)
                sp.dma_start(gb[:, l, 0:1], g.rearrange("(d o) -> d o", o=1)).then_inc(s_w_later, 16)
                sp.dma_start(gb[:, l, 1:2], be.rearrange("(d o) -> d o", o=1)).then_inc(s_w_later, 16)
            sp.dma_start(brow[0:1, L, 0:D], bl.rearrange("(o d) -> o d", o=1)).then_inc(s_w_later, 16)

            for l in range(L):
                def store(b, par, peeled):
                    g = b + l * G
                    if l == 0:
                        sp.wait_ge(s_adt_a, nth(g, T // 2, T // 2 - 1))
                        sp.wait_ge(s_adt_v, nth(g, T // 2, T // 2 - 1))
                        sp.dma_start(S.adt_dram[b], adt[par][:, :, :]).then_inc(s_adts[par], 16)
                    sp.wait_ge(read_rt, nth(g, 2, 1))
                    sp.dma_start(S.h_dram[l + 1, b], hout[par][:, :]).then_inc(s_hs[par], 16)

                each_graph(sp, store)

            def final(b, par, peeled):
                if not peeled:
                    sp.wait_ge(s_pp, b - 1)
                    sp.wait_ge(s_read, b - 1)
                else:
                    sp.wait_ge(s_hs[par], even(L * G - 2 + par, par))
                    sp.wait_ge(full["yz"], L * G * 2)
                for l in range(L):
                    sp.dma_start(hin[par][:, l, :], S.h_dram[l + 1, b]).then_inc(s_pin[par], 16)
                sp.dma_start(x3[par][:, :, :], S.x3_dram[b].rearrange("(t p) d -> p t d", p=P)).then_inc(s_pin[par], 16)
                if not peeled:
                    final_store(b - 2, par)

            def final_store(b, par):
                sp.wait_ge(s_out, nth(b, 1))
                sp.dma_start(S.out[b].rearrange("(t p) d -> p t d", p=P), xo[par][:, :, :]).then_inc(s_st[par], 16)

            each_graph(sp, final)
            for par in range(2):
                final_store(G - 2 + par, par)
            for par in range(2):
                sp.wait_ge(s_st[par], 8 * G)

        @block.gpsimd
        def _(gp):
            GP.memset(brow[:, :, :], 0.0)
            GP.memset(crow3[:, :], 0.0)
            gp.drain().then_inc(S.zeroed, 1)

            def load_h(l, b, par, peeled):
                g = b + l * G
                if l > 0:
                    gp.wait_ge(s_hs[par], even(g - G, par))
                if l > 0 or not peeled:
                    gp.wait_ge(full["yz"], (g - 1) * 2)
                gp.dma_start(hin[par][:, 0, :], S.h_dram[l, b]).then_inc(s_hin[par], 16)

            def graph(b, par, peeled):
                load_h(0, b, par, peeled)
                if not peeled:
                    gp.wait_ge(full["adt"], (b - 1) * T)
                gp.dma_start(ad[par][:, :, :], S.dilated[b].rearrange("(t p) c -> p t c", p=P)).then_inc(s_ad[par], 16)

            each_graph(gp, graph)
            for l in range(1, L):
                def later(b, par, peeled):
                    load_h(l, b, par, peeled)
                    gp.wait_ge(full["agg"], (b + (l * G - 1)) * GROUPS)
                    gp.dma_start(adt[par][:, :, :], S.adt_dram[b]).then_inc(s_adt[par], 16)

                if l == 1:
                    for par in range(2):
                        gp.wait_ge(s_adts[par], 8 * G)
                each_graph(gp, later)

        @block.tensor
        def _(pe):
            pe.wait_ge(s_w, 16 * 4)
            pe.wait_ge(S.zeroed, 1)
            PE.matmul(ps[:, 0:2 * D], row0[:, :], brow[:, 0, :], start=True, stop=True).then_inc(s_crow, 1)
            pe.wait_ge(s_crowc, 1)

            for l in range(L):
                def transpose_adj(b, par):
                    if l == 0:
                        pe.wait_ge(s_ad[par], even(b, par))
                        for j in range(T):
                            if j >= 2:
                                pe.wait_ge((s_adt_a, s_adt_v)[j % 2], nth(b, T // 2, j // 2 - 1))
                            else:
                                pe.wait_ge(read_yz_a, nth(b, 2, j))
                                pe.wait_ge(read_yz_v, nth(b, 2, j))
                            for i in range(T):
                                ins = PE.matmul(ps[:, (j % 2) * N + P * i:(j % 2) * N + P * i + P],
                                                ad[par][:, i, P * j:P * j + P], ident16[:, :], start=True, stop=True)
                            ins.then_inc(full["adt"], 1)

                def transform(b, par, start):
                    g = b + l * G
                    pe.wait_ge(s_hin[par], even(g, par))
                    w = wrx[:, 0, :] if l == 0 else wrx_s[:, :]
                    for c in range(2):
                        if l == 0:
                            if not start:
                                pe.wait_ge((s_adt_a, s_adt_v)[c], nth(b - 1, T // 2, T // 2 - 1))
                        else:
                            pe.wait_ge(read_yz_a, nth(g - 1, 2, c))
                            pe.wait_ge(read_yz_v, nth(g - 1, 2, c))
                        for t in range(4 * c, 4 * c + 4):
                            o = ps[:, 2 * D * t:2 * D * t + 2 * D]
                            PE.matmul(o, hin[par][:, 0, P * t:P * t + P], w, start=True, stop=False)
                            ins = PE.matmul(o, ones3[:, :], crow3[:, :], start=False, stop=True)
                        ins.then_inc(full["yz"], 1)

                def transpose_half(b, par, half):
                    g = b + l * G
                    pe.wait_ge(s_r, nth(g, 1))
                    if half == 1:
                        pe.wait_ge(read_rt, nth(g, 2, 0))
                    elif not (l == 0 and isinstance(b, int) and b == 0):
                        pe.wait_ge(read_rt, g * 2)
                    for t in range(4):
                        ins = PE.transpose(ps[:, RT_AT + P * t:RT_AT + P * t + P], z[par][:, 4 * half + t, :], ident[:, :])
                    ins.then_inc(full["rt"], 1)

                def aggregate(b, par, tiles, start):
                    g = b + l * G
                    for i in tiles:
                        if i == 0:
                            pe.wait_ge(s_y2, nth(g, 1))
                            if l == 0:
                                pe.wait_ge(s_adt_a, nth(b, T // 2, T // 2 - 1))
                                pe.wait_ge(s_adt_v, nth(b, T // 2, T // 2 - 1))
                            else:
                                pe.wait_ge(s_adt[par], even(b + (l - 1) * G, par))
                        if i % 3 == 0 and not (l == 0 and start):
                            pe.wait_ge(read_agg, nth(g - 1, GROUPS, i // 3))
                        r = agg_at(i)
                        for j in range(T):
                            wj = adt[par][:, j, P * i:P * i + P]
                            PE.matmul(ps[:, r:r + 129], wj, y3[par][:, 0, j, :], start=(j == 0), stop=False)
                            PE.matmul(ps[:, r:r + 128], wj, y3[par][:, 1, j, 0:D], start=False, stop=False)
                            ins = PE.matmul(ps[:, r:r + 128], wj, y3[par][:, 2, j, 0:D], start=False, stop=(j == T - 1))
                        if i % 3 == 2 or i == T - 1:
                            ins.then_inc(full["agg"], 1)

                def graph(b, par, start=False, last=False):
                    if not last:
                        transform(b + 1, 1 - par, False)
                    for k in range(GROUPS):
                        aggregate(b, par, range(3 * k, min(3 * k + 3, T)), start)
                        if k < 2 and not start:
                            transpose_half(b - 1, 1 - par, k)
                    if not last:
                        transpose_adj(b + 1, 1 - par)

                transform(0, 0, True)
                transpose_adj(0, 0)
                pipelined(pe, graph)
                for half in range(2):
                    transpose_half(G - 1, 1, half)
                pe.wait_ge(s_beta, l + 1)
                pe.wait_ge(s_w_later, 16 * (3 * (L - 1) + 3 * L + 1))
                if l < L - 1:
                    PE.matmul(ps[:, 0:2 * D], betas[:, l, :], wrx[:, l + 1, :], start=True, stop=False)
                    PE.matmul(ps[:, 0:2 * D], row0[:, :], brow[:, l + 1, :], start=False, stop=True).then_inc(s_crow, 1)
                else:
                    for m in range(L):
                        PE.matmul(ps[:, 0:D], betas[:, m, :], wl[:, m, :], start=(m == 0), stop=(m == L - 1))
                    PE.matmul(ps[:, N:N + D], row0[:, :], brow[:, L, 0:D], start=True, stop=True).then_inc(s_crow, 1)
                pe.wait_ge(s_crowc, l + 2)

            def final(b, par, peeled):
                pe.wait_ge(s_pin[par], even(b, par) * (L + 1))
                if not peeled:
                    pe.wait_ge(s_pr, b - 1)
                for t in range(T):
                    o = ps[:, N * par + P * t:N * par + P * t + P]
                    for l in range(L):
                        PE.matmul(o, hin[par][:, l, P * t:P * t + P], wl_s[:, l, :], start=(l == 0), stop=False)
                    ins = PE.matmul(o, ones3[:, :], crow3[:, 0:D], start=False, stop=True)
                ins.then_inc(s_pp, 1)

            each_graph(pe, final)

        @block.scalar
        def _(act):
            for l in range(L):
                def rounded(b, par, start):
                    g = b + l * G
                    if not (l == 0 and isinstance(b, int) and b < 2):
                        act.wait_ge(full["agg"], (g - 1) * GROUPS)
                    for c in range(2):
                        act.wait_ge(full["yz"], nth(g, 2, c))
                        A.copy(y3[par][:, 0, 4 * c:4 * c + 4, 0:D], yz(c)[:, :, 0:D]).then_inc(s_y0, 1)

                def other_parts(b, par):
                    g = b + l * G
                    act.wait_ge(s_rest, nth(g, 2, 0))
                    A.copy(y3[par][:, 1, :, 0:D], rest[:, :, :]).then_inc(s_y1, 1)
                    act.wait_ge(s_rest, nth(g, 2, 1))
                    A.copy(y3[par][:, 2, :, 0:D], rest[:, :, :]).then_inc(s_y2, 1)

                def evacuated(b, par):
                    g = b + l * G
                    for c in range(2):
                        act.wait_ge(read_yz_v, nth(g, 2, c))
                        A.copy(z[par][:, 4 * c:4 * c + 4, :], yz(c)[:, :, D:2 * D]).then_inc(read_yz_a, 1)
                    if l == 0:
                        adt_tiles(act, A.copy, b, par, 0, s_adt_a)

                def h_half(b, par, half, start=False):
                    g = b + l * G
                    if half == 0 and not (l == 0 and start):
                        act.wait_ge(s_hs[par], even(g - 2, par))
                    act.wait_ge(full["rt"], nth(g, 2, half))
                    o = ps[:, RT_AT:RT_AT + HALF]
                    at = bass.ds(b * 2 + half, 1)
                    A.activation(hout[par][:, HALF * half:HALF * half + HALF], o, ACT.Copy, accum_out=sums[:, 0, at])
                    A.activation(junk[:, 0:HALF], o, ACT.Square, accum_out=sums[:, 1, at])
                    act.drain().then_inc(read_rt, 1)

                def norms(b, par):
                    g = b + l * G
                    act.wait_ge(s_z, nth(g, 1))
                    for t in range(T):
                        A.activation(junk[:, P * t:P * t + P], z[par][:, t, :], ACT.Square, accum_out=ss[:, t:t + 1])
                    act.drain()
                    A.activation(nrm[:, :], ss[:, :], ACT.Sqrt).then_inc(s_nrm, 1)

                def graph(b, par, start=False, last=False):
                    if not last:
                        rounded(b + 1, 1 - par, False)
                        other_parts(b + 1, 1 - par)
                    if not start:
                        h_half(b - 1, 1 - par, 0, start=isinstance(b, int) and b < 3)
                        h_half(b - 1, 1 - par, 1)
                    if not last:
                        evacuated(b + 1, 1 - par)
                    norms(b, par)

                rounded(0, 0, True)
                other_parts(0, 0)
                evacuated(0, 0)
                pipelined(act, graph)
                for half in range(2):
                    h_half(G - 1, 1, half)
                act.wait_ge(s_bnv, l + 1)
                A.activation(bn[:, 3:4], bn[:, 2:3], ACT.Sqrt, bias=eps_t[:, 0:1]).then_inc(s_bns, 1)

            def final(b, par, peeled):
                act.wait_ge(s_var, nth(b, 1))
                A.activation(std[:, :], mv[:, :, 1], ACT.Sqrt, bias=eps_t[:, 0:1]).then_inc(s_std, 1)
                act.wait_ge(s_shift, nth(b, 1))
                for t in range(T):
                    A.activation(xo[par][:, t, :], xo[par][:, t, :], ACT.Identity, bias=shift[:, t:t + 1],
                                 scale=rden[:, t:t + 1])
                act.drain().then_inc(s_out, 1)

            each_graph(act, final)

        @block.vector
        def _(v):
            for par in range(2):
                V.memset(y3[par][:, 0, :, D:D + 1], 1.0)
            v.wait_ge(s_w, 16 * 4)
            V.tensor_copy(mf[:, :, :], mask_i[:, :, :])

            def crow_parts(n, count):
                v.wait_ge(s_crow, count)
                for s in range(3):
                    o = ps[:, 0:n] if s == 0 else crow[:, 0:n]
                    V.tensor_copy(crow16[:, s, 0:n], o)
                    v.drain()
                    V.tensor_copy(crow3[32 * s:32 * s + 1, 0:n], crow16[32 * s:32 * s + 1, s, 0:n])
                    if s < 2:
                        V.tensor_tensor(crow[:, 0:n], o, crow16[:, s, 0:n], ALU.subtract)
                    v.drain()

            v.wait_ge(S.zeroed, 1)
            crow_parts(2 * D, 1)
            v.sem_inc(s_crowc, 1)

            for l in range(L):
                def remainders(b, par, start):
                    g = b + l * G
                    if not (l == 0 and start):
                        v.wait_ge(s_y2, g)
                    for c in range(2):
                        v.wait_ge(s_y0, nth(g, 2, c))
                        V.tensor_tensor(rest[:, 4 * c:4 * c + 4, :], yz(c)[:, :, 0:D], y3[par][:, 0, 4 * c:4 * c + 4, 0:D],
                                        ALU.subtract).then_inc(read_yz_v, 1)
                    v.drain().then_inc(s_rest, 1)
                    v.wait_ge(s_y1, nth(g, 1))
                    V.tensor_tensor(rest[:, :, :], rest[:, :, :], y3[par][:, 1, :, 0:D], ALU.subtract)
                    v.drain().then_inc(s_rest, 1)

                def graph(b, par, start=False, last=False):
                    g = b + l * G
                    if not last:
                        remainders(b + 1, 1 - par, False)
                    v.wait_ge(read_yz_a, nth(g, 2, 1))
                    for k in range(GROUPS):
                        tiles = range(3 * k, min(3 * k + 3, T))
                        v.wait_ge(full["agg"], nth(g, GROUPS, k))
                        deg = ps[:, agg_at(3 * k):agg_at(3 * k) + 129 * len(tiles)].rearrange("p (t d) -> p t d", d=129)
                        some = rden[:, tiles[0]:tiles[-1] + 1]
                        V.tensor_scalar(some, deg[:, :, D], 1.0, None, ALU.max)
                        v.drain()
                        V.reciprocal(some, some)
                        v.drain()
                        for t in tiles:
                            V.scalar_tensor_tensor(z[par][:, t, :], ps[:, agg_at(t):agg_at(t) + D], rden[:, t:t + 1],
                                                   z[par][:, t, :], ALU.mult, ALU.add)
                        v.drain().then_inc(read_agg, 1)
                    v.sem_inc(s_z, 1)
                    if l == 0 and not last:
                        adt_tiles(v, V.tensor_copy, b + 1, 1 - par, 1, s_adt_v)
                    v.wait_ge(s_nrm, nth(g, 1))
                    V.tensor_scalar(nrm[:, :], nrm[:, :], 1e-12, None, ALU.max)
                    v.drain()
                    V.reciprocal(nrm[:, :], nrm[:, :])
                    v.drain()
                    V.tensor_tensor(nrm[:, :], nrm[:, :], mf[:, bass.ds(b, 1), :].rearrange("p o t -> p (o t)"), ALU.mult)
                    v.drain()
                    for t in range(T):
                        V.tensor_scalar(z[par][:, t, :], z[par][:, t, :], nrm[:, t:t + 1], 0.0, ALU.mult, ALU.max)
                    v.drain().then_inc(s_r, 1)

                remainders(0, 0, True)
                if l == 0:
                    adt_tiles(v, V.tensor_copy, 0, 0, 1, s_adt_v)
                pipelined(v, graph)
                v.wait_ge(s_w_later, 16 * (3 * (L - 1) + 3 * L + 1))
                v.wait_ge(read_rt, (l + 1) * G * 2)
                V.tensor_reduce(bn[:, 0:2], sums[:, :, :], AX.X, ALU.add)
                v.drain()
                V.tensor_scalar(bn[:, 0:2], bn[:, 0:2], 1.0 / (G * N), None, ALU.mult)
                v.drain()
                V.tensor_tensor(bn[:, 4:5], bn[:, 0:1], bn[:, 0:1], ALU.mult)
                v.drain()
                V.tensor_tensor(bn[:, 2:3], bn[:, 1:2], bn[:, 4:5], ALU.subtract)
                v.drain().then_inc(s_bnv, 1)
                v.wait_ge(s_bns, l + 1)
                V.reciprocal(bn[:, 5:6], bn[:, 3:4])
                v.drain()
                V.tensor_tensor(bn[:, 5:6], bn[:, 5:6], gb[:, l, 0:1], ALU.mult)
                v.drain()
                V.tensor_tensor(bn[:, 6:7], bn[:, 0:1], bn[:, 5:6], ALU.mult)
                v.drain()
                V.tensor_tensor(bn[:, 6:7], gb[:, l, 1:2], bn[:, 6:7], ALU.subtract)
                v.drain()
                V.tensor_copy(betas[:, l, :], bn[:, 6:7].broadcast_to([P, P]))
                V.tensor_scalar(wl_s[:, l, :], wl[:, l, :], bn[:, 5:6], None, ALU.mult)
                if l < L - 1:
                    V.tensor_scalar(wrx_s[:, :], wrx[:, l + 1, :], bn[:, 5:6], None, ALU.mult)
                v.drain().then_inc(s_beta, 1)
                crow_parts(2 * D if l < L - 1 else D, l + 2)
                if l == L - 1:
                    V.tensor_copy(blrow[:, :], ps[:, N:N + D])
                v.drain().then_inc(s_crowc, 1)

            def final(b, par, peeled):
                xf = xo[par]
                V.tensor_copy(mcol[:, :], mf[:, bass.ds(b, 1), :].rearrange("p o t -> p (o t)"))
                v.drain()
                if not peeled:
                    v.wait_ge(s_st[par], even(b - 2, par))
                v.wait_ge(s_pp, nth(b, 1))
                v.wait_ge(s_pin[par], even(b, par) * (L + 1))
                for t in range(T):
                    V.scalar_tensor_tensor(xf[:, t, :], ps[:, N * par + P * t:N * par + P * t + P], mcol[:, t:t + 1],
                                           blrow[:, :], ALU.mult, ALU.add)
                v.drain().then_inc(s_pr, 1)
                for t in range(T):
                    V.scalar_tensor_tensor(xf[:, t, :], xf[:, t, :], mcol[:, t:t + 1], x3[par][:, t, :], ALU.mult, ALU.add)
                v.drain().then_inc(s_read, 1)
                for t in range(T):
                    V.bn_stats(stats[:, t, :], xf[:, t, :])
                v.drain()
                for t in range(T):
                    V.bn_aggr(mv[:, t, :], stats[:, t, :])
                v.drain().then_inc(s_var, 1)
                v.wait_ge(s_std, nth(b, 1))
                if not (isinstance(b, int) and b == 0):
                    v.wait_ge(s_out, b)
                V.reciprocal(rden[:, :], std[:, :])
                v.drain()
                V.scalar_tensor_tensor(shift[:, :], mv[:, :, 0], -1.0, rden[:, :], ALU.mult, ALU.mult)
                v.drain().then_inc(s_shift, 1)

            each_graph(v, final)


def build(nc, S):
    f32, bf16, u8 = mybir.dt.float32, mybir.dt.bfloat16, mybir.dt.uint8
    S.dilated = nc.dram_tensor("dilated", [G, N, N], u8, kind="Internal").ap()
    S.adt_dram = nc.dram_tensor("adt_dram", [G, P, T, N], bf16, kind="Internal").ap()
    S.x3_dram = nc.dram_tensor("x3_dram", [G, N, D], f32, kind="Internal").ap()
    S.h_dram = nc.dram_tensor("h_dram", [4, G, D, N], f32, kind="Internal").ap()
    with ExitStack() as ctx:
        S.ones3 = ctx.enter_context(nc.sbuf_tensor("ones3", [P, P], bf16))
        S.ident = ctx.enter_context(nc.sbuf_tensor("ident", [P, P], f32))
        S.ident16 = ctx.enter_context(nc.sbuf_tensor("ident16", [P, P], bf16))
        S.row0 = ctx.enter_context(nc.sbuf_tensor("row0", [P, P], f32))
        S.eps_t = ctx.enter_context(nc.sbuf_tensor("eps_t", [P, 1], f32))
        S.zeroed = ctx.enter_context(nc.semaphore("bias_rows_zeroed"))
        layers_0_to_2(nc, S)
        layer_3(nc, S)


_NAMES = ["x", "adj", "nodemask", "L0_gnn_U", "L1_gnn_Wv", "L1_gnn_bv", "L1_gnn_Wk", "L1_gnn_bk",
          "L1_gnn_Wq", "L1_gnn_bq", "L2_gnn_W", "L2_gnn_a"]
_NAMES += [f"L3_gnn_{w}{l}" for l in (1, 2, 3) for w in ("Wr", "Wx", "b", "g", "be")]
_NAMES += ["L3_gnn_Wl", "L3_gnn_bl"]


def kernel(**inputs):
    from types import SimpleNamespace

    import numpy as np
    import concourse.bacc as bacc
    from concourse.bass_utils import run_bass_kernel_spmd

    nc = bacc.Bacc("TRN2", target_bir_lowering=False, num_devices=1)
    arrays, ap = {}, {}

    def give(name, a):
        arrays[name] = a
        ap[name] = nc.dram_tensor(name, a.shape, mybir.dt.from_np(a.dtype), kind="ExternalInput").ap()

    for name in _NAMES:
        a = np.ascontiguousarray(inputs[name])
        if name == "nodemask":
            give("mask_rows", np.ascontiguousarray(a.reshape(G, CH, W32).transpose(0, 2, 1)))
            give("mask_tiles", np.ascontiguousarray(a.reshape(G, T, P).transpose(2, 0, 1)))
        else:
            give(name, a)
    out = nc.dram_tensor("out", (G, N, D), mybir.dt.float32, kind="ExternalOutput").ap()
    S = SimpleNamespace(out=out)
    S.inputs_0_to_2 = [ap[n] for n in ["x", "adj", "mask_rows"] + _NAMES[3:12]]
    S.inputs_3 = (ap["mask_tiles"], [[ap[f"L3_gnn_{w}{l}"] for w in ("Wr", "Wx", "b", "g", "be")] for l in (1, 2, 3)],
                  ap["L3_gnn_Wl"], ap["L3_gnn_bl"])
    build(nc, S)
    r = run_bass_kernel_spmd(nc, [arrays], core_ids=[0])
    return r.results[0]["out"]
```
